# Optimizing a Trainium2 kernel written in Bass

```python
import numpy as np
import jax
import jax.numpy as jnp

def _softmax(x, axis=-1):
    return jax.nn.softmax(x, axis=axis)

def _gelu(x):
    return jax.nn.gelu(x, approximate=True)

def _silu(x):
    return jax.nn.silu(x)

def _sigmoid(x):
    return jax.nn.sigmoid(x)

def _layernorm(x, axis=-1, eps=1e-05):
    m = jnp.mean(x, axis=axis, keepdims=True)
    v = jnp.var(x, axis=axis, keepdims=True)
    return (x - m) / jnp.sqrt(v + eps)

def _scatter_add(tgt, idx, src, axis=0):
    return tgt.at[idx].add(src)

def _segment_sum(src, seg, n):
    return jax.ops.segment_sum(src, seg, n)
kernel_name = 'mk_gnn_resnorm_d4_gnn_r8_64e7d7'

def setup_inputs(seed: int=0):
    np.random.seed(seed)
    _w = jnp.asarray

    def _rec_inputs():
        import jax
        import jax.numpy as jnp
        _gk = jax.random.key(seed)
        x = 4.987e-05 + 0.125 * jax.random.normal(jax.random.fold_in(_gk, 1), (12500, 64), jnp.float32)
        _s = jax.random.randint(jax.random.fold_in(_gk, 2), (100000,), 0, 12500, jnp.int32)
        _d = jax.random.randint(jax.random.fold_in(_gk, 3), (100000,), 0, 12500, jnp.int32)
        _loop = jnp.arange(12500, dtype=jnp.int32)
        src = jnp.concatenate([_s, _d, _loop])
        dst = jnp.concatenate([_d, _s, _loop])
        _o = jnp.argsort(dst, stable=True)
        src = src[_o]
        dst = dst[_o]
        edge_attr_32 = 0.000102155 + 1.00015 * jax.random.normal(jax.random.fold_in(_gk, 11), (212500, 32), jnp.float32)
        edge_type_8 = jax.random.randint(jax.random.fold_in(_gk, 13), (212500,), 0, 8, jnp.int32)
        edge_weight = jax.random.uniform(jax.random.fold_in(_gk, 14), (212500,), jnp.float32, 0.0, 0.999998)
        return (x, src, dst, edge_attr_32, edge_type_8, edge_weight)
    x, src, dst, edge_attr_32, edge_type_8, edge_weight = _rec_inputs()

    def _L0_gnn_setup():
        import jax, jax.numpy as jnp
        import numpy as np
        N = 12500
        R = 8
        C = 64
        E = 200000

        def rgcn_conv(x, src, dst, edge_type, W, root, bias):
            seg = edge_type * N + dst
            msg = x[src]
            sums = jax.ops.segment_sum(msg, seg, num_segments=R * N)
            cnt = jax.ops.segment_sum(jnp.ones((src.shape[0],), x.dtype), seg, num_segments=R * N)
            mean = (sums / jnp.maximum(cnt, 1)[:, None]).reshape(R, N, C)
            agg = jnp.einsum('rnc,rcd->nd', mean, W)
            return agg + x @ root + bias
        key = jax.random.key(seed)
        ks = jax.random.split(key, 9)
        s = 1.0 / np.sqrt(C)
        return {'edge_index': jax.random.randint(ks[0], (2, E), 0, N, dtype=jnp.int32), 'edge_type': jax.random.randint(ks[1], (E,), 0, R, dtype=jnp.int32), 'node_emb': jax.random.normal(ks[2], (N, C), dtype=jnp.float32) * s, 'W1': jax.random.normal(ks[3], (R, C, C), dtype=jnp.float32) * s, 'root1': jax.random.normal(ks[4], (C, C), dtype=jnp.float32) * s, 'b1': jnp.zeros((C,), dtype=jnp.float32), 'W2': jax.random.normal(ks[5], (R, C, C), dtype=jnp.float32) * s, 'root2': jax.random.normal(ks[6], (C, C), dtype=jnp.float32) * s, 'b2': jnp.zeros((C,), dtype=jnp.float32)}
    _L0_gnn_all = _L0_gnn_setup()
    _L0_gnn_in = {k: v for k, v in _L0_gnn_all.items() if k in ('W1', 'root1', 'b1', 'W2', 'root2', 'b2')}
    del _L0_gnn_all

    def _L1_gnn_setup():
        import jax, jax.numpy as jnp
        import numpy as np
        N_NODES = 12500
        N_EDGES = 125000
        NODE_DIM = 64
        EDGE_DIM = 32
        HIDDEN = 64

        def _unif(key, shape, fan_in):
            bound = 1.0 / np.sqrt(fan_in)
            return jax.random.uniform(key, shape, jnp.float32, -bound, bound)
        key = jax.random.key(seed)
        ks = jax.random.split(key, 11)
        node_features = jax.random.normal(ks[0], (N_NODES, NODE_DIM), jnp.float32)
        edge_index = jax.random.randint(ks[1], (2, N_EDGES), 0, N_NODES, dtype=jnp.int64)
        edge_features = jax.random.normal(ks[2], (N_EDGES, EDGE_DIM), jnp.float32)
        in_dim = 2 * NODE_DIM + EDGE_DIM
        W1 = _unif(ks[3], (HIDDEN, in_dim), in_dim)
        b1 = _unif(ks[4], (HIDDEN,), in_dim)
        W2 = _unif(ks[5], (HIDDEN, HIDDEN), HIDDEN)
        b2 = _unif(ks[6], (HIDDEN,), HIDDEN)
        w_ih = _unif(ks[7], (3 * NODE_DIM, HIDDEN), NODE_DIM)
        w_hh = _unif(ks[8], (3 * NODE_DIM, NODE_DIM), NODE_DIM)
        b_ih = _unif(ks[9], (3 * NODE_DIM,), NODE_DIM)
        b_hh = _unif(ks[10], (3 * NODE_DIM,), NODE_DIM)
        return {'node_features': node_features, 'edge_index': edge_index, 'edge_features': edge_features, 'W1': W1, 'b1': b1, 'W2': W2, 'b2': b2, 'w_ih': w_ih, 'w_hh': w_hh, 'b_ih': b_ih, 'b_hh': b_hh}
    _L1_gnn_all = _L1_gnn_setup()
    _L1_gnn_in = {k: v for k, v in _L1_gnn_all.items() if k in ('W1', 'b1', 'W2', 'b2', 'w_ih', 'w_hh', 'b_ih', 'b_hh')}
    del _L1_gnn_all

    def _L2_gnn_setup():
        import jax, jax.numpy as jnp
        import numpy as np

        def gin_layer(x, src, dst, ew, w1, b1, w2, b2):
            msg = x[src] * ew[:, None]
            agg = jax.ops.segment_sum(msg, dst, num_segments=x.shape[0])
            h = agg + x
            h = jax.nn.relu(h @ w1 + b1)
            return h @ w2 + b2
        key = jax.random.key(seed)
        ks = jax.random.split(key, 16)
        N, E, D = (12500, 125000, 64)
        x = jax.random.normal(ks[0], (N, D), dtype=jnp.float32)
        edge_index = jax.random.randint(ks[1], (2, E), 0, N)
        edge_weight = jax.random.uniform(ks[2], (E,), dtype=jnp.float32)

        def lin(k, fi, fo):
            return jax.random.normal(k, (fi, fo), dtype=jnp.float32) * (1.0 / np.sqrt(fi))
        return {'x': x, 'edge_index': edge_index, 'edge_weight': edge_weight, 'w11': lin(ks[3], 64, 64), 'b11': jnp.zeros(64, jnp.float32), 'w12': lin(ks[4], 64, 64), 'b12': jnp.zeros(64, jnp.float32), 'w21': lin(ks[5], 64, 128), 'b21': jnp.zeros(128, jnp.float32), 'w22': lin(ks[6], 128, 64), 'b22': jnp.zeros(64, jnp.float32), 'w31': lin(ks[7], 64, 64), 'b31': jnp.zeros(64, jnp.float32), 'w32': lin(ks[8], 64, 64), 'b32': jnp.zeros(64, jnp.float32)}
    _L2_gnn_all = _L2_gnn_setup()
    _L2_gnn_in = {k: v for k, v in _L2_gnn_all.items() if k in ('w11', 'b11', 'w12', 'b12', 'w21', 'b21', 'w22', 'b22', 'w31', 'b31', 'w32', 'b32')}
    del _L2_gnn_all

    def _L3_gnn_setup():
        import jax, jax.numpy as jnp
        import numpy as np
        D = 4
        H = 16
        N = 6250
        E = 100000
        TI, TJ = np.tril_indices(D, -1)

        def _householder(params):
            A = jnp.zeros(params.shape[:-1] + (D, D), params.dtype)
            A = A.at[..., TI, TJ].set(params) + jnp.eye(D, dtype=params.dtype)
            Q, R = jnp.linalg.qr(A)
            s = jnp.sign(jnp.diagonal(R, axis1=-2, axis2=-1))
            s = jnp.where(s == 0, jnp.ones_like(s), s)
            return Q * s[..., None, :]

        def _mlp(z, w1, b1, w2, b2):
            h = jax.nn.relu(z @ w1.T + b1)
            return h @ w2.T + b2

        def _forward(x, edge_index, W1, W2, epsilons, mlp1_w, mlp1_b, mlp2_w, mlp2_b):
            n = x.shape[0]
            xr = x.reshape(n, D, H)
            xt = jnp.einsum('ndf,dk->nkf', xr, W1)
            xt = jnp.einsum('ndf,fg->ndg', xt, W2)
            loops = jnp.arange(n)
            row = jnp.concatenate([edge_index[0], loops])
            col = jnp.concatenate([edge_index[1], loops])
            deg = jax.ops.segment_sum(jnp.ones_like(row, x.dtype), row, num_segments=n)
            dis = jnp.where(deg > 0, deg ** (-0.5), jnp.zeros_like(deg))
            xf = xt.reshape(n, D * H)
            xi = xf[col]
            xj = xf[row]
            cat_ve = jnp.concatenate([xi, xj], axis=-1)
            cat_ue = jnp.concatenate([xj, xi], axis=-1)
            Fve = _householder(_mlp(cat_ve, mlp1_w, mlp1_b, mlp2_w, mlp2_b))
            Fue = _householder(_mlp(cat_ue, mlp1_w, mlp1_b, mlp2_w, mlp2_b))
            xjr = xj.reshape(-1, D, H)
            msg = jnp.einsum('eka,ekb,ebh->eah', Fve, Fue, xjr)
            msg = msg * (dis[col] * dis[row])[:, None, None]
            agg = jax.ops.segment_sum(msg.reshape(-1, D * H), col, num_segments=n)
            lap = jax.nn.elu(agg.reshape(n, D, H))
            coeff = (1.0 + jnp.tanh(epsilons))[None, :, None]
            return (coeff * xr - lap).reshape(n, D * H)
        key = jax.random.key(seed)
        ks = jax.random.split(key, 9)
        dh = D * H
        x = jax.random.normal(ks[0], (N, dh), jnp.float32)
        edge_index = jax.random.randint(ks[1], (2, E), 0, N, dtype=jnp.int64)
        W1 = jax.random.normal(ks[2], (D, D), jnp.float32) / np.sqrt(D)
        W2 = jax.random.normal(ks[3], (H, H), jnp.float32) / np.sqrt(H)
        epsilons = jnp.zeros((D,), jnp.float32)
        mlp1_w = jax.random.normal(ks[4], (H, 2 * dh), jnp.float32) / np.sqrt(2 * dh)
        mlp1_b = jnp.zeros((H,), jnp.float32)
        n_params = D * (D - 1) // 2
        mlp2_w = jax.random.normal(ks[5], (n_params, H), jnp.float32) / np.sqrt(H)
        mlp2_b = jnp.zeros((n_params,), jnp.float32)
        return {'x': x, 'edge_index': edge_index, 'W1': W1, 'W2': W2, 'epsilons': epsilons, 'mlp1_w': mlp1_w, 'mlp1_b': mlp1_b, 'mlp2_w': mlp2_w, 'mlp2_b': mlp2_b}
    _L3_gnn_all = _L3_gnn_setup()
    _L3_gnn_in = {k: v for k, v in _L3_gnn_all.items() if k in ('W1', 'W2', 'epsilons', 'mlp1_w', 'mlp1_b', 'mlp2_w', 'mlp2_b')}
    del _L3_gnn_all
    return {'x': x, 'src': src, 'dst': dst, 'edge_attr_32': edge_attr_32, 'edge_type_8': edge_type_8, 'edge_weight': edge_weight, 'L0_gnn_W1': _L0_gnn_in['W1'], 'L0_gnn_root1': _L0_gnn_in['root1'], 'L0_gnn_b1': _L0_gnn_in['b1'], 'L0_gnn_W2': _L0_gnn_in['W2'], 'L0_gnn_root2': _L0_gnn_in['root2'], 'L0_gnn_b2': _L0_gnn_in['b2'], 'L1_gnn_W1': _L1_gnn_in['W1'], 'L1_gnn_b1': _L1_gnn_in['b1'], 'L1_gnn_W2': _L1_gnn_in['W2'], 'L1_gnn_b2': _L1_gnn_in['b2'], 'L1_gnn_w_ih': _L1_gnn_in['w_ih'], 'L1_gnn_w_hh': _L1_gnn_in['w_hh'], 'L1_gnn_b_ih': _L1_gnn_in['b_ih'], 'L1_gnn_b_hh': _L1_gnn_in['b_hh'], 'L2_gnn_w11': _L2_gnn_in['w11'], 'L2_gnn_b11': _L2_gnn_in['b11'], 'L2_gnn_w12': _L2_gnn_in['w12'], 'L2_gnn_b12': _L2_gnn_in['b12'], 'L2_gnn_w21': _L2_gnn_in['w21'], 'L2_gnn_b21': _L2_gnn_in['b21'], 'L2_gnn_w22': _L2_gnn_in['w22'], 'L2_gnn_b22': _L2_gnn_in['b22'], 'L2_gnn_w31': _L2_gnn_in['w31'], 'L2_gnn_b31': _L2_gnn_in['b31'], 'L2_gnn_w32': _L2_gnn_in['w32'], 'L2_gnn_b32': _L2_gnn_in['b32'], 'L3_gnn_W1': _L3_gnn_in['W1'], 'L3_gnn_W2': _L3_gnn_in['W2'], 'L3_gnn_epsilons': _L3_gnn_in['epsilons'], 'L3_gnn_mlp1_w': _L3_gnn_in['mlp1_w'], 'L3_gnn_mlp1_b': _L3_gnn_in['mlp1_b'], 'L3_gnn_mlp2_w': _L3_gnn_in['mlp2_w'], 'L3_gnn_mlp2_b': _L3_gnn_in['mlp2_b']}

def reference(x, src, dst, edge_attr_32, edge_type_8, edge_weight, L0_gnn_W1, L0_gnn_root1, L0_gnn_b1, L0_gnn_W2, L0_gnn_root2, L0_gnn_b2, L1_gnn_W1, L1_gnn_b1, L1_gnn_W2, L1_gnn_b2, L1_gnn_w_ih, L1_gnn_w_hh, L1_gnn_b_ih, L1_gnn_b_hh, L2_gnn_w11, L2_gnn_b11, L2_gnn_w12, L2_gnn_b12, L2_gnn_w21, L2_gnn_b21, L2_gnn_w22, L2_gnn_b22, L2_gnn_w31, L2_gnn_b31, L2_gnn_w32, L2_gnn_b32, L3_gnn_W1, L3_gnn_W2, L3_gnn_epsilons, L3_gnn_mlp1_w, L3_gnn_mlp1_b, L3_gnn_mlp2_w, L3_gnn_mlp2_b):
    import jax
    import jax.numpy as jnp

    def _L0_gnn_ref(edge_index, edge_type, node_emb, W1, root1, b1, W2, root2, b2):
        import jax, jax.numpy as jnp
        import numpy as np
        N = 12500
        R = 8
        C = 64
        E = 200000

        def rgcn_conv(x, src, dst, edge_type, W, root, bias):
            seg = edge_type * N + dst
            msg = x[src]
            sums = jax.ops.segment_sum(msg, seg, num_segments=R * N)
            cnt = jax.ops.segment_sum(jnp.ones((src.shape[0],), x.dtype), seg, num_segments=R * N)
            mean = (sums / jnp.maximum(cnt, 1)[:, None]).reshape(R, N, C)
            agg = jnp.einsum('rnc,rcd->nd', mean, W)
            return agg + x @ root + bias
        src, dst = (edge_index[0], edge_index[1])
        x = rgcn_conv(node_emb, src, dst, edge_type, W1, root1, b1)
        x = jax.nn.relu(x)
        x = rgcn_conv(x, src, dst, edge_type, W2, root2, b2)
        return x

    def _L1_gnn_ref(node_features, edge_index, edge_features, W1, b1, W2, b2, w_ih, w_hh, b_ih, b_hh):
        import jax, jax.numpy as jnp
        import numpy as np
        N_NODES = 12500
        N_EDGES = 125000
        NODE_DIM = 64
        EDGE_DIM = 32
        HIDDEN = 64

        def _unif(key, shape, fan_in):
            bound = 1.0 / np.sqrt(fan_in)
            return jax.random.uniform(key, shape, jnp.float32, -bound, bound)
        src, dst = (edge_index[0], edge_index[1])
        x = jnp.concatenate([node_features[src], node_features[dst], edge_features], axis=-1)
        h = jax.nn.relu(x @ W1.T + b1)
        messages = h @ W2.T + b2
        agg = jax.ops.segment_sum(messages, dst, num_segments=node_features.shape[0])
        gi = agg @ w_ih.T + b_ih
        gh = node_features @ w_hh.T + b_hh
        i_r, i_z, i_n = jnp.split(gi, 3, axis=-1)
        h_r, h_z, h_n = jnp.split(gh, 3, axis=-1)
        r = jax.nn.sigmoid(i_r + h_r)
        z = jax.nn.sigmoid(i_z + h_z)
        n = jnp.tanh(i_n + r * h_n)
        return (1.0 - z) * n + z * node_features

    def _L2_gnn_ref(x, edge_index, edge_weight, w11, b11, w12, b12, w21, b21, w22, b22, w31, b31, w32, b32):
        import jax, jax.numpy as jnp
        import numpy as np

        def gin_layer(x, src, dst, ew, w1, b1, w2, b2):
            msg = x[src] * ew[:, None]
            agg = jax.ops.segment_sum(msg, dst, num_segments=x.shape[0])
            h = agg + x
            h = jax.nn.relu(h @ w1 + b1)
            return h @ w2 + b2
        src, dst = (edge_index[0], edge_index[1])
        h = gin_layer(x, src, dst, edge_weight, w11, b11, w12, b12)
        h = jax.nn.relu(h)
        h = gin_layer(h, src, dst, edge_weight, w21, b21, w22, b22)
        h = jax.nn.relu(h)
        h = gin_layer(h, src, dst, edge_weight, w31, b31, w32, b32)
        return h

    def _L3_gnn_ref(x, edge_index, W1, W2, epsilons, mlp1_w, mlp1_b, mlp2_w, mlp2_b):
        import jax, jax.numpy as jnp
        import numpy as np
        D = 4
        H = 16
        N = 6250
        E = 100000
        TI, TJ = np.tril_indices(D, -1)

        def _householder(params):
            A = jnp.zeros(params.shape[:-1] + (D, D), params.dtype)
            A = A.at[..., TI, TJ].set(params) + jnp.eye(D, dtype=params.dtype)
            Q, R = jnp.linalg.qr(A)
            s = jnp.sign(jnp.diagonal(R, axis1=-2, axis2=-1))
            s = jnp.where(s == 0, jnp.ones_like(s), s)
            return Q * s[..., None, :]

        def _mlp(z, w1, b1, w2, b2):
            h = jax.nn.relu(z @ w1.T + b1)
            return h @ w2.T + b2

        def _forward(x, edge_index, W1, W2, epsilons, mlp1_w, mlp1_b, mlp2_w, mlp2_b):
            n = x.shape[0]
            xr = x.reshape(n, D, H)
            xt = jnp.einsum('ndf,dk->nkf', xr, W1)
            xt = jnp.einsum('ndf,fg->ndg', xt, W2)
            loops = jnp.arange(n)
            row = jnp.concatenate([edge_index[0], loops])
            col = jnp.concatenate([edge_index[1], loops])
            deg = jax.ops.segment_sum(jnp.ones_like(row, x.dtype), row, num_segments=n)
            dis = jnp.where(deg > 0, deg ** (-0.5), jnp.zeros_like(deg))
            xf = xt.reshape(n, D * H)
            xi = xf[col]
            xj = xf[row]
            cat_ve = jnp.concatenate([xi, xj], axis=-1)
            cat_ue = jnp.concatenate([xj, xi], axis=-1)
            Fve = _householder(_mlp(cat_ve, mlp1_w, mlp1_b, mlp2_w, mlp2_b))
            Fue = _householder(_mlp(cat_ue, mlp1_w, mlp1_b, mlp2_w, mlp2_b))
            xjr = xj.reshape(-1, D, H)
            msg = jnp.einsum('eka,ekb,ebh->eah', Fve, Fue, xjr)
            msg = msg * (dis[col] * dis[row])[:, None, None]
            agg = jax.ops.segment_sum(msg.reshape(-1, D * H), col, num_segments=n)
            lap = jax.nn.elu(agg.reshape(n, D, H))
            coeff = (1.0 + jnp.tanh(epsilons))[None, :, None]
            return (coeff * xr - lap).reshape(n, D * H)
        return _forward(x, edge_index, W1, W2, epsilons, mlp1_w, mlp1_b, mlp2_w, mlp2_b)
    edge_index = jnp.stack([src, dst])
    x = _layernorm(x + _L0_gnn_ref(edge_index, edge_type_8, x, L0_gnn_W1, L0_gnn_root1, L0_gnn_b1, L0_gnn_W2, L0_gnn_root2, L0_gnn_b2), axis=-1)
    x = _layernorm(x + _L1_gnn_ref(x, edge_index, edge_attr_32, L1_gnn_W1, L1_gnn_b1, L1_gnn_W2, L1_gnn_b2, L1_gnn_w_ih, L1_gnn_w_hh, L1_gnn_b_ih, L1_gnn_b_hh), axis=-1)
    x = _layernorm(x + _L2_gnn_ref(x, edge_index, edge_weight, L2_gnn_w11, L2_gnn_b11, L2_gnn_w12, L2_gnn_b12, L2_gnn_w21, L2_gnn_b21, L2_gnn_w22, L2_gnn_b22, L2_gnn_w31, L2_gnn_b31, L2_gnn_w32, L2_gnn_b32), axis=-1)
    x = _layernorm(x + _L3_gnn_ref(x, edge_index, L3_gnn_W1, L3_gnn_W2, L3_gnn_epsilons, L3_gnn_mlp1_w, L3_gnn_mlp1_b, L3_gnn_mlp2_w, L3_gnn_mlp2_b), axis=-1)
    return x

_drawn_inputs = setup_inputs


def setup_inputs(seed=0):
    import zlib

    import numpy as np

    out = dict(_drawn_inputs(seed))
    spreads = {'L0_gnn_b1': (0.0, 0.1),
     'L0_gnn_b2': (0.0, 0.1),
     'L2_gnn_b11': (0.0, 0.646),
     'L2_gnn_b12': (0.0, 0.274),
     'L2_gnn_b21': (0.0, 0.8),
     'L2_gnn_b22': (0.0, 0.8),
     'L2_gnn_b31': (0.0, 2.0),
     'L2_gnn_b32': (0.0, 2.0),
     'L3_gnn_epsilons': (0.0, 0.1),
     'L3_gnn_mlp1_b': (0.0, 0.8),
     'L3_gnn_mlp2_b': (0.0, 2.0)}
    factors = {'edge_attr_32': 8.0,
     'L1_gnn_b_ih': 5.309,
     'L1_gnn_b_hh': 7.445,
     'L3_gnn_mlp1_w': 6.429,
     'L3_gnn_mlp2_w': 5.767}
    for name, (base, spread) in spreads.items():
        noise = np.random.default_rng([zlib.crc32(name.encode()), seed]).standard_normal(out[name].shape)
        drawn = base * np.exp(spread * noise) if base else spread * noise
        out[name] = jnp.asarray(drawn.astype(out[name].dtype))
    for name, factor in factors.items():
        out[name] = (out[name] * factor).astype(out[name].dtype)
    return out
```

```python
import concourse.bass as bass
from concourse import mybir
from contextlib import ExitStack

F32 = mybir.dt.float32
BF16 = mybir.dt.bfloat16
I32 = mybir.dt.int32
ALU = mybir.AluOpType
ACT = mybir.ActivationFunctionType
AX = mybir.AxisListType
DVE_ENGINE = mybir.EngineType.DVE
PE_ENGINE = mybir.EngineType.PE
ACT_ENGINE = mybir.EngineType.Activation
SP_ENGINE = mybir.EngineType.SP

P = 128
N = 12500
E = 212500
C = 64
R = 8
FE = 32
TILES = -(-N // P)
UNIT = 4
TILES_P = -(-TILES // (2 * UNIT)) * 2 * UNIT
UNITS = TILES_P // UNIT
NODES_P = TILES_P * P
EDGE_COLS = -(-E // P) + 1
EDGES_P = EDGE_COLS * P
NO_NODE = 1 << 20
PAD_SRC = NODES_P - 1
GROUP = 4
RING = 4
BODY = 8
STEPS_MIN = E // P + TILES
BODIES = -(-STEPS_MIN // (GROUP * BODY))
STEPS = BODIES * GROUP * BODY
BSTEPS = GROUP * BODY
BATCH = 16
SHEAF_BODY = 4
SHEAF_BODIES = -(-STEPS_MIN // (BATCH * SHEAF_BODY))
PLAN_GROUPS = -(-(max(STEPS, SHEAF_BODIES * BATCH * SHEAF_BODY) + BATCH) // P)
PLAN_GROUPS += PLAN_GROUPS % 2
STEPS_P = PLAN_GROUPS * P
EPS = 1e-5
HID = 16
NPAR = 6
SHEAF_LINKS = 30 + 5 * BATCH // GROUP
TROW = C + 2 * HID


class Signal:

    def __init__(self, ctx, nc, name):
        self.sem = ctx.enter_context(nc.semaphore(name))
        self.base = 0

    def at(self, k):
        return self.base + k

    def passed(self, total):
        self.base += total


class Links:

    def __init__(self, links, before=0, per_body=0, i=0):
        self.links, self.n, self.later = links, before, per_body * i if per_body else 0

    def next(self):
        self.n += 1
        return self.links.sem, 1

    def done(self):
        return self.links.sem, self.links.at(self.n) + self.later

    def close(self):
        self.links.passed(self.n)


class Memory:
    pass


def tiles_of_steps(nc, mem, engine, first, count=GROUP):
    _, values = nc.values_load_multi_w_load_instructions(
        mem.tile_row[0:1, bass.ds(first, count)], engines=[engine], min_val=0, max_val=TILES - 1,
        skip_runtime_bounds_check_because="the plan counts at most TILES - 1 tiles passed")
    return values


def wait_apart(eng, mem, sem, value):
    eng.wait_ge(sem, value)
    eng.sem_inc(mem.sems["waited"].sem, 1)


def bc(ap, axis, n):
    return ap.unsqueeze(axis).to_broadcast(list(ap.shape[:axis]) + [n] + list(ap.shape[axis:]))


def constants_and_plan(nc, mem, dram):
    ctx = ExitStack()
    with ctx:
        sb = lambda name, shape, dt=F32: ctx.enter_context(nc.sbuf_tensor(name, shape, dt))
        dst_i = sb("plan_dst_i", [P, EDGE_COLS], I32)
        dst_f = sb("plan_dst_f", [P, EDGE_COLS])
        below_junk = sb("plan_below_junk", [P, EDGE_COLS])
        iota_i = sb("plan_iota_i", [P, P], I32)
        part_i = sb("plan_part_i", [P, 1], I32)
        bound_i = sb("plan_bound_i", [P, TILES + 1], I32)
        bound = sb("plan_bound", [P, TILES + 1])
        step_i = sb("plan_step_i", [P, PLAN_GROUPS], I32)
        step_f = sb("plan_step_f", [P, PLAN_GROUPS])
        ones = sb("plan_ones", [P, P])
        below = sb("plan_below", [P, TILES + 1])
        first = sb("plan_first", [P, TILES + 1])
        steps_f = sb("plan_steps_f", [P, TILES])
        steps_i = sb("plan_steps_i", [P, TILES], I32)
        zeros = sb("plan_zeros", [P, TILES])
        step0 = sb("plan_step0", [P, TILES])
        delta = sb("plan_delta", [P, TILES - 1])
        offset = sb("plan_offset", [P, TILES - 1])
        reached = sb("plan_reached", [P, TILES - 1])
        junk = sb("plan_junk", [P, TILES - 1])
        tile_f = sb("plan_tile_f", [P, PLAN_GROUPS])
        start_f = sb("plan_start_f", [P, PLAN_GROUPS])
        rows_i = sb("plan_rows_i", [PLAN_GROUPS, 2, P], I32)
        count_ps = ctx.enter_context(nc.psum_tensor("plan_count_ps", [P, 512], F32))
        rows_ps = ctx.enter_context(nc.psum_tensor("plan_rows_ps", [P, 512], F32))
        sem = mem.sems
        loaded, iotas, chain = sem["load"], sem["made"], sem["dve_chain"]
        counted, counts_ready, stored = sem["pe_done"], sem["dve_done"], sem["store"]

        block = ctx.enter_context(nc.Block())

        @block.sync
        def _(sp):
            sp.dma_start(dst_i[:, :], dram["dst"][0:EDGES_P].rearrange("(p c) -> p c", p=P)).then_inc(loaded.sem, 16)
            sp.dma_start(mem.xs[:, :].rearrange("p (t c) -> p t c", c=C),
                         dram["x"].rearrange("(t p) c -> p t c", p=P)).then_inc(loaded.sem, 16)
            sp.wait_ge(counts_ready.sem, counts_ready.at(3))
            for a in range(2):
                sp.dma_start(dram["plan_rows"][a].rearrange("(g s) -> g s", s=P), rows_i[:, a, :]).then_inc(stored.sem, 16)
            sp.wait_ge(stored.sem, stored.at(32))
            sp.dma_start(mem.tile_row[0:1, :], dram["plan_rows"][0:1, :]).then_inc(stored.sem, 16)
            sp.dma_start(mem.start_row[0:1, :], dram["plan_rows"][1:2, :]).then_inc(stored.sem, 16)
            sp.wait_ge(stored.sem, stored.at(64))
            sp.wait_ge(loaded.sem, loaded.at(32))

        @block.gpsimd
        def _(pool):
            nc.gpsimd.memset(mem.ident[:, :], 0.0).then_inc(iotas.sem, 1)
            nc.gpsimd.iota(iota_i[:, :], [[1, P]], base=0, channel_multiplier=0).then_inc(iotas.sem, 1)
            nc.gpsimd.iota(part_i[:, :], [[0, 1]], base=0, channel_multiplier=1).then_inc(iotas.sem, 1)
            nc.gpsimd.iota(bound_i[:, :], [[P, TILES + 1]], base=0, channel_multiplier=0).then_inc(iotas.sem, 1)
            nc.gpsimd.iota(step_i[:, :], [[P, PLAN_GROUPS]], base=0, channel_multiplier=1).then_inc(iotas.sem, 1)
            nc.gpsimd.memset(ones[:, :], 1.0).then_inc(iotas.sem, 1)
            pool.wait_ge(iotas.sem, iotas.at(6))
            nc.gpsimd.affine_select(out=mem.ident[:, :], in_=mem.ident[:, :], compare_op=ALU.not_equal, fill=1.0,
                                    base=0, pattern=[[-1, P]], channel_multiplier=1).then_inc(iotas.sem, 1)

        @block.tensor
        def _(pe):
            pe.wait_ge(counts_ready.sem, counts_ready.at(1))
            nc.tensor.matmul(count_ps[:, 0:TILES + 1], ones[:, :], below[:, :], start=True, stop=True).then_inc(counted.sem, 1)
            pe.wait_ge(counts_ready.sem, counts_ready.at(2))
            pe.wait_ge(iotas.sem, iotas.at(7))
            nc.tensor.transpose(rows_ps[0:PLAN_GROUPS, 0:P], tile_f[:, :], mem.ident[:, :])
            nc.tensor.transpose(rows_ps[0:PLAN_GROUPS, P:2 * P], start_f[:, :], mem.ident[:, :]).then_inc(counted.sem, 1)

        @block.vector
        def _(dve):
            link = Links(chain)
            dve.wait_ge(iotas.sem, iotas.at(6))
            nc.vector.tensor_copy(mem.iota[:, :], iota_i[:, :]).then_inc(*link.next())
            dve.wait_ge(*link.done())
            nc.vector.tensor_copy(mem.iota_h[:, :], mem.iota[:, :]).then_inc(*link.next())
            dve.wait_ge(*link.done())
            nc.vector.tensor_copy(bound[:, :], bound_i[:, :]).then_inc(*link.next())
            dve.wait_ge(*link.done())
            nc.vector.tensor_copy(step_f[:, :], step_i[:, :]).then_inc(*link.next())
            dve.wait_ge(*link.done())
            nc.vector.memset(below[:, :], 0.0).then_inc(*link.next())
            dve.wait_ge(*link.done())
            nc.vector.memset(zeros[:, :], 0.0).then_inc(*link.next())
            dve.wait_ge(*link.done())
            dve.wait_ge(loaded.sem, loaded.at(32))
            nc.vector.tensor_copy(dst_f[:, :], dst_i[:, :]).then_inc(*link.next())
            dve.wait_ge(*link.done())
            with dve.Fori(1, TILES + 1) as t:
                dve.wait_ge(chain.sem, chain.at(link.n) - 1 + t)
                nc.vector.tensor_scalar(below_junk[:, :], dst_f[:, :], bound[:, bass.ds(t, 1)], None, ALU.is_lt,
                                        ALU.add, accum_out=below[:, bass.ds(t, 1)]).then_inc(chain.sem, 1)
            link.n += TILES
            dve.wait_ge(chain.sem, chain.at(link.n))
            dve.sem_inc(counts_ready.sem, 1)
            dve.wait_ge(counted.sem, counted.at(1))
            nc.vector.tensor_copy(first[:, :], count_ps[:, 0:TILES + 1]).then_inc(*link.next())
            dve.wait_ge(*link.done())
            nc.vector.tensor_tensor(steps_f[:, :], first[:, 1:TILES + 1], first[:, 0:TILES], ALU.subtract).then_inc(*link.next())
            dve.wait_ge(*link.done())
            nc.vector.tensor_scalar(steps_f[:, :], steps_f[:, :], float(P - 1), None, ALU.add).then_inc(*link.next())
            dve.wait_ge(*link.done())
            nc.vector.tensor_copy(steps_i[:, :], steps_f[:, :]).then_inc(*link.next())
            dve.wait_ge(*link.done())
            nc.vector.tensor_scalar(steps_i[:, :], steps_i[:, :], 7, None, ALU.arith_shift_right).then_inc(*link.next())
            dve.wait_ge(*link.done())
            nc.vector.tensor_copy(steps_f[:, :], steps_i[:, :]).then_inc(*link.next())
            dve.wait_ge(*link.done())
            nc.vector.tensor_tensor_scan(step0[:, :], steps_f[:, :], zeros[:, :], 0.0, ALU.add, ALU.add).then_inc(*link.next())
            dve.wait_ge(*link.done())
            nc.vector.scalar_tensor_tensor(offset[:, :], step0[:, 0:TILES - 1], -float(P), first[:, 1:TILES],
                                           ALU.mult, ALU.add).then_inc(*link.next())
            dve.wait_ge(*link.done())
            nc.vector.tensor_copy(delta[:, 0:1], offset[:, 0:1]).then_inc(*link.next())
            dve.wait_ge(*link.done())
            nc.vector.tensor_tensor(delta[:, 1:], offset[:, 1:], offset[:, :TILES - 2], ALU.subtract).then_inc(*link.next())
            dve.wait_ge(*link.done())
            for g in range(PLAN_GROUPS):
                nc.vector.tensor_scalar(reached[:, :], step0[:, 0:TILES - 1], step_f[:, g:g + 1], None,
                                        ALU.is_le, ALU.add, accum_out=tile_f[:, g:g + 1]).then_inc(*link.next())
                dve.wait_ge(*link.done())
                nc.vector.tensor_tensor_reduce(out=junk[:, :], in0=reached[:, :], in1=delta[:, :], scale=1.0,
                                               scalar=0.0, op0=ALU.mult, op1=ALU.add,
                                               accum_out=start_f[:, g:g + 1]).then_inc(*link.next())
                dve.wait_ge(*link.done())
            nc.vector.scalar_tensor_tensor(start_f[:, :], step_f[:, :], float(P), start_f[:, :], ALU.mult, ALU.add).then_inc(*link.next())
            dve.wait_ge(*link.done())
            nc.vector.tensor_scalar(start_f[:, :], start_f[:, :], float(E), None, ALU.min).then_inc(*link.next())
            dve.wait_ge(*link.done())
            nc.vector.tensor_copy(mem.start_i[:, :], start_f[:, :]).then_inc(*link.next())
            dve.wait_ge(*link.done())
            nc.vector.tensor_scalar(mem.node0[:, :], tile_f[:, :], float(P), None, ALU.mult).then_inc(*link.next())
            dve.wait_ge(*link.done())
            dve.sem_inc(counts_ready.sem, 1)
            dve.wait_ge(counted.sem, counted.at(2))
            nc.vector.tensor_copy(rows_i[:, :, :], rows_ps[0:PLAN_GROUPS, 0:2 * P].rearrange("g (a s) -> g a s", a=2)).then_inc(*link.next())
            dve.wait_ge(*link.done())
            dve.sem_inc(counts_ready.sem, 1)
            link.close()

    loaded.passed(32), iotas.passed(7), counted.passed(2), counts_ready.passed(3), stored.passed(64)


def align_edges(nc, mem, dram):
    ctx = ExitStack()
    with ctx:
        sb = lambda name, shape, dt=F32: ctx.enter_context(nc.sbuf_tensor(name, shape, dt))
        raw_i = sb("align_raw_i", [P, 2, 3, P], I32)
        raw_w = sb("align_raw_w", [P, 2, P])
        raw_f = sb("align_raw_f", [P, 2, 3, P])
        start_now = sb("align_start", [P, 2], I32)
        ps = [ctx.enter_context(nc.psum_tensor(f"align_ps{j}", [P, 512], F32)) for j in range(2)]
        sem = mem.sems
        gathered = [sem["gather0"], sem["gather1"]]
        chain, starts, raw_ready, turned, evacuated = (sem["dve_chain"], sem["made"], sem["dve_done"],
                                                       sem["pe_done"], sem["act_done"])
        arrays = [dram["dst"], dram["src"], dram["typ"]]
        block = ctx.enter_context(nc.Block())

        @block.gpsimd
        def _(pool):
            with pool.Fori(0, PLAN_GROUPS // 2) as i:
                for j in range(2):
                    wait_apart(pool, mem, starts.sem, starts.at(1 + j) + 2 * i)
                    for a, array in enumerate(arrays + [dram["ew"]]):
                        out = raw_i[:, j, a, :] if a < 3 else raw_w[:, j, :]
                        nc.gpsimd.indirect_dma_start(
                            out=out, out_offset=None, in_=array.rearrange("(e o) -> e o", o=1),
                            in_offset=bass.IndirectOffsetOnAxis(ap=start_now[:, j:j + 1], axis=0)).then_inc(gathered[j].sem, 16)

        @block.vector
        def _(dve):
            link = Links(chain)
            with dve.Fori(0, PLAN_GROUPS // 2) as i:
                k = 0
                for j in range(2):
                    nc.vector.tensor_copy(start_now[:, j:j + 1], mem.start_i[:, bass.ds(2 * i + j, 1)]).then_inc(starts.sem, 1)
                for j in range(2):
                    dve.wait_ge(gathered[j].sem, gathered[j].at(64) + 64 * i)
                    nc.vector.tensor_copy(raw_f[:, j, :, :], raw_i[:, j, :, :]).then_inc(chain.sem, 1)
                    k += 1
                    dve.wait_ge(chain.sem, chain.at(k) + 4 * i)
                    nc.vector.tensor_scalar(raw_f[:, j, 0, :], raw_f[:, j, 0, :], mem.node0[:, bass.ds(2 * i + j, 1)], None,
                                            ALU.subtract).then_inc(raw_ready.sem, 1)
                for j in range(2):
                    dve.wait_ge(turned.sem, turned.at(j + 1) + 2 * i)
                    cols = bass.ds((2 * i + j) * P, P)
                    nc.vector.tensor_copy(mem.drel[:, cols], ps[j][:, 0:P])
                    nc.vector.tensor_copy(mem.typ[:, cols], ps[j][:, 2 * P:3 * P]).then_inc(chain.sem, 1)
                    nc.vector.tensor_copy(mem.ew[:, cols], ps[j][:, 3 * P:4 * P])
                    nc.vector.tensor_copy(mem.src_i[:, cols], ps[j][:, P:2 * P])
                    k += 1
                    dve.wait_ge(chain.sem, chain.at(k) + 4 * i)
                    nc.vector.scalar_tensor_tensor(mem.row_i[:, cols], ps[j][:, P:2 * P], float(R), mem.typ[:, cols],
                                                   ALU.mult, ALU.add).then_inc(evacuated.sem, 1)

        @block.tensor
        def _(pe):
            with pe.Fori(0, PLAN_GROUPS // 2) as i:
                for j in range(2):
                    pe.wait_ge(raw_ready.sem, raw_ready.at(j + 1) + 2 * i)
                    for a in range(3):
                        nc.tensor.transpose(ps[j][:, a * P:(a + 1) * P], raw_f[:, j, a, :], mem.ident[:, :])
                    nc.tensor.transpose(ps[j][:, 3 * P:4 * P], raw_w[:, j, :], mem.ident[:, :]).then_inc(turned.sem, 1)

    n = PLAN_GROUPS // 2
    for g in gathered:
        g.passed(64 * n)
    chain.passed(4 * n), starts.passed(2 * n), raw_ready.passed(2 * n), turned.passed(2 * n), evacuated.passed(2 * n)


def count_relations(nc, mem, dram):
    ctx = ExitStack()
    with ctx:
        sb = lambda name, shape, dt=F32: ctx.enter_context(nc.sbuf_tensor(name, shape, dt))
        onehot = sb("count_onehot", [P, RING * GROUP, P], BF16)
        typ_hot = sb("count_typ_hot", [P, BSTEPS, R], BF16)
        zero_h = sb("count_zero", [1, 512], BF16)
        drel_now = sb("count_drel", [P, BSTEPS])
        table = ctx.enter_context(nc.psum_tensor("count_table", [P, 1024], F32))
        sem = mem.sems
        chain, built, summed, zeroed = sem["dve_chain"], sem["built"], sem["used"], sem["made"]
        block = ctx.enter_context(nc.Block())
        ring = RING * GROUP

        @block.tensor
        def _(pe):
            pe.wait_ge(zeroed.sem, zeroed.at(1))
            for b in range(2):
                nc.tensor.matmul(table[:, 512 * b:512 * (b + 1)], zero_h[0:1, 0:P], zero_h[0:1, :], start=True, stop=True,
                                 skip_group_check=True)
            pe.sem_inc(summed.sem, RING)
            with pe.Fori(0, BODIES) as i:
                for j in range(BODY):
                    tiles = tiles_of_steps(nc, mem, PE_ENGINE, i * BSTEPS + GROUP * j)
                    pe.wait_ge(built.sem, built.at(j + 1) + BODY * i)
                    for u in range(GROUP):
                        k = GROUP * j + u
                        ins = nc.tensor.matmul(table[:, bass.ds(tiles[u] * R, R)], onehot[:, k % ring, :], typ_hot[:, k, :],
                                               start=False, stop=True, skip_group_check=True)
                    ins.then_inc(summed.sem, 1)

        @block.vector
        def _(dve):
            link = Links(chain)
            nc.vector.memset(zero_h[:, :], 0.0).then_inc(zeroed.sem, 1)
            with dve.Fori(0, BODIES) as i:
                dve.wait_ge(summed.sem, summed.at(RING) + BODY * i)
                nc.vector.tensor_copy(drel_now[:, :], mem.drel[:, bass.ds(i * BSTEPS, BSTEPS)]).then_inc(chain.sem, 1)
                nc.vector.tensor_tensor(typ_hot[:, :, :], bc(mem.typ[:, bass.ds(i * BSTEPS, BSTEPS)], 2, R),
                                        bc(mem.iota[:, 0:R], 1, BSTEPS), ALU.is_equal).then_inc(chain.sem, 1)
                dve.wait_ge(chain.sem, chain.at(2) + 2 * i)
                for j in range(BODY):
                    dve.wait_ge(summed.sem, summed.at(j + 1) + BODY * i)
                    for u in range(GROUP):
                        k = GROUP * j + u
                        ins = nc.vector.tensor_scalar(onehot[:, k % ring, :], mem.iota_h[:, :], drel_now[:, k:k + 1], None,
                                                      ALU.is_equal)
                    ins.then_inc(built.sem, 1)
            dve.wait_ge(summed.sem, summed.at(RING + BODY * BODIES))
            link.n += 2 * BODIES
            nc.vector.tensor_copy(mem.counts[:, 0:512], table[:, 0:512]).then_inc(*link.next())
            dve.wait_ge(*link.done())
            nc.vector.tensor_copy(mem.counts[:, 512:], table[:, 512:TILES_P * R]).then_inc(*link.next())
            dve.wait_ge(*link.done())
            nc.vector.tensor_reduce(mem.degree[:, :], mem.counts[:, :].rearrange("p (t r) -> p t r", r=R), AX.X, ALU.add).then_inc(*link.next())
            dve.wait_ge(*link.done())
            nc.vector.tensor_scalar(mem.counts[:, :], mem.counts[:, :], 1.0, None, ALU.max).then_inc(*link.next())
            dve.wait_ge(*link.done())
            nc.vector.reciprocal(mem.counts[:, :], mem.counts[:, :]).then_inc(*link.next())
            dve.wait_ge(*link.done())
            nc.vector.memset(mem.norm[:, :], 0.0).then_inc(*link.next())
            dve.wait_ge(*link.done())
            link.close()

    zeroed.passed(1), built.passed(BODY * BODIES), summed.passed(RING + BODY * BODIES)


USED0 = RING + 1
ADDED0 = GROUP * RING


def gather_program(nc, mem, table, index_now, rows, width, ahead=0):
    sem = mem.sems
    used, index_ready = sem["used"], sem["index_ready"]

    def gather_group(pool, j, i):
        half = j // (BODY // 2)
        if j % (BODY // 2) == 0:
            wait_apart(pool, mem, index_ready.sem, index_ready.at(half + 1) + 2 * i)
        wait_apart(pool, mem, used.sem, used.at(j - RING + USED0 + 1) + BODY * i)
        for u in range(GROUP):
            k = GROUP * j + u
            slot = k % (RING * GROUP)
            nc.gpsimd.indirect_dma_start(
                out=rows[:, slot * width:(slot + 1) * width], out_offset=None, in_=table,
                in_offset=bass.IndirectOffsetOnAxis(ap=index_now[:, k:k + 1], axis=0),
            ).then_inc(sem[f"gather{j % RING}"].sem, 16)

    def program(pool):
        with pool.Fori(0, BODIES) as i:
            for j in range(BODY):
                gather_group(pool, j, i)
        for j in range(ahead):
            gather_group(pool, j, BODIES)
    return program


def copy_indices(nc, mem, act, i, half, index_now, index):
    used, index_ready = mem.sems["used"], mem.sems["index_ready"]
    n = BSTEPS // 2
    act.wait_ge(used.sem, used.at(half * (BODY // 2) - BODY // 2 + USED0) + BODY * i)
    nc.scalar.activation(index_now[:, half * n:(half + 1) * n], index[:, bass.ds(i * BSTEPS + half * n, n)],
                         ACT.Copy).then_inc(index_ready.sem, 1)


def gathered(mem, j, i):
    s = mem.sems[f"gather{j % RING}"]
    return s.sem, s.at(16 * GROUP * (j // RING + 1)) + 16 * GROUP * (BODY // RING) * i


def pass_ends(mem, ahead=0, groups=BODY * BODIES):
    s = mem.sems
    for q in range(RING):
        s[f"gather{q}"].passed(16 * GROUP * groups // RING)
    s["used"].passed(USED0 + groups)
    s["added"].passed(ADDED0 + GROUP * groups)
    for q in range(ahead):
        s[f"gather{q}"].passed(16 * GROUP)


def add_and_build(nc, mem, dve, i, j, ps, onehot, drel_now, weight_now, lag):
    used, added, built = mem.sems["used"], mem.sems["added"], mem.sems["built"]
    tiles = tiles_of_steps(nc, mem, DVE_ENGINE, i * BSTEPS + GROUP * j)
    dve.wait_ge(used.sem, used.at(USED0 + j + 1) + BODY * i)
    for u in range(GROUP):
        k = GROUP * j + u
        dve.wait_ge(added.sem, added.at(ADDED0 + k) + BSTEPS * i)
        columns = mem.acc[:, bass.ds(tiles[u] * C, C)]
        nc.vector.tensor_tensor(columns, columns, ps[j % RING][:, u * C:(u + 1) * C], ALU.add).then_inc(added.sem, 1)
        build_onehot(nc, mem, onehot, k + GROUP * lag, drel_now[:, k:k + 1],
                     None if weight_now is None else weight_now[:, k:k + 1])


def build_onehot(nc, mem, onehot, k, place, weight):
    out = onehot[:, k % (RING * GROUP), :]
    if weight is None:
        ins = nc.vector.tensor_scalar(out, mem.iota[:, :], place, None, ALU.is_equal)
    else:
        ins = nc.vector.tensor_scalar(out, mem.iota[:, :], place, weight, ALU.is_equal, ALU.mult)
    ins.then_inc(mem.sems["built"].sem, 1)


def stage_columns(nc, mem, dve, i, lag, pairs):
    chain, built = mem.sems["dve_chain"], mem.sems["built"]
    dve.wait_ge(built.sem, built.at(GROUP * lag) + BSTEPS * i)
    for now, table in pairs:
        nc.vector.tensor_copy(now[:, :], table[:, bass.ds(i * BSTEPS + GROUP * lag, BSTEPS)]).then_inc(chain.sem, 1)
    dve.wait_ge(chain.sem, chain.at(len(pairs)) + len(pairs) * i)


def gather_pass(nc, mem, tag, table, index, weight, lag=2, count_sources=False):
    ctx = ExitStack()
    with ctx:
        sb = lambda name, shape, dt=F32: ctx.enter_context(nc.sbuf_tensor(f"{tag}_{name}", shape, dt))
        rows = sb("rows", [P, RING * GROUP * C])
        onehot = sb("onehot", [P, RING * GROUP, P])
        drel_now = sb("drel_now", [P, BSTEPS])
        weight_now = sb("weight_now", [P, BSTEPS])
        index_now = sb("index_now", [P, BSTEPS], I32)
        ps = [ctx.enter_context(nc.psum_tensor(f"{tag}_ps{j}", [P, 512], F32)) for j in range(RING)]
        sem = mem.sems
        used, added, built = sem["used"], sem["added"], sem["built"]
        if count_sources:
            low_now = sb("low_now", [P, BSTEPS])
            high_now = sb("high_now", [P, BSTEPS])
            low_hot = sb("low_hot", [P, 2 * GROUP, P], BF16)
            high_hot = sb("high_hot", [P, 2 * GROUP, TILES_P], BF16)
            zero_h = sb("zero_h", [1, P], BF16)
            source_ps = ctx.enter_context(nc.psum_tensor(f"{tag}_source_ps", [P, 512], F32))
            hots, tallied, zeroed = sem["dve_done"], sem["pe_done"], sem["made"]
        block = ctx.enter_context(nc.Block())
        block.gpsimd(gather_program(nc, mem, table, index_now, rows, C))

        @block.scalar
        def _(act):
            with act.Fori(0, BODIES) as i:
                for half in range(2):
                    copy_indices(nc, mem, act, i, half, index_now, index)

        @block.tensor
        def _(pe):
            pe.sem_inc(used.sem, USED0)
            if count_sources:
                pe.wait_ge(zeroed.sem, zeroed.at(1))
                nc.tensor.matmul(source_ps[:, 0:TILES_P], zero_h[:, :], zero_h[:, 0:TILES_P], start=True, stop=True,
                                 skip_group_check=True)
                pe.sem_inc(tallied.sem, 2)
            with pe.Fori(0, BODIES) as i:
                for j in range(BODY):
                    pe.wait_ge(built.sem, built.at(GROUP * (j + 1)) + BSTEPS * i)
                    pe.wait_ge(added.sem, added.at(GROUP * (j + 1)) + BSTEPS * i)
                    pe.wait_ge(*gathered(mem, j, i))
                    for u in range(GROUP):
                        slot = (GROUP * j + u) % (RING * GROUP)
                        ins = nc.tensor.matmul(ps[j % RING][:, u * C:(u + 1) * C], onehot[:, slot, :],
                                               rows[:, slot * C:(slot + 1) * C], start=True, stop=True)
                    ins.then_inc(used.sem, 1)
                    if count_sources:
                        pe.wait_ge(hots.sem, hots.at(j + 1) + BODY * i)
                        for u in range(GROUP):
                            k = GROUP * (j % 2) + u
                            ins = nc.tensor.matmul(source_ps[:, 0:TILES_P], low_hot[:, k, :], high_hot[:, k, :],
                                                   start=False, stop=True, skip_group_check=True)
                        ins.then_inc(tallied.sem, 1)

        @block.vector
        def _(dve):
            dve.sem_inc(added.sem, ADDED0)
            if count_sources:
                nc.vector.memset(zero_h[:, :], 0.0).then_inc(zeroed.sem, 1)
            for k in range(GROUP * lag):
                build_onehot(nc, mem, onehot, k, mem.drel[:, k:k + 1], weight[:, k:k + 1])
            with dve.Fori(0, BODIES) as i:
                if count_sources:
                    dve.wait_ge(hots.sem, hots.at(0) + BODY * i)
                    chain = sem["dve_chain"]
                    nc.vector.tensor_copy(low_now[:, :], mem.typ[:, bass.ds(i * BSTEPS, BSTEPS)])
                    nc.vector.tensor_copy(high_now[:, :], mem.norm[:, bass.ds(i * BSTEPS, BSTEPS)])
                stage_columns(nc, mem, dve, i, lag, [(drel_now, mem.drel), (weight_now, weight)])
                for j in range(BODY):
                    add_and_build(nc, mem, dve, i, j, ps, onehot, drel_now, weight_now, lag)
                    if count_sources:
                        dve.wait_ge(tallied.sem, tallied.at(j + 1) + BODY * i)
                        for u in range(GROUP):
                            k, slot = GROUP * j + u, GROUP * (j % 2) + u
                            nc.vector.tensor_scalar(low_hot[:, slot, :], mem.iota_h[:, :], low_now[:, k:k + 1], None, ALU.is_equal)
                            ins = nc.vector.tensor_scalar(high_hot[:, slot, :], mem.iota_h[:, 0:TILES_P], high_now[:, k:k + 1],
                                                          None, ALU.is_equal)
                        ins.then_inc(hots.sem, 1)
            if count_sources:
                dve.wait_ge(tallied.sem, tallied.at(2 + BODY * BODIES))
                nc.vector.tensor_scalar(mem.src_scale[:, :], source_ps[:, 0:TILES_P], 1.0, None, ALU.add).then_inc(hots.sem, 1)

    pass_ends(mem)
    sem["index_ready"].passed(2 * BODIES), sem["dve_chain"].passed(2 * BODIES), built.passed(STEPS + GROUP * lag)
    if count_sources:
        hots.passed(BODY * BODIES + 1), tallied.passed(2 + BODY * BODIES), zeroed.passed(1)


def split_sources(nc, mem, dram):
    sem = mem.sems
    loaded, chain = sem["load"], sem["dve_chain"]
    with nc.sbuf_tensor("split_src", [P, STEPS], I32) as src, nc.sbuf_tensor("split_part", [P, STEPS], I32) as part, \
            nc.Block() as block:
        @block.sync
        def _(sp):
            sp.dma_start(src[:, :], dram["src"][0:P * STEPS].rearrange("(p c) -> p c", p=P)).then_inc(loaded.sem, 16)

        @block.vector
        def _(dve):
            link = Links(chain)
            dve.wait_ge(loaded.sem, loaded.at(16))
            nc.vector.tensor_scalar(part[:, :], src[:, :], 7, None, ALU.arith_shift_right).then_inc(*link.next())
            dve.wait_ge(*link.done())
            nc.vector.tensor_copy(mem.norm[:, 0:STEPS], part[:, :]).then_inc(*link.next())
            dve.wait_ge(*link.done())
            nc.vector.tensor_scalar(part[:, :], src[:, :], P - 1, None, ALU.bitwise_and).then_inc(*link.next())
            dve.wait_ge(*link.done())
            nc.vector.tensor_copy(mem.typ[:, 0:STEPS], part[:, :]).then_inc(*link.next())
            dve.wait_ge(*link.done())
            link.close()
    loaded.passed(16)


def relation_pass(nc, mem, dram, tag="rel", lag=3):
    ctx = ExitStack()
    per_body = 2 + 3 * BODY
    with ctx:
        sb = lambda name, shape, dt=F32: ctx.enter_context(nc.sbuf_tensor(f"{tag}_{name}", shape, dt))
        rows = sb("rows", [P, RING * GROUP * C])
        onehot = sb("onehot", [P, RING * GROUP, P])
        turned_hot = sb("turned_hot", [P, 2, GROUP, P])
        typ_now = sb("typ_now", [P, BSTEPS])
        typ_hot = sb("typ_hot", [P, 2, GROUP, R])
        picked = sb("picked", [P, 2, GROUP, R])
        norm_now = sb("norm_now", [P, 2, GROUP])
        drel_now = sb("drel_now", [P, BSTEPS])
        index_now = sb("index_now", [P, BSTEPS], I32)
        ps = [ctx.enter_context(nc.psum_tensor(f"{tag}_ps{j}", [P, 512], F32)) for j in range(RING)]
        turn_ps = [ctx.enter_context(nc.psum_tensor(f"{tag}_turn_ps{j}", [P, GROUP, P], F32)) for j in range(2)]
        pick_ps = [ctx.enter_context(nc.psum_tensor(f"{tag}_pick_ps{j}", [P, 512], F32)) for j in range(2)]
        sem = mem.sems
        used, added, built, chain = sem["used"], sem["added"], sem["built"], sem["dve_chain"]
        turned, copied, expanded, weighed, scaled = (sem["pe_done"], sem["act_done"], sem["pe_done2"], sem["dve_done"],
                                                     sem["act_done2"])
        block = ctx.enter_context(nc.Block())
        block.gpsimd(gather_program(nc, mem, dram["relation_table"], index_now, rows, C, ahead=1))


        @block.tensor
        def _(pe):
            def turn(g, i):
                pe.wait_ge(built.sem, built.at(GROUP * (g + 1)) + BSTEPS * i)
                if g >= 2:
                    pe.wait_ge(copied.sem, copied.at(g - 1) + BODY * i)
                for u in range(GROUP):
                    slot = (GROUP * g + u) % (RING * GROUP)
                    ins = nc.tensor.transpose(turn_ps[g % 2][:, u, :], onehot[:, slot, :], mem.ident[:, :])
                ins.then_inc(turned.sem, 1)

            def expand(g, i):
                tiles = tiles_of_steps(nc, mem, PE_ENGINE, i * BSTEPS + GROUP * g)
                pe.wait_ge(copied.sem, copied.at(g + 1) + BODY * i)
                if g >= 1:
                    pe.wait_ge(weighed.sem, weighed.at(g) + BODY * i)
                for u in range(GROUP):
                    ins = nc.tensor.matmul(pick_ps[g % 2][:, u * R:(u + 1) * R], turned_hot[:, g % 2, u, :],
                                           mem.counts[:, bass.ds(tiles[u] * R, R)], start=True, stop=True)
                ins.then_inc(expanded.sem, 1)

            pe.sem_inc(used.sem, USED0)
            turn(0, 0)
            turn(1, 0)
            expand(0, 0)
            with pe.Fori(0, BODIES) as i:
                for j in range(BODY):
                    turn(j + 2, i)
                    expand(j + 1, i)
                    pe.wait_ge(scaled.sem, scaled.at(j + 1) + BODY * i)
                    pe.wait_ge(added.sem, added.at(GROUP * (j + 1)) + BSTEPS * i)
                    for u in range(GROUP):
                        slot = (GROUP * j + u) % (RING * GROUP)
                        ins = nc.tensor.matmul(ps[j % RING][:, u * C:(u + 1) * C], onehot[:, slot, :],
                                               rows[:, slot * C:(slot + 1) * C], start=True, stop=True)
                    ins.then_inc(used.sem, 1)

        @block.scalar
        def _(act):
            def copy(g, i):
                act.wait_ge(turned.sem, turned.at(g + 1) + BODY * i)
                if g >= 2:
                    act.wait_ge(expanded.sem, expanded.at(g - 1) + BODY * i)
                nc.scalar.activation(turned_hot[:, g % 2, :, :], turn_ps[g % 2][:, :, :], ACT.Copy).then_inc(copied.sem, 1)

            def scale(g, i):
                act.wait_ge(weighed.sem, weighed.at(g + 1) + BODY * i)
                act.wait_ge(*gathered(mem, g, i))
                for u in range(GROUP):
                    slot = (GROUP * g + u) % (RING * GROUP)
                    row = rows[:, slot * C:(slot + 1) * C]
                    ins = nc.scalar.activation(row, row, ACT.Copy, scale=norm_now[:, g % 2, u:u + 1])
                ins.then_inc(scaled.sem, 1)

            copy(0, 0)
            copy(1, 0)
            for half in range(2):
                copy_indices(nc, mem, act, 0, half, index_now, mem.row_i)
            scale(0, 0)
            with act.Fori(0, BODIES) as i:
                for j in range(BODY):
                    copy(j + 2, i)
                    scale(j + 1, i)
                    if j in (BODY // 2 - 1, BODY - 1):
                        copy_indices(nc, mem, act, i + 1, j // (BODY // 2), index_now, mem.row_i)

        @block.vector
        def _(dve):
            def relation(g, typ_columns):
                return nc.vector.tensor_tensor(typ_hot[:, g % 2, :, :], bc(typ_columns, 2, R), bc(mem.iota[:, 0:R], 1, GROUP),
                                               ALU.is_equal).then_inc(chain.sem, 1)

            def weigh(g, i, c):
                dve.wait_ge(chain.sem, c)
                dve.wait_ge(expanded.sem, expanded.at(g + 1) + BODY * i)
                nc.vector.tensor_tensor(picked[:, g % 2, :, :],
                                        pick_ps[g % 2][:, 0:GROUP * R].rearrange("p (u r) -> p u r", r=R),
                                        typ_hot[:, g % 2, :, :], ALU.mult).then_inc(chain.sem, 1)
                dve.wait_ge(chain.sem, c + 1)
                nc.vector.tensor_reduce(norm_now[:, g % 2, :], picked[:, g % 2, :, :], AX.X, ALU.add).then_inc(weighed.sem, 1)

            dve.sem_inc(added.sem, ADDED0)
            for k in range(GROUP * lag):
                build_onehot(nc, mem, onehot, k, mem.drel[:, k:k + 1], None)
            relation(0, mem.typ[:, 0:GROUP])
            weigh(0, 0, chain.at(1))
            with dve.Fori(0, BODIES) as i:
                dve.wait_ge(built.sem, built.at(GROUP * lag) + BSTEPS * i)
                nc.vector.tensor_copy(drel_now[:, :], mem.drel[:, bass.ds(i * BSTEPS + GROUP * lag, BSTEPS)]).then_inc(chain.sem, 1)
                nc.vector.tensor_copy(typ_now[:, :], mem.typ[:, bass.ds(i * BSTEPS + GROUP, BSTEPS)]).then_inc(chain.sem, 1)
                dve.wait_ge(chain.sem, chain.at(4) + per_body * i)
                for j in range(BODY):
                    relation(j + 1, typ_now[:, GROUP * j:GROUP * (j + 1)])
                    weigh(j + 1, i, chain.at(5 + 3 * j) + per_body * i)
                    add_and_build(nc, mem, dve, i, j, ps, onehot, drel_now, None, lag)
                    nc.vector.tensor_copy(mem.norm[:, bass.ds(i * BSTEPS + GROUP * j, GROUP)],
                                          norm_now[:, j % 2, :]).then_inc(chain.sem, 1)

    pass_ends(mem, ahead=1)
    groups = BODY * BODIES
    built.passed(STEPS + GROUP * lag), chain.passed(2 + per_body * BODIES)
    turned.passed(groups + 2), copied.passed(groups + 2), expanded.passed(groups + 1)
    weighed.passed(groups + 1), scaled.passed(groups + 1), sem["index_ready"].passed(2 * BODIES + 2)


def message_pass(nc, mem, dram, tag="msg", lag=3):
    ctx = ExitStack()
    with ctx:
        sb = lambda name, shape, dt=F32: ctx.enter_context(nc.sbuf_tensor(f"{tag}_{name}", shape, dt))
        rows = sb("rows", [P, RING * GROUP * C])
        onehot = sb("onehot", [P, RING * GROUP, P])
        turned_hot = sb("turned_hot", [P, 2, GROUP, P])
        features = sb("features", [FE, RING * GROUP, P])
        feature_w = sb("feature_w", [FE, C])
        messages = sb("messages", [P, 2, GROUP * C])
        drel_now = sb("drel_now", [P, BSTEPS])
        index_now = sb("index_now", [P, BSTEPS], I32)
        ps = [ctx.enter_context(nc.psum_tensor(f"{tag}_ps{j}", [P, 512], F32)) for j in range(RING)]
        turn_ps = [ctx.enter_context(nc.psum_tensor(f"{tag}_turn_ps{j}", [P, GROUP, P], F32)) for j in range(2)]
        pre_ps = [ctx.enter_context(nc.psum_tensor(f"{tag}_pre_ps{j}", [P, 512], F32)) for j in range(2)]
        sem = mem.sems
        used, added, built, chain = sem["used"], sem["added"], sem["built"], sem["dve_chain"]
        turned, copied, joined, rectified, weights = sem["pe_done"], sem["act_done"], sem["pe_done2"], sem["act_done2"], sem["load"]
        loads = [sem["load1"], sem["load2"], sem["load3"], sem["load4"]]
        block = ctx.enter_context(nc.Block())
        block.gpsimd(gather_program(nc, mem, dram["message_table"], index_now, rows, C, ahead=1))

        @block.sync
        def _(sp):
            sp.dma_start(feature_w[:, :], dram["w_edge"]).then_inc(weights.sem, 16)

            def load_group(j, i):
                _, starts = nc.values_load_multi_w_load_instructions(
                    mem.start_row[0:1, bass.ds(i * BSTEPS + GROUP * j, GROUP)], engines=[SP_ENGINE], min_val=0, max_val=E,
                    skip_runtime_bounds_check_because="the plan caps the first edge at E")
                wait_apart(sp, mem, used.sem, used.at(j - RING + USED0 + 1) + BODY * i)
                for u in range(GROUP):
                    sp.dma_start(features[:, (GROUP * j + u) % (RING * GROUP), :],
                                 dram["features"][:, bass.ds(starts[u], P)]).then_inc(loads[j % RING].sem, 16)

            with sp.Fori(0, BODIES) as i:
                for j in range(BODY):
                    load_group(j, i)
            load_group(0, BODIES)

        @block.tensor
        def _(pe):
            def turn(g, i):
                pe.wait_ge(built.sem, built.at(GROUP * (g + 1)) + BSTEPS * i)
                if g >= 2:
                    pe.wait_ge(copied.sem, copied.at(g - 1) + BODY * i)
                for u in range(GROUP):
                    slot = (GROUP * g + u) % (RING * GROUP)
                    ins = nc.tensor.transpose(turn_ps[g % 2][:, u, :], onehot[:, slot, :], mem.ident[:, :])
                ins.then_inc(turned.sem, 1)

            def join(g, i):
                tiles = tiles_of_steps(nc, mem, PE_ENGINE, i * BSTEPS + GROUP * g)
                pe.wait_ge(copied.sem, copied.at(g + 1) + BODY * i)
                pe.wait_ge(*gathered(mem, g, i))
                landed = loads[g % RING]
                pe.wait_ge(landed.sem, landed.at(16 * GROUP * (g // RING + 1)) + 16 * GROUP * (BODY // RING) * i)
                if g >= 1:
                    pe.wait_ge(rectified.sem, rectified.at(g) + BODY * i)
                for u in range(GROUP):
                    slot = (GROUP * g + u) % (RING * GROUP)
                    out = pre_ps[g % 2][:, u * C:(u + 1) * C]
                    nc.tensor.matmul(out, features[:, slot, :], feature_w[:, :], start=True, stop=False)
                    nc.tensor.matmul(out, turned_hot[:, g % 2, u, :], mem.dst_side[:, bass.ds(tiles[u] * C, C)],
                                     start=False, stop=False)
                    ins = nc.tensor.matmul(out, mem.ident[:, :], rows[:, slot * C:(slot + 1) * C], start=False, stop=True)
                ins.then_inc(joined.sem, 1)

            pe.wait_ge(weights.sem, weights.at(16))
            pe.sem_inc(used.sem, USED0)
            turn(0, 0)
            turn(1, 0)
            join(0, 0)
            with pe.Fori(0, BODIES) as i:
                for j in range(BODY):
                    turn(j + 2, i)
                    join(j + 1, i)
                    pe.wait_ge(rectified.sem, rectified.at(j + 1) + BODY * i)
                    pe.wait_ge(added.sem, added.at(GROUP * (j + 1)) + BSTEPS * i)
                    for u in range(GROUP):
                        slot = (GROUP * j + u) % (RING * GROUP)
                        ins = nc.tensor.matmul(ps[j % RING][:, u * C:(u + 1) * C], onehot[:, slot, :],
                                               messages[:, j % 2, u * C:(u + 1) * C], start=True, stop=True)
                    ins.then_inc(used.sem, 1)

        @block.scalar
        def _(act):
            def copy(g, i):
                act.wait_ge(turned.sem, turned.at(g + 1) + BODY * i)
                if g >= 2:
                    act.wait_ge(joined.sem, joined.at(g - 1) + BODY * i)
                nc.scalar.activation(turned_hot[:, g % 2, :, :], turn_ps[g % 2][:, :, :], ACT.Copy).then_inc(copied.sem, 1)

            def rectify(g, i):
                act.wait_ge(joined.sem, joined.at(g + 1) + BODY * i)
                act.wait_ge(used.sem, used.at(USED0 + g - 1) + BODY * i)
                nc.scalar.activation(messages[:, g % 2, :], pre_ps[g % 2][:, 0:GROUP * C], ACT.Relu).then_inc(rectified.sem, 1)

            for half in range(2):
                copy_indices(nc, mem, act, 0, half, index_now, mem.src_i)
            copy(0, 0)
            copy(1, 0)
            rectify(0, 0)
            with act.Fori(0, BODIES) as i:
                for j in range(BODY):
                    copy(j + 2, i)
                    if j in (BODY // 2, BODY - 1):
                        copy_indices(nc, mem, act, i + 1, 0 if j == BODY // 2 else 1, index_now, mem.src_i)
                    rectify(j + 1, i)

        @block.vector
        def _(dve):
            dve.sem_inc(added.sem, ADDED0)
            for k in range(GROUP * lag):
                build_onehot(nc, mem, onehot, k, mem.drel[:, k:k + 1], None)
            with dve.Fori(0, BODIES) as i:
                stage_columns(nc, mem, dve, i, lag, [(drel_now, mem.drel)])
                for j in range(BODY):
                    add_and_build(nc, mem, dve, i, j, ps, onehot, drel_now, None, lag)

    pass_ends(mem, ahead=1)
    groups = BODY * BODIES
    weights.passed(16), built.passed(STEPS + GROUP * lag), chain.passed(BODIES)
    turned.passed(groups + 2), copied.passed(groups + 2), joined.passed(groups + 1), rectified.passed(groups + 1)
    sem["index_ready"].passed(2 * BODIES + 2)
    for q in loads:
        q.passed(16 * GROUP * groups // RING)
    loads[0].passed(16 * GROUP)


def load_weights(sp, mem, pairs):
    for tile, source in pairs:
        sp.dma_start(tile, source).then_inc(mem.sems["load"].sem, 16)


def unit_columns(i, width=C):
    return bass.ds(i * (UNIT * width), UNIT * width)


def unit_done(signal, s, i, per=1):
    return signal.sem, signal.at(per * (s + 3)) + 2 * per * i


def credit_units(eng, signals, per=1):
    for signal in signals:
        eng.sem_inc(signal.sem, 2 * per)


def units_passed(signals, per=1):
    for signal in signals:
        signal.passed(per * (2 + UNITS))


def unit_rows(table, u):
    return table[bass.ds(u * (UNIT * P), UNIT * P), :].rearrange("(t p) c -> p t c", p=P)


def store_units(sp, mem, ready, released, table, staged, per=1):
    stored = mem.sems["store"]
    credit_units(sp, [released])
    with sp.Fori(0, UNITS // 2) as i:
        for s in range(2):
            sp.wait_ge(*unit_done(ready, s, i, per))
            sp.dma_start(unit_rows(table, 2 * i + s), staged(s)).then_inc(stored.sem, 16)
            sp.wait_ge(stored.sem, stored.at(16 * (s + 1)) + 32 * i)
            sp.sem_inc(released.sem, 1)
    stored.passed(16 * UNITS)


def turn_unit(nc, mem, pe, s, i, started, copied, turned, h, turn_ps, width=C):
    pe.wait_ge(*unit_done(started, s, i))
    wait_apart(pe, mem, *unit_done(copied, s - 2, i))
    for t in range(UNIT):
        ins = nc.tensor.transpose(turn_ps[:, t * P:(t + 1) * P], h[:, t * width:(t + 1) * width], mem.ident[:, :])
    ins.then_inc(turned.sem, 1)


def relation_nodes(nc, mem, dram, tag, w_all, root_b, rectify):
    ctx = ExitStack()
    with ctx:
        sb = lambda name, shape, dt=F32: ctx.enter_context(nc.sbuf_tensor(f"{tag}_{name}", shape, dt))
        w_sb = sb("w", [C, R * C])
        root_sb = sb("root", [C + 1, C])
        h = sb("h", [P, 2, UNIT * C])
        h_turned = sb("h_turned", [C + 1, 2, UNIT * P])
        table = sb("table", [P, UNIT, R * C])
        turn_ps = [ctx.enter_context(nc.psum_tensor(f"{tag}_turn_ps{j}", [C, UNIT * P], F32)) for j in range(2)]
        root_ps = [ctx.enter_context(nc.psum_tensor(f"{tag}_root_ps{j}", [P, 512], F32)) for j in range(2)]
        table_ps = [ctx.enter_context(nc.psum_tensor(f"{tag}_table_ps{j}", [P, R * C], F32)) for j in range(UNIT)]
        sem = mem.sems
        weights, started, turned, copied = sem["load"], sem["act_done"], sem["pe_done"], sem["act_done2"]
        made, rooted, table_copied, released = sem["pe_done2"], sem["pe_done3"], sem["dve_done3"], sem["act_done4"]
        ones_set, acc_set = sem["made"], sem["dve_done2"]
        source = mem.acc if rectify else mem.xs
        block = ctx.enter_context(nc.Block())
        rows = dram["relation_table"].rearrange("(n r) c -> n (r c)", r=R)

        @block.sync
        def _(sp):
            load_weights(sp, mem, [(w_sb[:, :], w_all), (root_sb[:, :], root_b)])
            store_units(sp, mem, table_copied, released, rows, lambda s: table[:, :, :], per=UNIT)

        @block.scalar
        def _(act):
            credit_units(act, [started, copied])
            with act.Fori(0, UNITS // 2) as i:
                for s in range(2):
                    act.wait_ge(*unit_done(turned, s - 2, i))
                    nc.scalar.activation(h[:, s, :], source[:, unit_columns(2 * i + s)],
                                         ACT.Relu if rectify else ACT.Copy).then_inc(started.sem, 1)
                    act.wait_ge(*unit_done(turned, s, i))
                    act.wait_ge(*unit_done(rooted, s - 2, i))
                    nc.scalar.activation(h_turned[0:C, s, :], turn_ps[s][:, :], ACT.Copy).then_inc(copied.sem, 1)

        @block.vector
        def _(dve):
            nc.vector.memset(h_turned[C:C + 1, :, :], 1.0).then_inc(ones_set.sem, 1)
            credit_units(dve, [acc_set])
            credit_units(dve, [table_copied], UNIT)
            with dve.Fori(0, UNITS // 2) as i:
                for s in range(2):
                    dve.wait_ge(*unit_done(released, s - 1, i))
                    for t in range(UNIT):
                        dve.wait_ge(made.sem, made.at(2 * UNIT + UNIT * s + t + 1) + 2 * UNIT * i)
                        nc.vector.tensor_copy(table[:, t, :], table_ps[t][:, :]).then_inc(table_copied.sem, 1)
                    dve.wait_ge(*unit_done(rooted, s, i))
                    nc.vector.tensor_copy(mem.acc[:, unit_columns(2 * i + s)], root_ps[s][:, 0:UNIT * C]).then_inc(acc_set.sem, 1)

        @block.tensor
        def _(pe):
            pe.wait_ge(weights.sem, weights.at(32))
            pe.wait_ge(ones_set.sem, ones_set.at(1))
            credit_units(pe, [turned, rooted])
            credit_units(pe, [made], UNIT)
            with pe.Fori(0, UNITS // 2) as i:
                for s in range(2):
                    turn_unit(nc, mem, pe, s, i, started, copied, turned, h[:, s, :], turn_ps[s])
                    pe.wait_ge(*unit_done(copied, s, i))
                    pe.wait_ge(*unit_done(acc_set, s - 2, i))
                    for t in range(UNIT):
                        turned_t = h_turned[:, s, t * P:(t + 1) * P]
                        pe.wait_ge(table_copied.sem, table_copied.at(2 * UNIT + UNIT * (s - 1) + t + 1) + 2 * UNIT * i)
                        nc.tensor.matmul(table_ps[t][:, :], turned_t[0:C, :], w_sb[:, :], start=True, stop=True).then_inc(made.sem, 1)
                        ins = nc.tensor.matmul(root_ps[s][:, t * C:(t + 1) * C], turned_t, root_sb[:, :], start=True, stop=True)
                    ins.then_inc(rooted.sem, 1)

    weights.passed(32), ones_set.passed(1)
    units_passed([started, turned, copied, rooted, released, acc_set])
    units_passed([made, table_copied], UNIT)


def project_nodes(nc, mem, dram, tag, table, width, w_all, by_source_degree):
    ctx = ExitStack()
    with ctx:
        sb = lambda name, shape, dt=F32: ctx.enter_context(nc.sbuf_tensor(f"{tag}_{name}", shape, dt))
        w_sb = sb("w", [C + 1, P])
        h = sb("h", [P, 2, UNIT * C])
        h_turned = sb("h_turned", [C + 1, 2, UNIT * P])
        staged = sb("staged", [P, 2, UNIT, width])
        turn_ps = [ctx.enter_context(nc.psum_tensor(f"{tag}_turn_ps{j}", [C, UNIT * P], F32)) for j in range(2)]
        out_ps = [ctx.enter_context(nc.psum_tensor(f"{tag}_out_ps{j}", [P, UNIT, P], F32)) for j in range(2)]
        sem = mem.sems
        weights, started, turned, copied = sem["load"], sem["act_done"], sem["pe_done"], sem["act_done2"]
        projected, taken, released, ones_set, chain = (sem["pe_done2"], sem["dve_done"], sem["dve_done2"], sem["made"],
                                                       sem["dve_chain"])
        block = ctx.enter_context(nc.Block())

        @block.sync
        def _(sp):
            load_weights(sp, mem, [(w_sb[:, :], w_all)])
            store_units(sp, mem, taken, released, table, lambda s: staged[:, s, :, :])

        @block.scalar
        def _(act):
            credit_units(act, [started, copied])
            with act.Fori(0, UNITS // 2) as i:
                for s in range(2):
                    act.wait_ge(*unit_done(turned, s - 2, i))
                    nc.scalar.activation(h[:, s, :], mem.xs[:, unit_columns(2 * i + s)], ACT.Copy).then_inc(started.sem, 1)
                    act.wait_ge(*unit_done(turned, s, i))
                    act.wait_ge(*unit_done(projected, s - 2, i))
                    nc.scalar.activation(h_turned[0:C, s, :], turn_ps[s][:, :], ACT.Copy).then_inc(copied.sem, 1)

        @block.vector
        def _(dve):
            nc.vector.memset(h_turned[C:C + 1, :, :], 1.0).then_inc(ones_set.sem, 1)
            if not by_source_degree:
                nc.vector.memset(mem.acc[:, :], 0.0).then_inc(chain.sem, 1)
            credit_units(dve, [taken])
            side = P - width
            with dve.Fori(0, UNITS // 2) as i:
                for s in range(2):
                    dve.wait_ge(*unit_done(projected, s, i))
                    dve.wait_ge(*unit_done(released, s - 2, i))
                    nc.vector.tensor_copy(mem.dst_side[:, unit_columns(2 * i + s, side)],
                                          out_ps[s][:, :, width:P])
                    if by_source_degree:
                        nc.vector.tensor_copy(staged[:, s, :, C:width], out_ps[s][:, :, C:width])
                        scale = mem.src_scale[:, bass.ds((2 * i + s) * UNIT, UNIT)]
                        nc.vector.tensor_tensor(mem.acc[:, unit_columns(2 * i + s)], out_ps[s][:, :, 0:C], bc(scale, 2, C),
                                                ALU.mult)
                        nc.vector.tensor_tensor(staged[:, s, :, 0:C], out_ps[s][:, :, 0:C], bc(scale, 2, C),
                                                ALU.mult).then_inc(taken.sem, 1)
                    else:
                        nc.vector.tensor_copy(staged[:, s, :, :], out_ps[s][:, :, 0:width]).then_inc(taken.sem, 1)

        @block.tensor
        def _(pe):
            pe.wait_ge(weights.sem, weights.at(16))
            pe.wait_ge(ones_set.sem, ones_set.at(1))
            credit_units(pe, [turned, projected])
            with pe.Fori(0, UNITS // 2) as i:
                for s in range(2):
                    turn_unit(nc, mem, pe, s, i, started, copied, turned, h[:, s, :], turn_ps[s])
                    pe.wait_ge(*unit_done(copied, s, i))
                    pe.wait_ge(*unit_done(taken, s - 2, i))
                    for t in range(UNIT):
                        ins = nc.tensor.matmul(out_ps[s][:, t, :], h_turned[:, s, t * P:(t + 1) * P], w_sb[:, :],
                                               start=True, stop=True)
                    ins.then_inc(projected.sem, 1)

    weights.passed(16), ones_set.passed(1)
    units_passed([started, turned, copied, projected, taken, released])
    if not by_source_degree:
        chain.passed(1)


def mlp_nodes(nc, mem, dram, tag, table, hidden, w1, w2, b2, last):
    ctx = ExitStack()
    with ctx:
        sb = lambda name, shape, dt=F32: ctx.enter_context(nc.sbuf_tensor(f"{tag}_{name}", shape, dt))
        w1_sb = sb("w1", [C + 1, hidden])
        w2_sb = sb("w2", [hidden, C])
        b2_sb = sb("b2", [1, C])
        ones = sb("ones", [1, P])
        h = sb("h", [P, 2, UNIT * C])
        h_turned = sb("h_turned", [C + 1, 2, UNIT * P])
        inner = sb("inner", [hidden, 2, UNIT * P])
        staged = sb("staged", [P, 2, UNIT * C])
        turn_ps = [ctx.enter_context(nc.psum_tensor(f"{tag}_turn_ps{j}", [C, UNIT * P], F32)) for j in range(2)]
        inner_ps = [ctx.enter_context(nc.psum_tensor(f"{tag}_inner_ps{j}", [hidden, UNIT * P], F32)) for j in range(2)]
        out_ps = [ctx.enter_context(nc.psum_tensor(f"{tag}_out_ps{j}", [P, UNIT * C], F32)) for j in range(2)]
        sem = mem.sems
        weights, started, turned, copied = sem["load"], sem["act_done"], sem["pe_done"], sem["act_done2"]
        widened, rectified, narrowed = sem["pe_done2"], sem["act_done3"], sem["pe_done3"]
        staged_set, acc_set, released, ones_set = sem["act_done4"], sem["dve_done"], sem["dve_done2"], sem["made"]
        block = ctx.enter_context(nc.Block())

        @block.sync
        def _(sp):
            load_weights(sp, mem, [(w1_sb[:, :], w1), (w2_sb[:, :], w2), (b2_sb[:, :], b2)])
            if not last:
                store_units(sp, mem, staged_set, released, table,
                            lambda s: staged[:, s, :].rearrange("p (t c) -> p t c", c=C))

        @block.scalar
        def _(act):
            credit_units(act, [started, copied, rectified] + [staged_set] * (not last))
            with act.Fori(0, UNITS // 2) as i:
                for s in range(2):
                    act.wait_ge(*unit_done(turned, s - 2, i))
                    nc.scalar.activation(h[:, s, :], mem.acc[:, unit_columns(2 * i + s)], ACT.Copy).then_inc(started.sem, 1)
                    act.wait_ge(*unit_done(turned, s, i))
                    act.wait_ge(*unit_done(widened, s - 2, i))
                    nc.scalar.activation(h_turned[0:C, s, :], turn_ps[s][:, :], ACT.Copy).then_inc(copied.sem, 1)
                    act.wait_ge(*unit_done(widened, s, i))
                    act.wait_ge(*unit_done(narrowed, s - 2, i))
                    nc.scalar.activation(inner[:, s, :], inner_ps[s][:, :], ACT.Relu).then_inc(rectified.sem, 1)
                    if not last:
                        act.wait_ge(*unit_done(narrowed, s, i))
                        act.wait_ge(*unit_done(released, s - 2, i))
                        act.wait_ge(*unit_done(acc_set, s - 2, i))
                        nc.scalar.activation(staged[:, s, :], out_ps[s][:, :], ACT.Relu).then_inc(staged_set.sem, 1)

        @block.vector
        def _(dve):
            nc.vector.memset(h_turned[C:C + 1, :, :], 1.0).then_inc(ones_set.sem, 1)
            nc.vector.memset(ones[:, :], 1.0).then_inc(ones_set.sem, 1)
            credit_units(dve, [acc_set])
            with dve.Fori(0, UNITS // 2) as i:
                for s in range(2):
                    if last:
                        dve.wait_ge(*unit_done(narrowed, s, i))
                        nc.vector.tensor_tensor(mem.acc[:, unit_columns(2 * i + s)], out_ps[s][:, :],
                                                mem.xs[:, unit_columns(2 * i + s)], ALU.add).then_inc(acc_set.sem, 1)
                    else:
                        dve.wait_ge(*unit_done(staged_set, s, i))
                        nc.vector.tensor_copy(mem.acc[:, unit_columns(2 * i + s)], staged[:, s, :]).then_inc(acc_set.sem, 1)

        @block.tensor
        def _(pe):
            pe.wait_ge(weights.sem, weights.at(48))
            pe.wait_ge(ones_set.sem, ones_set.at(2))
            credit_units(pe, [turned, widened, narrowed])
            with pe.Fori(0, UNITS // 2) as i:
                for s in range(2):
                    turn_unit(nc, mem, pe, s, i, started, copied, turned, h[:, s, :], turn_ps[s])
                    pe.wait_ge(*unit_done(copied, s, i))
                    pe.wait_ge(*unit_done(rectified, s - 2, i))
                    nc.tensor.matmul(inner_ps[s][:, :], w1_sb[:, :], h_turned[:, s, :], start=True, stop=True).then_inc(widened.sem, 1)
                    pe.wait_ge(*unit_done(rectified, s, i))
                    if last:
                        pe.wait_ge(*unit_done(acc_set, s - 2, i))
                    else:
                        pe.wait_ge(*unit_done(staged_set, s - 2, i))
                    for t in range(UNIT):
                        out = out_ps[s][:, t * C:(t + 1) * C]
                        nc.tensor.matmul(out, ones[:, :], b2_sb[:, :], start=True, stop=False)
                        ins = nc.tensor.matmul(out, inner[:, s, t * P:(t + 1) * P], w2_sb[:, :], start=False, stop=True)
                    ins.then_inc(narrowed.sem, 1)

    weights.passed(48), ones_set.passed(2)
    units_passed([started, turned, copied, widened, rectified, narrowed, acc_set])
    if not last:
        units_passed([staged_set, released])


def gru_nodes(nc, mem, dram, tag="gru"):
    ctx = ExitStack()
    W = C + 1
    with ctx:
        sb = lambda name, shape, dt=F32: ctx.enter_context(nc.sbuf_tensor(f"{tag}_{name}", shape, dt))
        w2_sb = sb("w2", [W, C])
        wi_sb = sb("wi", [W, 3 * C])
        wh_sb = sb("wh", [W, 3 * C])
        sums = sb("sums", [P, 2, UNIT, W])
        h = sb("h", [P, 2, UNIT * C])
        sums_turned = sb("sums_turned", [W, 2, UNIT * P])
        h_turned = sb("h_turned", [W, 2, UNIT * P])
        agg = sb("agg", [W, 2, UNIT * P])
        gates = sb("gates", [P, 2, UNIT, 2 * C])
        fresh = sb("fresh", [P, 2, UNIT, C])
        blend = sb("blend", [P, 2, UNIT, C])
        turn_ps = [ctx.enter_context(nc.psum_tensor(f"{tag}_turn_ps{j}", [W, UNIT * P], F32)) for j in range(2)]
        agg_ps = ctx.enter_context(nc.psum_tensor(f"{tag}_agg_ps", [C, UNIT * P], F32))
        gate_ps = [ctx.enter_context(nc.psum_tensor(f"{tag}_gate_ps{j}", [P, UNIT, 2 * C], F32)) for j in range(2)]
        fresh_ps = [ctx.enter_context(nc.psum_tensor(f"{tag}_fresh_ps{j}", [P, UNIT, 2, C], F32)) for j in range(2)]
        sem = mem.sems
        weights, started, turned, copied = sem["load"], sem["act_done"], sem["pe_done"], sem["act_done2"]
        summed, summed_copied, gated, opened = sem["pe_done2"], sem["act_done3"], sem["pe_done3"], sem["act_done4"]
        mixed, squashed, acc_set, ones_set, chain = (sem["dve_done"], sem["act_done5"], sem["dve_done2"], sem["made"],
                                                     sem["dve_chain"])
        block = ctx.enter_context(nc.Block())

        @block.sync
        def _(sp):
            load_weights(sp, mem, [(w2_sb[:, :], dram["w2_msg"]), (wi_sb[:, :], dram["w_ih"]), (wh_sb[:, :], dram["w_hh"])])

        @block.scalar
        def _(act):
            credit_units(act, [started, copied, summed_copied, opened, squashed])
            with act.Fori(0, UNITS // 2) as i:
                for s in range(2):
                    u = 2 * i + s
                    act.wait_ge(*unit_done(turned, s - 2, i))
                    nc.scalar.activation(sums[:, s, :, 0:C], mem.acc[:, unit_columns(u)].rearrange("p (t c) -> p t c", c=C), ACT.Copy)
                    nc.scalar.activation(sums[:, s, :, C:W], mem.degree[:, bass.ds(u * UNIT, UNIT)].unsqueeze(2), ACT.Copy)
                    act.wait_ge(*unit_done(acc_set, s - 2, i))
                    nc.scalar.activation(h[:, s, :], mem.xs[:, unit_columns(u)], ACT.Copy).then_inc(started.sem, 1)
                    act.wait_ge(*unit_done(turned, s, i))
                    act.wait_ge(*unit_done(gated, s - 2, i))
                    nc.scalar.activation(sums_turned[:, s, :], turn_ps[0][:, :], ACT.Copy)
                    nc.scalar.activation(h_turned[0:C, s, :], turn_ps[1][0:C, :], ACT.Copy).then_inc(copied.sem, 1)
                    act.wait_ge(*unit_done(summed, s, i))
                    nc.scalar.activation(agg[0:C, s, :], agg_ps[:, :], ACT.Copy).then_inc(summed_copied.sem, 1)
                    act.wait_ge(*unit_done(gated, s, i))
                    act.wait_ge(*unit_done(acc_set, s - 2, i))
                    nc.scalar.activation(gates[:, s, :, :], gate_ps[s][:, :, :], ACT.Sigmoid).then_inc(opened.sem, 1)
                    act.wait_ge(*unit_done(mixed, s, i))
                    nc.scalar.activation(fresh[:, s, :, :], blend[:, s, :, :], ACT.Tanh).then_inc(squashed.sem, 1)

        @block.vector
        def _(dve):
            nc.vector.memset(h_turned[C:W, :, :], 1.0).then_inc(ones_set.sem, 1)
            nc.vector.memset(agg[C:W, :, :], 1.0).then_inc(ones_set.sem, 1)
            credit_units(dve, [mixed, acc_set])
            with dve.Fori(0, UNITS // 2) as i:
                for s in range(2):
                    c = 4 * s
                    dve.wait_ge(*unit_done(opened, s, i))
                    nc.vector.tensor_tensor(blend[:, s, :, :], gates[:, s, :, 0:C], fresh_ps[s][:, :, 1, :], ALU.mult).then_inc(chain.sem, 1)
                    dve.wait_ge(chain.sem, chain.at(c + 1) + 8 * i)
                    nc.vector.tensor_tensor(blend[:, s, :, :], blend[:, s, :, :], fresh_ps[s][:, :, 0, :], ALU.add).then_inc(mixed.sem, 1)
                    dve.wait_ge(*unit_done(squashed, s, i))
                    x = h[:, s, :].rearrange("p (t c) -> p t c", c=C)
                    nc.vector.tensor_tensor(blend[:, s, :, :], x, fresh[:, s, :, :], ALU.subtract).then_inc(chain.sem, 1)
                    dve.wait_ge(chain.sem, chain.at(c + 2) + 8 * i)
                    nc.vector.tensor_tensor(blend[:, s, :, :], blend[:, s, :, :], gates[:, s, :, C:2 * C], ALU.mult).then_inc(chain.sem, 1)
                    dve.wait_ge(chain.sem, chain.at(c + 3) + 8 * i)
                    nc.vector.tensor_tensor(blend[:, s, :, :], blend[:, s, :, :], fresh[:, s, :, :], ALU.add).then_inc(chain.sem, 1)
                    dve.wait_ge(chain.sem, chain.at(c + 4) + 8 * i)
                    nc.vector.tensor_tensor(mem.acc[:, unit_columns(2 * i + s)].rearrange("p (t c) -> p t c", c=C),
                                            blend[:, s, :, :], x, ALU.add).then_inc(acc_set.sem, 1)

        @block.tensor
        def _(pe):
            pe.wait_ge(weights.sem, weights.at(48))
            pe.wait_ge(ones_set.sem, ones_set.at(2))
            credit_units(pe, [turned, summed, gated])
            with pe.Fori(0, UNITS // 2) as i:
                for s in range(2):
                    pe.wait_ge(*unit_done(started, s, i))
                    pe.wait_ge(*unit_done(copied, s - 1, i))
                    for t in range(UNIT):
                        nc.tensor.transpose(turn_ps[0][:, t * P:(t + 1) * P], sums[:, s, t, :], mem.ident[:, :])
                        ins = nc.tensor.transpose(turn_ps[1][0:C, t * P:(t + 1) * P], h[:, s, t * C:(t + 1) * C], mem.ident[:, :])
                    ins.then_inc(turned.sem, 1)
                    pe.wait_ge(*unit_done(copied, s, i))
                    pe.wait_ge(*unit_done(summed_copied, s - 1, i))
                    nc.tensor.matmul(agg_ps[:, :], w2_sb[:, :], sums_turned[:, s, :], start=True, stop=True).then_inc(summed.sem, 1)
                    pe.wait_ge(*unit_done(summed_copied, s, i))
                    pe.wait_ge(*unit_done(mixed, s - 2, i))
                    for t in range(UNIT):
                        cols = slice(t * P, (t + 1) * P)
                        nc.tensor.matmul(gate_ps[s][:, t, :], agg[:, s, cols], wi_sb[:, 0:2 * C], start=True, stop=False)
                        nc.tensor.matmul(gate_ps[s][:, t, :], h_turned[:, s, cols], wh_sb[:, 0:2 * C], start=False, stop=True)
                        nc.tensor.matmul(fresh_ps[s][:, t, 0, :], agg[:, s, cols], wi_sb[:, 2 * C:], start=True, stop=True)
                        ins = nc.tensor.matmul(fresh_ps[s][:, t, 1, :], h_turned[:, s, cols], wh_sb[:, 2 * C:], start=True, stop=True)
                    ins.then_inc(gated.sem, 1)

    weights.passed(48), ones_set.passed(2), chain.passed(4 * UNITS)
    units_passed([started, turned, copied, summed, summed_copied, gated, opened, mixed, squashed, acc_set])


def layernorm(nc, mem, tag, table=None):
    ctx = ExitStack()
    with ctx:
        sb = lambda name, shape, dt=F32: ctx.enter_context(nc.sbuf_tensor(f"{tag}_{name}", shape, dt))
        parts = 2
        T = TILES_P // parts
        squares = sb("squares", [P, T * C])
        mean = sb("mean", [P, parts, T])
        var = sb("var", [P, parts, T])
        dev = sb("dev", [P, parts, T])
        sem = mem.sems
        chain, centred, rooted, squared, done, stored, scaled = (sem["dve_chain"], sem["dve_done"], sem["act_done"], sem["act_done2"],
                                                         sem["dve_done2"], sem["store"], sem["dve_done3"])
        block = ctx.enter_context(nc.Block())
        view = lambda m, q: m[:, q * T * C:(q + 1) * T * C].rearrange("p (t c) -> p t c", c=C)

        @block.scalar
        def _(act):
            for q in range(parts):
                act.wait_ge(centred.sem, centred.at(2 * q + 1))
                nc.scalar.activation(squares[:, :], mem.acc[:, q * T * C:(q + 1) * T * C], ACT.Square).then_inc(squared.sem, 1)
                act.wait_ge(centred.sem, centred.at(2 * q + 2))
                nc.scalar.activation(dev[:, q, :], var[:, q, :], ACT.Sqrt).then_inc(rooted.sem, 1)

        @block.vector
        def _(dve):
            link = Links(chain)
            for q in range(parts):
                x = view(mem.acc, q)
                nc.vector.tensor_reduce(mean[:, q, :], x, AX.X, ALU.add).then_inc(*link.next())
                dve.wait_ge(*link.done())
                nc.vector.tensor_scalar(mean[:, q, :], mean[:, q, :], 1.0 / C, None, ALU.mult).then_inc(*link.next())
                dve.wait_ge(*link.done())
                nc.vector.tensor_tensor(x, x, bc(mean[:, q, :], 2, C), ALU.subtract).then_inc(centred.sem, 1)
                dve.wait_ge(squared.sem, squared.at(q + 1))
                nc.vector.tensor_reduce(var[:, q, :], squares[:, :].rearrange("p (t c) -> p t c", c=C), AX.X, ALU.add).then_inc(*link.next())
                dve.wait_ge(*link.done())
                nc.vector.tensor_scalar(var[:, q, :], var[:, q, :], 1.0 / C, EPS, ALU.mult, ALU.add).then_inc(centred.sem, 1)
                dve.wait_ge(rooted.sem, rooted.at(q + 1))
                nc.vector.reciprocal(dev[:, q, :], dev[:, q, :]).then_inc(*link.next())
                dve.wait_ge(*link.done())
                nc.vector.tensor_tensor(view(mem.xs, q), x, bc(dev[:, q, :], 2, C), ALU.mult).then_inc(done.sem, 1)
                if table is not None:
                    dve.wait_ge(done.sem, done.at(q + 1))
                    nc.vector.tensor_copy(x, view(mem.xs, q)).then_inc(scaled.sem, 1)
            link.close()

        if table is not None:
            @block.sync
            def _(sp):
                for q in range(parts):
                    sp.wait_ge(done.sem, done.at(q + 1))
                    sp.dma_start(table[q * T * P:(q + 1) * T * P, :].rearrange("(t p) c -> p t c", p=P),
                                 view(mem.xs, q)).then_inc(stored.sem, 16)
                sp.wait_ge(stored.sem, stored.at(16 * parts))

    centred.passed(2 * parts), squared.passed(parts), rooted.passed(parts), done.passed(parts)
    if table is not None:
        scaled.passed(parts), stored.passed(16 * parts)


def residual_sum(nc, mem, tag):
    done = mem.sems["dve_done"]
    with nc.Block() as block:
        @block.vector
        def _(dve):
            nc.vector.tensor_tensor(mem.acc[:, :], mem.acc[:, :], mem.xs[:, :], ALU.add).then_inc(done.sem, 1)
    done.passed(1)


def sheaf_pass(nc, mem, dram, tag="sheaf"):
    ctx = ExitStack()
    B, SB = BATCH, SHEAF_BODY
    GB = B // GROUP
    D, H = 4, C // 4
    F = 2 * B
    with ctx:
        sb = lambda name, shape, dt=F32: ctx.enter_context(nc.sbuf_tensor(f"{tag}_{name}", shape, dt))
        rows = sb("rows", [P, SB * B * TROW])
        onehot = [table[:, :].rearrange("p (u n) -> p u n", n=P) for table in (mem.typ, mem.norm)]
        turned_hot = sb("turned_hot", [P, 2, GROUP, P])
        side_now = sb("side_now", [P, 2, GROUP, 2 * HID])
        hidden = sb("hidden", [2 * HID + 1, 2, GROUP * P])
        w2_sb = sb("w2", [2 * HID + 1, 2 * NPAR])
        drel_now = sb("drel_now", [P, SB * B])
        index_now = sb("index_now", [P, SB * B], I32)
        par = sb("par", [P, 2, NPAR, F])
        cols = sb("cols", [P, 6, D, F])
        prods = sb("prods", [P, 4, D, F])
        halves = sb("halves", [P, 4, 2, F])
        norms = sb("norms", [P, D, F])
        roots = sb("roots", [P, D, F])
        dots = sb("dots", [P, 2, F])
        small = sb("small", [P, 4, F])
        maps = sb("maps", [P, D, D, F])
        outer = sb("outer", [P, D, D * D * B])
        pair = sb("pair", [P, 2, D * D * B])
        both = sb("both", [P, D * D, B])
        parts = sb("parts", [P, D, GROUP * C])
        part2 = sb("part2", [P, 2, GROUP * C])
        messages = mem.ew[:, 0:B * C].rearrange("p (g w) -> p g w", g=GB)
        turn_ps = [ctx.enter_context(nc.psum_tensor(f"{tag}_turn_ps{j}", [P, GROUP, P], F32)) for j in range(2)]
        hidden_ps = [ctx.enter_context(nc.psum_tensor(f"{tag}_hidden_ps{j}", [2 * HID, GROUP * P], F32)) for j in range(2)]
        par_ps = [ctx.enter_context(nc.psum_tensor(f"{tag}_par_ps{j}", [P, 512], F32)) for j in range(2)]
        sum_ps = [ctx.enter_context(nc.psum_tensor(f"{tag}_sum_ps{j}", [P, 512], F32)) for j in range(2)]
        sem = mem.sems
        weights, ones_set, chain = sem["load"], sem["made"], sem["dve_chain"]
        built, turned, copied, joined, rectified = sem["built"], sem["pe_done"], sem["act_done"], sem["pe_done2"], sem["act_done2"]
        widened, taken, indices, batch_read = sem["pe_done3"], sem["act_done3"], sem["index_ready"], sem["dve_done"]
        normed, rooted, message_ready, used, added = (sem["dve_done2"], sem["act_done4"], sem["dve_done3"], sem["used"],
                                                      sem["added"])
        gathers = [sem[f"gather{q}"] for q in range(4)]
        block = ctx.enter_context(nc.Block())


        @block.sync
        def _(sp):
            load_weights(sp, mem, [(w2_sb[:, :], dram["w2_sheaf"])])

        @block.gpsimd
        def _(pool):
            with pool.Fori(0, SHEAF_BODIES) as i:
                for s in range(SB):
                    wait_apart(pool, mem, indices.sem, indices.at(s + 1) + SB * i)
                    wait_apart(pool, mem, batch_read.sem, batch_read.at(s + 2) + SB * i)
                    for u in range(B):
                        slot = s * B + u
                        nc.gpsimd.indirect_dma_start(
                            out=rows[:, slot * TROW:(slot + 1) * TROW], out_offset=None, in_=dram["sheaf_table"],
                            in_offset=bass.IndirectOffsetOnAxis(ap=index_now[:, slot:slot + 1], axis=0),
                        ).then_inc(gathers[s].sem, 16)
            wait_apart(pool, mem, indices.sem, indices.at(1) + SB * SHEAF_BODIES)
            wait_apart(pool, mem, batch_read.sem, batch_read.at(2) + SB * SHEAF_BODIES)
            for u in range(B):
                nc.gpsimd.indirect_dma_start(
                    out=rows[:, u * TROW:(u + 1) * TROW], out_offset=None, in_=dram["sheaf_table"],
                    in_offset=bass.IndirectOffsetOnAxis(ap=index_now[:, u:u + 1], axis=0),
                ).then_inc(gathers[0].sem, 16)

        def gathered_batch(s, i):
            g = gathers[s % SB]
            return g.sem, g.at(16 * B * (s // SB + 1)) + 16 * B * i

        @block.scalar
        def _(act):
            def copy(s, g, i):
                n = GB * s + g
                tiles = tiles_of_steps(nc, mem, ACT_ENGINE, i * (SB * B) + GROUP * n)
                act.wait_ge(turned.sem, turned.at(n + 1) + SB * GB * i)
                act.wait_ge(joined.sem, joined.at(n + 1) + SB * GB * i)
                nc.scalar.activation(turned_hot[:, n % 2, :, :], turn_ps[n % 2][:, :, :], ACT.Copy)
                for u in range(GROUP):
                    ins = nc.scalar.activation(side_now[:, n % 2, u, :],
                                               mem.dst_side[:, bass.ds(tiles[u] * (2 * HID), 2 * HID)], ACT.Copy)
                ins.then_inc(copied.sem, 1)

            def rectify(s, g, i):
                n = GB * s + g
                act.wait_ge(joined.sem, joined.at(n + 3) + SB * GB * i)
                act.wait_ge(widened.sem, widened.at(n + 1) + SB * GB * i)
                nc.scalar.activation(hidden[0:2 * HID, n % 2, :], hidden_ps[n % 2][:, :], ACT.Relu).then_inc(rectified.sem, 1)

            def take(s, i):
                act.wait_ge(widened.sem, widened.at(2 + GB * (s + 1)) + SB * GB * i)
                act.wait_ge(batch_read.sem, batch_read.at(s + SB) + SB * i)
                nc.scalar.activation(par[:, s % 2, :, :].rearrange("p f (m u) -> p u f m", u=B),
                                     par_ps[s % 2][:, 0:B * 2 * NPAR].rearrange("p (u f m) -> p u f m", u=B, m=2),
                                     ACT.Copy).then_inc(taken.sem, 1)

            def front(s, i):
                copy(s, 0, i)
                for g in range(1, GB):
                    copy(s, g, i)
                    rectify(s, g - 1, i)
                rectify(s, GB - 1, i)
                take(s, i)

            def place_indices(s, i):
                act.wait_ge(batch_read.sem, batch_read.at(s + 2) + SB * i)
                nc.scalar.activation(index_now[:, (s % SB) * B:(s % SB + 1) * B], mem.src_i[:, bass.ds(i * (SB * B) + s * B, B)],
                                     ACT.Copy).then_inc(indices.sem, 1)

            for s in range(SB):
                place_indices(s, 0)
            front(0, 0)
            with act.Fori(0, SHEAF_BODIES) as i:
                for s in range(SB):
                    front(s + 1, i)
                    act.wait_ge(normed.sem, normed.at(s + 1) + SB * i)
                    nc.scalar.activation(roots[:, :, :], norms[:, :, :], ACT.Sqrt).then_inc(rooted.sem, 1)
                    if s > 0:
                        place_indices(SB + s - 1, i)
                place_indices(SB + SB - 1, i)

        @block.tensor
        def _(pe):
            def turn(s, g, i):
                n = GB * s + g
                pe.wait_ge(built.sem, built.at(GROUP * (n + 1)) + SB * B * i)
                pe.wait_ge(copied.sem, copied.at(n + 1) + SB * GB * i)
                for u in range(GROUP):
                    ins = nc.tensor.transpose(turn_ps[n % 2][:, u, :], onehot[s % 2][:, GROUP * g + u, :], mem.ident[:, :])
                ins.then_inc(turned.sem, 1)

            def join(s, g, i):
                n = GB * s + g
                pe.wait_ge(copied.sem, copied.at(n + 3) + SB * GB * i)
                pe.wait_ge(rectified.sem, rectified.at(n + 1) + SB * GB * i)
                if g == 0:
                    pe.wait_ge(*gathered_batch(s, i))
                for u in range(GROUP):
                    slot = (s % SB) * B + GROUP * g + u
                    out = hidden_ps[n % 2][:, u * P:(u + 1) * P]
                    nc.tensor.matmul(out, side_now[:, n % 2, u, :], turned_hot[:, n % 2, u, :], start=True, stop=False)
                    ins = nc.tensor.matmul(out, rows[:, slot * TROW + C:(slot + 1) * TROW], mem.ident[:, :], start=False, stop=True)
                ins.then_inc(joined.sem, 1)

            def widen(s, g, i):
                n = GB * s + g
                pe.wait_ge(rectified.sem, rectified.at(n + 3) + SB * GB * i)
                if g == 0:
                    pe.wait_ge(taken.sem, taken.at(s + 1) + SB * i)
                for u in range(GROUP):
                    at = (GROUP * g + u) * 2 * NPAR
                    ins = nc.tensor.matmul(par_ps[s % 2][:, at:at + 2 * NPAR], hidden[:, n % 2, u * P:(u + 1) * P], w2_sb[:, :],
                                           start=True, stop=True)
                ins.then_inc(widened.sem, 1)

            def front(s, i):
                turn(s, 0, i)
                turn(s, 1, i)
                join(s, 0, i)
                for g in range(2, GB):
                    turn(s, g, i)
                    join(s, g - 1, i)
                    widen(s, g - 2, i)
                join(s, GB - 1, i)
                widen(s, GB - 2, i)
                widen(s, GB - 1, i)

            def add_up(s, i):
                for g in range(GB):
                    pe.wait_ge(message_ready.sem, message_ready.at(GB * s + g + 1) + SB * GB * i)
                    for u in range(GROUP):
                        at = (g % 2) * GROUP * C + u * C
                        ins = nc.tensor.matmul(sum_ps[g // 2][:, at:at + C], onehot[s % 2][:, GROUP * g + u, :],
                                               messages[:, g, u * C:(u + 1) * C], start=True, stop=True)
                    ins.then_inc(used.sem, 1)

            pe.wait_ge(weights.sem, weights.at(16))
            pe.wait_ge(ones_set.sem, ones_set.at(1))
            pe.sem_inc(joined.sem, 2)
            pe.sem_inc(widened.sem, 2)
            front(0, 0)
            with pe.Fori(0, SHEAF_BODIES) as i:
                for s in range(SB):
                    front(s + 1, i)
                    add_up(s, i)

        per_body = 1 + SB * SHEAF_LINKS

        @block.vector
        def _(dve):
            def build(s, g, columns):
                for u in range(GROUP):
                    nc.vector.tensor_scalar(onehot[s % 2][:, GROUP * g + u, :], mem.iota[:, :],
                                            columns[:, GROUP * g + u:GROUP * g + u + 1], None, ALU.is_equal).then_inc(built.sem, 1)

            def algebra(s, i, link):
                p0, p1, p3, p2, p4, p5 = (par[:, s % 2, f, :] for f in range(NPAR))
                w, v, u = cols[:, 0:4:3], cols[:, 4:6], cols[:, 1:3]
                nc.vector.tensor_copy(cols[:, 0, 1:4, :], par[:, s % 2, 0:3, :]).then_inc(*link.next())
                nc.vector.tensor_copy(cols[:, 4, 2:4, :], par[:, s % 2, 3:5, :]).then_inc(*link.next())
                nc.vector.tensor_scalar(cols[:, 3, 2, :], p5, -1.0, None, ALU.mult).then_inc(*link.next())
                nc.vector.tensor_scalar(cols[:, 5, 1, :], p2, -1.0, None, ALU.mult).then_inc(*link.next())
                nc.vector.tensor_tensor(small[:, 0, :], p2, p0, ALU.mult).then_inc(*link.next())
                nc.vector.tensor_tensor(small[:, 1, :], p2, p5, ALU.mult).then_inc(*link.next())
                nc.vector.tensor_tensor(small[:, 2, :], p1, p5, ALU.mult).then_inc(*link.next())
                dve.wait_ge(*link.done())
                nc.vector.tensor_tensor(cols[:, 3, 1, :], small[:, 1, :], p4, ALU.subtract).then_inc(*link.next())
                nc.vector.tensor_tensor(cols[:, 5, 0, :], small[:, 0, :], p1, ALU.subtract).then_inc(*link.next())
                dve.wait_ge(*link.done())
                nc.vector.tensor_tensor(small[:, 3, :], cols[:, 3, 1, :], p0, ALU.mult).then_inc(*link.next())
                dve.wait_ge(*link.done())
                nc.vector.tensor_tensor(small[:, 3, :], small[:, 3, :], small[:, 2, :], ALU.subtract).then_inc(*link.next())
                dve.wait_ge(*link.done())
                nc.vector.scalar_tensor_tensor(cols[:, 3, 0, :], small[:, 3, :], -1.0, p3, ALU.mult, ALU.subtract).then_inc(*link.next())
                dve.wait_ge(*link.done())
                nc.vector.tensor_tensor(prods[:, 0:2], w, w, ALU.mult).then_inc(*link.next())
                nc.vector.tensor_tensor(prods[:, 2:4], w, v, ALU.mult).then_inc(*link.next())
                dve.wait_ge(*link.done())
                nc.vector.tensor_tensor(halves[:, :, :, :], prods[:, :, 0:2, :], prods[:, :, 2:4, :], ALU.add).then_inc(*link.next())
                dve.wait_ge(*link.done())
                nc.vector.tensor_tensor(norms[:, 0:4:3, :], halves[:, 0:2, 0, :], halves[:, 0:2, 1, :], ALU.add).then_inc(*link.next())
                nc.vector.tensor_tensor(dots[:, :, :], halves[:, 2:4, 0, :], halves[:, 2:4, 1, :], ALU.add).then_inc(*link.next())
                dve.wait_ge(*link.done())
                nc.vector.tensor_tensor(prods[:, 0:2], v, bc(norms[:, 0:4:3, :], 2, D), ALU.mult).then_inc(*link.next())
                nc.vector.tensor_tensor(prods[:, 2:4], w, bc(dots[:, :, :], 2, D), ALU.mult).then_inc(*link.next())
                dve.wait_ge(*link.done())
                nc.vector.tensor_tensor(u, prods[:, 0:2], prods[:, 2:4], ALU.subtract).then_inc(*link.next())
                dve.wait_ge(*link.done())
                nc.vector.tensor_tensor(prods[:, 0:2], u, u, ALU.mult).then_inc(*link.next())
                dve.wait_ge(*link.done())
                nc.vector.tensor_tensor(halves[:, 0:2, :, :], prods[:, 0:2, 0:2, :], prods[:, 0:2, 2:4, :], ALU.add).then_inc(*link.next())
                dve.wait_ge(*link.done())
                nc.vector.tensor_tensor(norms[:, 1:3, :], halves[:, 0:2, 0, :], halves[:, 0:2, 1, :], ALU.add).then_inc(normed.sem, 1)
                dve.wait_ge(rooted.sem, rooted.at(s + 1) + SB * i)
                nc.vector.reciprocal(roots[:, :, :], roots[:, :, :]).then_inc(*link.next())
                dve.wait_ge(*link.done())
                nc.vector.tensor_tensor(maps[:, :, :, :], cols[:, 0:4], bc(roots[:, :, :], 2, D), ALU.mult).then_inc(*link.next())
                dve.wait_ge(*link.done())
                for r in range(D):
                    ve = maps[:, :, r, 0:B]
                    ue = maps[:, :, r, B:F]
                    nc.vector.tensor_tensor(outer[:, r, :].rearrange("p (a b u) -> p a b u", a=D, b=D), bc(ve, 2, D), bc(ue, 1, D),
                                            ALU.mult).then_inc(*link.next())
                dve.wait_ge(*link.done())
                nc.vector.tensor_tensor(pair[:, :, :], outer[:, 0:2, :], outer[:, 2:4, :], ALU.add).then_inc(*link.next())
                dve.wait_ge(*link.done())
                nc.vector.tensor_tensor(both[:, :, :], pair[:, 0, :].rearrange("p (m u) -> p m u", u=B),
                                        pair[:, 1, :].rearrange("p (m u) -> p m u", u=B), ALU.add).then_inc(*link.next())
                dve.wait_ge(*link.done())

            def apply(s, g, i, link):
                x = rows[:, (s * B + GROUP * g) * TROW:(s * B + GROUP * (g + 1)) * TROW].rearrange("p (u w) -> p u w", u=GROUP)
                for b in range(D):
                    xb = bc(x[:, :, b * H:(b + 1) * H], 2, D)
                    m = both[:, b::D, GROUP * g:GROUP * (g + 1)].rearrange("p a u -> p u a")
                    nc.vector.tensor_tensor(parts[:, b, :].rearrange("p (u a h) -> p u a h", a=D, h=H), xb,
                                            bc(m, 3, H), ALU.mult).then_inc(*link.next())
                dve.wait_ge(*link.done())
                nc.vector.tensor_tensor(part2[:, :, :], parts[:, 0:2, :], parts[:, 2:4, :], ALU.add).then_inc(*link.next())
                dve.wait_ge(*link.done())
                nc.vector.tensor_tensor(messages[:, g, :], part2[:, 0, :], part2[:, 1, :], ALU.add).then_inc(message_ready.sem, 1)

            nc.vector.memset(hidden[2 * HID:2 * HID + 1, :, :], 1.0).then_inc(ones_set.sem, 1)
            nc.vector.memset(cols[:, :, :, :], 0.0).then_inc(chain.sem, 1)
            dve.wait_ge(chain.sem, chain.at(1))
            nc.vector.memset(cols[:, 0, 0, :], 1.0).then_inc(chain.sem, 1)
            nc.vector.memset(cols[:, 3, 3, :], 1.0).then_inc(chain.sem, 1)
            nc.vector.memset(cols[:, 4, 1, :], 1.0).then_inc(chain.sem, 1)
            nc.vector.memset(cols[:, 5, 2, :], 1.0).then_inc(chain.sem, 1)
            dve.wait_ge(chain.sem, chain.at(5))
            dve.sem_inc(copied.sem, 2)
            dve.sem_inc(rectified.sem, 2)
            dve.sem_inc(batch_read.sem, SB + 1)
            dve.sem_inc(taken.sem, 1)
            dve.sem_inc(added.sem, 1)
            for g in range(GB):
                build(0, g, mem.drel)
            with dve.Fori(0, SHEAF_BODIES) as i:
                link = Links(chain, 5, per_body, i)

                dve.wait_ge(built.sem, built.at(B) + SB * B * i)
                nc.vector.tensor_copy(drel_now[:, :], mem.drel[:, bass.ds(i * (SB * B) + B, SB * B)]).then_inc(*link.next())
                dve.wait_ge(*link.done())
                for s in range(SB):
                    for g in range(GB):
                        build(s + 1, g, drel_now[:, s * B:(s + 1) * B])
                    dve.wait_ge(taken.sem, taken.at(s + 2) + SB * i)
                    algebra(s, i, link)
                    for g in range(GB):
                        apply(s, g, i, link)
                    dve.wait_ge(message_ready.sem, message_ready.at(GB * (s + 1)) + SB * GB * i)
                    dve.sem_inc(batch_read.sem, 1)
                    for g in range(GB):
                        tiles = tiles_of_steps(nc, mem, DVE_ENGINE, i * (SB * B) + s * B + GROUP * g)
                        if g % 2 == 0:
                            dve.wait_ge(used.sem, used.at(GB * s + g + 2) + SB * GB * i)
                        for u in range(GROUP):
                            k = s * B + GROUP * g + u
                            dve.wait_ge(added.sem, added.at(1 + k) + SB * B * i)
                            at = (g % 2) * GROUP * C + u * C
                            columns = mem.acc[:, bass.ds(tiles[u] * C, C)]
                            nc.vector.tensor_tensor(columns, columns, sum_ps[g // 2][:, at:at + C], ALU.add).then_inc(added.sem, 1)
                assert link.n == 5 + per_body, link.n

    n = SHEAF_BODIES
    groups, batches = SB * GB * n, SB * n
    weights.passed(16), ones_set.passed(1), chain.passed(5 + per_body * n), built.passed(B * (batches + 1))
    turned.passed(groups + GB), copied.passed(groups + GB + 2), joined.passed(groups + GB + 2), rectified.passed(groups + GB + 2)
    widened.passed(groups + GB + 2), taken.passed(batches + 2), indices.passed(batches + SB), batch_read.passed(batches + SB + 1)
    normed.passed(batches), rooted.passed(batches), message_ready.passed(groups), used.passed(groups), added.passed(1 + B * batches)
    for g in gathers:
        g.passed(16 * B * n)
    gathers[0].passed(16 * B)


def sheaf_weights(nc, mem, dram, tag="sheafw"):
    ctx = ExitStack()
    with ctx:
        sb = lambda name, shape, dt=F32: ctx.enter_context(nc.sbuf_tensor(f"{tag}_{name}", shape, dt))
        w1t = sb("w1t", [C, C])
        w2 = sb("w2", [C, C])
        halves = sb("halves", [C, 2 * HID])
        kt = sb("kt", [C, C])
        all_sb = sb("all", [C, P])
        root = sb("root", [P, TILES_P])
        ps = [ctx.enter_context(nc.psum_tensor(f"{tag}_ps{j}", [C, 512], F32)) for j in range(3)]
        sem = mem.sems
        weights, products, taken, stored, chain, rooted = (sem["load"], sem["pe_done"], sem["dve_done"], sem["store"],
                                                           sem["dve_chain"], sem["act_done"])
        block = ctx.enter_context(nc.Block())

        @block.sync
        def _(sp):
            load_weights(sp, mem, [(w1t[:, :], dram["w1_mix"]), (w2[:, :], dram["w2_mix"]), (halves[:, :], dram["mlp1"])])
            sp.wait_ge(taken.sem, taken.at(2))
            sp.dma_start(dram["w_sheaf"][0:C, :], all_sb[:, :]).then_inc(stored.sem, 16)
            sp.dma_start(dram["w_sheaf"][C:C + 1, :], dram["sheaf_bias"]).then_inc(stored.sem, 16)
            sp.wait_ge(stored.sem, stored.at(32))

        @block.tensor
        def _(pe):
            pe.wait_ge(weights.sem, weights.at(48))
            nc.tensor.matmul(ps[0][:, 0:C], w1t[:, :], w2[:, :], start=True, stop=True)
            nc.tensor.matmul(ps[1][:, 0:C], w2[:, :], w1t[:, :], start=True, stop=True).then_inc(products.sem, 1)
            pe.wait_ge(taken.sem, taken.at(1))
            nc.tensor.matmul(ps[2][:, 0:2 * HID], kt[:, :], halves[:, :], start=True, stop=True).then_inc(products.sem, 1)

        @block.scalar
        def _(act):
            nc.scalar.activation(root[:, :], mem.src_scale[:, :], ACT.Sqrt).then_inc(rooted.sem, 1)

        @block.vector
        def _(dve):
            dve.wait_ge(products.sem, products.at(1))
            nc.vector.tensor_copy(kt[:, :], ps[1][:, 0:C]).then_inc(taken.sem, 1)
            nc.vector.tensor_copy(all_sb[:, 0:C], ps[0][:, 0:C])
            dve.wait_ge(products.sem, products.at(2))
            nc.vector.tensor_copy(all_sb[:, C:C + 2 * HID], ps[2][:, 0:2 * HID])
            nc.vector.tensor_copy(all_sb[:, C + 2 * HID:C + 3 * HID], ps[2][:, HID:2 * HID])
            nc.vector.tensor_copy(all_sb[:, C + 3 * HID:C + 4 * HID], ps[2][:, 0:HID]).then_inc(taken.sem, 1)
            dve.wait_ge(rooted.sem, rooted.at(1))
            nc.vector.reciprocal(mem.src_scale[:, :], root[:, :]).then_inc(chain.sem, 1)

    weights.passed(48), products.passed(2), taken.passed(2), stored.passed(32), chain.passed(1), rooted.passed(1)


def sheaf_finish(nc, mem, dram, tag="finish"):
    ctx = ExitStack()
    parts = 2
    T = TILES_P // parts
    H = C // 4
    with ctx:
        sb = lambda name, shape, dt=F32: ctx.enter_context(nc.sbuf_tensor(f"{tag}_{name}", shape, dt))
        eps = sb("eps", [P, 4])
        factor = sb("factor", [P, 4])
        below = sb("below", [P, T * C])
        sem = mem.sems
        weights, chain, ready, raised = sem["load"], sem["dve_chain"], sem["dve_done"], sem["act_done"]
        block = ctx.enter_context(nc.Block())
        view = lambda m, q: m[:, q * T * C:(q + 1) * T * C].rearrange("p (t c) -> p t c", c=C)

        @block.sync
        def _(sp):
            load_weights(sp, mem, [(eps[:, :], dram["epsilons"].rearrange("(o d) -> o d", o=1).to_broadcast([P, 4]))])

        @block.scalar
        def _(act):
            act.wait_ge(weights.sem, weights.at(16))
            nc.scalar.activation(factor[:, :], eps[:, :], ACT.Tanh).then_inc(raised.sem, 1)
            for q in range(parts):
                act.wait_ge(ready.sem, ready.at(q + 1))
                nc.scalar.activation(below[:, :], below[:, :], ACT.Exp).then_inc(raised.sem, 1)

        @block.vector
        def _(dve):
            link = Links(chain)
            dve.wait_ge(raised.sem, raised.at(1))
            nc.vector.tensor_scalar(factor[:, :], factor[:, :], 2.0, None, ALU.add).then_inc(*link.next())
            dve.wait_ge(*link.done())
            for q in range(parts):
                v, x = view(mem.acc, q), view(mem.xs, q)
                nc.vector.tensor_tensor(v, v, bc(mem.src_scale[:, q * T:(q + 1) * T], 2, C), ALU.mult).then_inc(*link.next())
                dve.wait_ge(*link.done())
                nc.vector.tensor_scalar(below[:, :], mem.acc[:, q * T * C:(q + 1) * T * C], 0.0, None, ALU.min).then_inc(ready.sem, 1)
                dve.wait_ge(raised.sem, raised.at(q + 2))
                nc.vector.scalar_tensor_tensor(v, v, 0.0, below[:, :].rearrange("p (t c) -> p t c", c=C), ALU.max, ALU.add).then_inc(*link.next())
                dve.wait_ge(*link.done())
                xd, bd = (m.rearrange("p t (d h) -> p t d h", h=H) for m in (x, below[:, :].rearrange("p (t c) -> p t c", c=C)))
                for d in range(4):
                    nc.vector.tensor_scalar(bd[:, :, d, :], xd[:, :, d, :], factor[:, d:d + 1], 1.0, ALU.mult, ALU.add).then_inc(*link.next())
                    dve.wait_ge(*link.done())
                nc.vector.tensor_tensor(v, below[:, :].rearrange("p (t c) -> p t c", c=C), v, ALU.subtract).then_inc(*link.next())
                dve.wait_ge(*link.done())
            link.close()

    weights.passed(16), ready.passed(parts), raised.passed(parts + 1)


def store_output(nc, mem, out):
    stored = mem.sems["store"]
    full = N // P
    with nc.Block() as block:
        @block.sync
        def _(sp):
            sp.dma_start(out[0:full * P, :].rearrange("(t p) c -> p t c", p=P),
                         mem.xs[:, 0:full * C].rearrange("p (t c) -> p t c", c=C)).then_inc(stored.sem, 16)
            sp.dma_start(out[full * P:N, :], mem.xs[0:N - full * P, full * C:(full + 1) * C]).then_inc(stored.sem, 16)
            sp.wait_ge(stored.sem, stored.at(32))
    stored.passed(32)


def allocate(nc, ctx):
    mem = Memory()
    sb = lambda name, shape, dt=F32: ctx.enter_context(nc.sbuf_tensor(name, shape, dt))
    mem.ident = sb("ident", [P, P])
    mem.iota = sb("iota", [P, P])
    mem.iota_h = sb("iota_h", [P, P], BF16)
    mem.acc = sb("acc", [P, TILES_P * C])
    mem.xs = sb("xs", [P, TILES_P * C])
    mem.dst_side = sb("dst_side", [P, TILES_P * C])
    mem.counts = sb("counts", [P, TILES_P * R])
    mem.degree = sb("degree", [P, TILES_P])
    mem.src_i = sb("src_i", [P, STEPS_P], I32)
    mem.row_i = sb("row_i", [P, STEPS_P], I32)
    mem.drel = sb("drel", [P, STEPS_P])
    mem.typ = sb("typ", [P, STEPS_P])
    mem.ew = sb("ew", [P, STEPS_P])
    mem.norm = sb("norm", [P, STEPS_P])
    mem.tile_row = sb("tile_row", [1, STEPS_P], I32)
    mem.start_row = sb("start_row", [1, STEPS_P], I32)
    mem.start_i = sb("start_i", [P, PLAN_GROUPS], I32)
    mem.node0 = sb("node0", [P, PLAN_GROUPS])
    mem.src_scale = sb("src_scale", [P, TILES_P])
    names = ["load", "load1", "load2", "load3", "load4", "made", "store", "store2", "dve_chain", "act_chain", "dve_done", "dve_done2", "pe_done",
             "pe_done2", "pe_done3", "pe_done4", "act_done", "act_done2", "act_done3", "act_done4", "act_done5", "dve_done3", "built", "used", "added",
             "index_ready", "waited", "gather0", "gather1", "gather2", "gather3"]
    mem.sems = {name: Signal(ctx, nc, name) for name in names}
    return mem


def program(nc, dram, out):
    ctx = ExitStack()
    scratch = lambda name, shape, dt=F32: nc.dram_tensor(name, shape, dt, kind="Internal").ap()
    dram["plan_rows"] = scratch("plan_rows", [2, STEPS_P], I32)
    dram["relation_table"] = scratch("relation_table", [NODES_P * R, C])
    dram["message_table"] = scratch("message_table", [NODES_P, C])
    dram["node_table"] = scratch("node_table", [NODES_P, C])
    dram["node_table2"] = scratch("node_table2", [NODES_P, C])
    dram["sheaf_table"] = scratch("sheaf_table", [NODES_P, TROW])
    dram["w_sheaf"] = scratch("w_sheaf", [C + 1, P])
    with ctx:
        mem = allocate(nc, ctx)
        constants_and_plan(nc, mem, dram)
        align_edges(nc, mem, dram)
        count_relations(nc, mem, dram)
        relation_nodes(nc, mem, dram, "rel1", dram["rel_w1"], dram["rel_root1"], False)
        relation_pass(nc, mem, dram)
        relation_nodes(nc, mem, dram, "rel2", dram["rel_w2"], dram["rel_root2"], True)
        gather_pass(nc, mem, "rel2", dram["relation_table"], mem.row_i, mem.norm)
        residual_sum(nc, mem, "rel_sum")
        layernorm(nc, mem, "ln0")
        project_nodes(nc, mem, dram, "msg", dram["message_table"], C, dram["msg_w"], False)
        message_pass(nc, mem, dram, "msgp")
        gru_nodes(nc, mem, dram)
        layernorm(nc, mem, "ln1", dram["node_table"])
        split_sources(nc, mem, dram)
        gather_pass(nc, mem, "gin1", dram["node_table"], mem.src_i, mem.ew, count_sources=True)
        mlp_nodes(nc, mem, dram, "mlp1", dram["node_table2"], C, dram["gin_w11"], dram["gin_w12"], dram["gin_b12"], False)
        gather_pass(nc, mem, "gin2", dram["node_table2"], mem.src_i, mem.ew)
        mlp_nodes(nc, mem, dram, "mlp2", dram["node_table"], 2 * C, dram["gin_w21"], dram["gin_w22"], dram["gin_b22"], False)
        gather_pass(nc, mem, "gin3", dram["node_table"], mem.src_i, mem.ew)
        mlp_nodes(nc, mem, dram, "mlp3", None, C, dram["gin_w31"], dram["gin_w32"], dram["gin_b32"], True)
        layernorm(nc, mem, "ln2")
        sheaf_weights(nc, mem, dram)
        project_nodes(nc, mem, dram, "shf", dram["sheaf_table"], TROW, dram["w_sheaf"], True)
        sheaf_pass(nc, mem, dram)
        sheaf_finish(nc, mem, dram)
        layernorm(nc, mem, "ln3")
        store_output(nc, mem, out)


def kernel(**inputs):
    import numpy as np
    import concourse.bacc as bacc
    from concourse.bass_utils import run_bass_kernel_spmd

    a = {k: np.asarray(v) for k, v in inputs.items()}

    def edges(x, fill, length=P * STEPS_P):
        padded = np.full(length, fill, x.dtype)
        padded[:E] = x
        return padded

    def rows(*parts):
        return np.concatenate([p[None] if p.ndim == 1 else p for p in parts], 0)

    x = np.zeros((NODES_P, C), np.float32)
    x[:N] = a["x"]
    features = np.zeros((FE, EDGES_P + P), np.float32)
    features[:, :E] = a["edge_attr_32"].T
    zeros = np.zeros(C, np.float32)
    w1 = a["L1_gnn_W1"]
    w1_mix, w2_mix = np.zeros((C, C), np.float32), np.zeros((C, C), np.float32)
    for k in range(4):
        for d in range(4):
            for f in range(HID):
                w1_mix[k * HID + f, d * HID + f] = a["L3_gnn_W1"][d, k]
        w2_mix[k * HID:(k + 1) * HID, k * HID:(k + 1) * HID] = a["L3_gnn_W2"]
    m1, m2, b2 = a["L3_gnn_mlp1_w"], a["L3_gnn_mlp2_w"], a["L3_gnn_mlp2_b"]
    w2_sheaf = np.zeros((2 * HID + 1, NPAR, 2), np.float32)
    for f, source in enumerate((0, 1, 3, 2, 4, 5)):
        for m in range(2):
            w2_sheaf[m * HID:(m + 1) * HID, f, m] = m2[source]
            w2_sheaf[2 * HID, f, m] = b2[source]
    bias = np.zeros((1, P), np.float32)
    bias[0, TROW:TROW + HID] = a["L3_gnn_mlp1_b"]
    bias[0, TROW + HID:] = a["L3_gnn_mlp1_b"]
    given = {
        "dst": edges(a["dst"], NO_NODE), "src": edges(a["src"], PAD_SRC), "typ": edges(a["edge_type_8"], 0),
        "ew": edges(a["edge_weight"], 0), "x": x, "features": features,
        "rel_w1": a["L0_gnn_W1"].transpose(1, 0, 2).reshape(C, R * C), "rel_root1": rows(a["L0_gnn_root1"], a["L0_gnn_b1"]),
        "rel_w2": a["L0_gnn_W2"].transpose(1, 0, 2).reshape(C, R * C), "rel_root2": rows(a["L0_gnn_root2"], a["L0_gnn_b2"]),
        "msg_w": np.concatenate([rows(w1[:, :C].T, zeros), rows(w1[:, C:2 * C].T, a["L1_gnn_b1"])], 1),
        "w_edge": w1[:, 2 * C:].T, "w2_msg": rows(a["L1_gnn_W2"].T, a["L1_gnn_b2"]),
        "w_ih": rows(a["L1_gnn_w_ih"].T, a["L1_gnn_b_ih"]), "w_hh": rows(a["L1_gnn_w_hh"].T, a["L1_gnn_b_hh"]),
        "w1_mix": w1_mix, "w2_mix": w2_mix, "mlp1": np.concatenate([m1[:, C:].T, m1[:, :C].T], 1), "sheaf_bias": bias,
        "w2_sheaf": w2_sheaf.reshape(2 * HID + 1, 2 * NPAR), "epsilons": a["L3_gnn_epsilons"],
    }
    for n in "123":
        given[f"gin_w{n}1"] = rows(a[f"L2_gnn_w{n}1"], a[f"L2_gnn_b{n}1"])
        given[f"gin_w{n}2"] = a[f"L2_gnn_w{n}2"]
        given[f"gin_b{n}2"] = a[f"L2_gnn_b{n}2"][None]
    given = {k: np.ascontiguousarray(v) for k, v in given.items()}

    nc = bacc.Bacc("TRN2", target_bir_lowering=False, num_devices=1)
    dram = {k: nc.dram_tensor(f"in_{k}", v.shape, mybir.dt.from_np(v.dtype), kind="ExternalInput").ap() for k, v in given.items()}
    out = nc.dram_tensor("out", (N, C), F32, kind="ExternalOutput").ap()
    program(nc, dram, out)
    r = run_bass_kernel_spmd(nc, [{f"in_{k}": v for k, v in given.items()}], core_ids=[0])
    return r.results[0]["out"]
```

```python
import concourse.bass as bass
from concourse import mybir
from contextlib import ExitStack

F32 = mybir.dt.float32
BF16 = mybir.dt.bfloat16
I32 = mybir.dt.int32
ALU = mybir.AluOpType
ACT = mybir.ActivationFunctionType
AX = mybir.AxisListType
DVE_ENGINE = mybir.EngineType.DVE
PE_ENGINE = mybir.EngineType.PE
ACT_ENGINE = mybir.EngineType.Activation
SP_ENGINE = mybir.EngineType.SP

P = 128
N = 12500
E = 212500
C = 64
R = 8
FE = 32
TILES = -(-N // P)
UNIT = 4
TILES_P = -(-TILES // (2 * UNIT)) * 2 * UNIT
UNITS = TILES_P // UNIT
NODES_P = TILES_P * P
EDGE_COLS = -(-E // P) + 1
EDGES_P = EDGE_COLS * P
NO_NODE = 1 << 20
PAD_SRC = NODES_P - 1
GROUP = 4
RING = 4
BODY = 8
STEPS_MIN = E // P + TILES
BODIES = -(-STEPS_MIN // (GROUP * BODY))
STEPS = BODIES * GROUP * BODY
BSTEPS = GROUP * BODY
BATCH = 16
SHEAF_BODY = 4
SHEAF_BODIES = -(-STEPS_MIN // (BATCH * SHEAF_BODY))
PLAN_GROUPS = -(-(max(STEPS, SHEAF_BODIES * BATCH * SHEAF_BODY) + BATCH) // P)
PLAN_GROUPS += PLAN_GROUPS % 2
STEPS_P = PLAN_GROUPS * P
EPS = 1e-5
HID = 16
NPAR = 6
SHEAF_USED0 = 3 * BATCH // GROUP
SHEAF_LINKS = 31 + 2 * 5
TROW = C + 2 * HID


class Signal:

    def __init__(self, ctx, nc, name):
        self.sem = ctx.enter_context(nc.semaphore(name))
        self.base = 0

    def at(self, k):
        return self.base + k

    def passed(self, total):
        self.base += total


class Links:

    def __init__(self, links, before=0, per_body=0, i=0):
        self.links, self.n, self.later = links, before, per_body * i if per_body else 0

    def next(self):
        self.n += 1
        return self.links.sem, 1

    def done(self):
        return self.links.sem, self.links.at(self.n) + self.later

    def close(self):
        self.links.passed(self.n)


class Memory:
    pass


def tiles_of_steps(nc, mem, engine, first, count=GROUP):
    _, values = nc.values_load_multi_w_load_instructions(
        mem.tile_row[0:1, bass.ds(first, count)], engines=[engine], min_val=0, max_val=TILES - 1,
        skip_runtime_bounds_check_because="the plan counts at most TILES - 1 tiles passed")
    return values


def wait_apart(eng, mem, sem, value):
    eng.wait_ge(sem, value)
    eng.sem_inc(mem.sems["waited"].sem, 1)


def bc(ap, axis, n):
    return ap.unsqueeze(axis).to_broadcast(list(ap.shape[:axis]) + [n] + list(ap.shape[axis:]))


def constants_and_plan(nc, mem, dram):
    ctx = ExitStack()
    with ctx:
        sb = lambda name, shape, dt=F32: ctx.enter_context(nc.sbuf_tensor(name, shape, dt))
        head_i = sb("plan_head_i", [P, 16], I32)
        head = sb("plan_head", [P, 1])
        headed = sb("plan_headed", [P, P])
        run_f = sb("plan_run_f", [P, 1])
        run_i = sb("plan_run_i", [P, 1], I32)
        dst_i = sb("plan_dst_i", [P, EDGE_COLS], I32)
        dst_f = sb("plan_dst_f", [P, EDGE_COLS])
        below_junk = sb("plan_below_junk", [P, EDGE_COLS])
        part_f = sb("plan_part_f", [P, 1])
        first_f = sb("plan_first_f", [P, 1])
        iota_i = sb("plan_iota_i", [P, P], I32)
        part_i = sb("plan_part_i", [P, 1], I32)
        bound_i = sb("plan_bound_i", [P, P], I32)
        bound = sb("plan_bound", [P, P])
        step_i = sb("plan_step_i", [P, PLAN_GROUPS], I32)
        step_f = sb("plan_step_f", [P, PLAN_GROUPS])
        ones = sb("plan_ones", [P, P])
        spread = sb("plan_spread", [P, TILES + 1])
        first = sb("plan_first", [P, TILES + 1])
        steps_f = sb("plan_steps_f", [P, TILES])
        steps_i = sb("plan_steps_i", [P, TILES], I32)
        zeros = sb("plan_zeros", [P, TILES])
        step0 = sb("plan_step0", [P, TILES])
        delta = sb("plan_delta", [P, TILES - 1])
        offset = sb("plan_offset", [P, TILES - 1])
        reached = sb("plan_reached", [P, TILES - 1])
        junk = sb("plan_junk", [P, TILES - 1])
        tile_f = sb("plan_tile_f", [P, PLAN_GROUPS])
        start_f = sb("plan_start_f", [P, PLAN_GROUPS])
        rows_i = sb("plan_rows_i", [PLAN_GROUPS, 2, P], I32)
        count_ps = ctx.enter_context(nc.psum_tensor("plan_count_ps", [P, 512], F32))
        rows_ps = ctx.enter_context(nc.psum_tensor("plan_rows_ps", [P, 512], F32))
        sem = mem.sems
        loaded, iotas, chain = sem["load"], sem["made"], sem["dve_chain"]
        counted, counts_ready, stored = sem["pe_done"], sem["dve_done"], sem["store"]

        fetched = sem["gather2"]
        runs = dram["dst"][0:EDGES_P].rearrange("(p c) -> p c", p=P)

        block = ctx.enter_context(nc.Block())

        @block.sync
        def _(sp):
            sp.dma_start(head_i[:, :], runs[:, 0:16]).then_inc(loaded.sem, 16)
            sp.dma_start(mem.xs[:, :].rearrange("p (t c) -> p t c", c=C),
                         dram["x"].rearrange("(t p) c -> p t c", p=P)).then_inc(loaded.sem, 16)
            sp.wait_ge(counts_ready.sem, counts_ready.at(5))
            for a in range(2):
                sp.dma_start(dram["plan_rows"][a].rearrange("(g s) -> g s", s=P), rows_i[:, a, :]).then_inc(stored.sem, 16)
            sp.wait_ge(stored.sem, stored.at(32))
            sp.dma_start(mem.tile_row[0:1, :], dram["plan_rows"][0:1, :]).then_inc(stored.sem, 16)
            sp.dma_start(mem.start_row[0:1, :], dram["plan_rows"][1:2, :]).then_inc(stored.sem, 16)
            sp.wait_ge(stored.sem, stored.at(64))
            sp.wait_ge(loaded.sem, loaded.at(32))

        @block.gpsimd
        def _(pool):
            nc.gpsimd.memset(mem.ident[:, :], 0.0).then_inc(iotas.sem, 1)
            nc.gpsimd.iota(iota_i[:, :], [[1, P]], base=0, channel_multiplier=0).then_inc(iotas.sem, 1)
            nc.gpsimd.iota(part_i[:, :], [[0, 1]], base=0, channel_multiplier=1).then_inc(iotas.sem, 1)
            nc.gpsimd.iota(bound_i[:, :], [[P, P]], base=0, channel_multiplier=0).then_inc(iotas.sem, 1)
            nc.gpsimd.iota(step_i[:, :], [[P, PLAN_GROUPS]], base=0, channel_multiplier=1).then_inc(iotas.sem, 1)
            nc.gpsimd.memset(ones[:, :], 1.0).then_inc(iotas.sem, 1)
            pool.wait_ge(iotas.sem, iotas.at(6))
            nc.gpsimd.affine_select(out=mem.ident[:, :], in_=mem.ident[:, :], compare_op=ALU.not_equal, fill=1.0,
                                    base=0, pattern=[[-1, P]], channel_multiplier=1).then_inc(iotas.sem, 1)
            pool.wait_ge(counts_ready.sem, counts_ready.at(2))
            nc.gpsimd.indirect_dma_start(out=dst_i[:, :], out_offset=None, in_=runs,
                                         in_offset=bass.IndirectOffsetOnAxis(ap=run_i[:, 0:1], axis=0)).then_inc(fetched.sem, 16)

        @block.tensor
        def _(pe):
            pe.wait_ge(counts_ready.sem, counts_ready.at(1))
            nc.tensor.matmul(rows_ps[:, 0:1], headed[:, :], ones[:, 0:1], start=True, stop=True).then_inc(counted.sem, 1)
            pe.wait_ge(counts_ready.sem, counts_ready.at(3))
            nc.tensor.matmul(count_ps[:, 0:TILES + 1], ones[:, :], spread[:, :], start=True, stop=True).then_inc(counted.sem, 1)
            pe.wait_ge(counts_ready.sem, counts_ready.at(4))
            pe.wait_ge(iotas.sem, iotas.at(7))
            nc.tensor.transpose(rows_ps[0:PLAN_GROUPS, 0:P], tile_f[:, :], mem.ident[:, :])
            nc.tensor.transpose(rows_ps[0:PLAN_GROUPS, P:2 * P], start_f[:, :], mem.ident[:, :]).then_inc(counted.sem, 1)

        @block.vector
        def _(dve):
            link = Links(chain)
            dve.wait_ge(iotas.sem, iotas.at(6))
            nc.vector.tensor_copy(mem.iota[:, :], iota_i[:, :]).then_inc(*link.next())
            dve.wait_ge(*link.done())
            nc.vector.tensor_copy(mem.iota_h[:, :], mem.iota[:, :]).then_inc(*link.next())
            dve.wait_ge(*link.done())
            nc.vector.tensor_copy(bound[:, :], bound_i[:, :]).then_inc(*link.next())
            dve.wait_ge(*link.done())
            nc.vector.tensor_copy(step_f[:, :], step_i[:, :]).then_inc(*link.next())
            dve.wait_ge(*link.done())
            nc.vector.memset(zeros[:, :], 0.0).then_inc(*link.next())
            dve.wait_ge(*link.done())
            dve.wait_ge(loaded.sem, loaded.at(32))
            nc.vector.tensor_copy(head[:, :], head_i[:, 0:1]).then_inc(*link.next())
            dve.wait_ge(*link.done())
            nc.vector.tensor_scalar(headed[:, :], bound[:, :], head[:, 0:1], None, ALU.is_gt).then_inc(*link.next())
            nc.vector.tensor_scalar(part_f[:, :], part_i[:, :], float(P), None, ALU.mult).then_inc(*link.next())
            dve.wait_ge(*link.done())
            dve.sem_inc(counts_ready.sem, 1)
            dve.wait_ge(counted.sem, counted.at(1))
            nc.vector.tensor_scalar(run_f[:, :], rows_ps[:, 0:1], -1.0, 0.0, ALU.add, ALU.max).then_inc(*link.next())
            dve.wait_ge(*link.done())
            nc.vector.tensor_copy(run_i[:, :], run_f[:, :]).then_inc(*link.next())
            dve.wait_ge(*link.done())
            dve.sem_inc(counts_ready.sem, 1)
            dve.wait_ge(fetched.sem, fetched.at(16))
            nc.vector.tensor_copy(dst_f[:, :], dst_i[:, :]).then_inc(*link.next())
            dve.wait_ge(*link.done())
            nc.vector.tensor_scalar(below_junk[:, :], dst_f[:, :], part_f[:, 0:1], None, ALU.is_lt, ALU.add,
                                    accum_out=first_f[:, 0:1]).then_inc(*link.next())
            dve.wait_ge(*link.done())
            nc.vector.scalar_tensor_tensor(first_f[:, :], run_f[:, :], float(EDGE_COLS), first_f[:, :],
                                           ALU.mult, ALU.add).then_inc(*link.next())
            dve.wait_ge(*link.done())
            dve.wait_ge(iotas.sem, iotas.at(7))
            nc.vector.tensor_scalar(spread[:, :], mem.ident[:, 0:TILES + 1], first_f[:, 0:1], None, ALU.mult).then_inc(*link.next())
            dve.wait_ge(*link.done())
            dve.sem_inc(counts_ready.sem, 1)
            dve.wait_ge(counted.sem, counted.at(2))
            nc.vector.tensor_copy(first[:, :], count_ps[:, 0:TILES + 1]).then_inc(*link.next())
            dve.wait_ge(*link.done())
            nc.vector.tensor_tensor(steps_f[:, :], first[:, 1:TILES + 1], first[:, 0:TILES], ALU.subtract).then_inc(*link.next())
            dve.wait_ge(*link.done())
            nc.vector.tensor_scalar(steps_f[:, :], steps_f[:, :], float(P - 1), None, ALU.add).then_inc(*link.next())
            dve.wait_ge(*link.done())
            nc.vector.tensor_copy(steps_i[:, :], steps_f[:, :]).then_inc(*link.next())
            dve.wait_ge(*link.done())
            nc.vector.tensor_scalar(steps_i[:, :], steps_i[:, :], 7, None, ALU.arith_shift_right).then_inc(*link.next())
            dve.wait_ge(*link.done())
            nc.vector.tensor_copy(steps_f[:, :], steps_i[:, :]).then_inc(*link.next())
            dve.wait_ge(*link.done())
            nc.vector.tensor_tensor_scan(step0[:, :], steps_f[:, :], zeros[:, :], 0.0, ALU.add, ALU.add).then_inc(*link.next())
            dve.wait_ge(*link.done())
            nc.vector.scalar_tensor_tensor(offset[:, :], step0[:, 0:TILES - 1], -float(P), first[:, 1:TILES],
                                           ALU.mult, ALU.add).then_inc(*link.next())
            dve.wait_ge(*link.done())
            nc.vector.tensor_copy(delta[:, 0:1], offset[:, 0:1]).then_inc(*link.next())
            dve.wait_ge(*link.done())
            nc.vector.tensor_tensor(delta[:, 1:], offset[:, 1:], offset[:, :TILES - 2], ALU.subtract).then_inc(*link.next())
            dve.wait_ge(*link.done())
            for g in range(PLAN_GROUPS):
                nc.vector.tensor_scalar(reached[:, :], step0[:, 0:TILES - 1], step_f[:, g:g + 1], None,
                                        ALU.is_le, ALU.add, accum_out=tile_f[:, g:g + 1]).then_inc(*link.next())
                dve.wait_ge(*link.done())
                nc.vector.tensor_tensor_reduce(out=junk[:, :], in0=reached[:, :], in1=delta[:, :], scale=1.0,
                                               scalar=0.0, op0=ALU.mult, op1=ALU.add,
                                               accum_out=start_f[:, g:g + 1]).then_inc(*link.next())
                dve.wait_ge(*link.done())
            nc.vector.scalar_tensor_tensor(start_f[:, :], step_f[:, :], float(P), start_f[:, :], ALU.mult, ALU.add).then_inc(*link.next())
            dve.wait_ge(*link.done())
            nc.vector.tensor_scalar(start_f[:, :], start_f[:, :], float(E), None, ALU.min).then_inc(*link.next())
            dve.wait_ge(*link.done())
            nc.vector.tensor_copy(mem.start_i[:, :], start_f[:, :]).then_inc(*link.next())
            dve.wait_ge(*link.done())
            nc.vector.tensor_scalar(mem.node0[:, :], tile_f[:, :], float(P), None, ALU.mult).then_inc(*link.next())
            dve.wait_ge(*link.done())
            dve.sem_inc(counts_ready.sem, 1)
            dve.wait_ge(counted.sem, counted.at(3))
            nc.vector.tensor_copy(rows_i[:, :, :], rows_ps[0:PLAN_GROUPS, 0:2 * P].rearrange("g (a s) -> g a s", a=2)).then_inc(*link.next())
            dve.wait_ge(*link.done())
            dve.sem_inc(counts_ready.sem, 1)
            link.close()

    loaded.passed(32), iotas.passed(7), counted.passed(3), counts_ready.passed(5), stored.passed(64)
    fetched.passed(16)


def align_edges(nc, mem, dram):
    ctx = ExitStack()
    with ctx:
        sb = lambda name, shape, dt=F32: ctx.enter_context(nc.sbuf_tensor(name, shape, dt))
        raw_i = sb("align_raw_i", [P, 2, 3, P], I32)
        raw_w = sb("align_raw_w", [P, 2, P])
        raw_f = sb("align_raw_f", [P, 2, 3, P])
        start_now = sb("align_start", [P, 2], I32)
        ps = [ctx.enter_context(nc.psum_tensor(f"align_ps{j}", [P, 512], F32)) for j in range(2)]
        sem = mem.sems
        gathered = [sem["gather0"], sem["gather1"]]
        chain, starts, raw_ready, turned, evacuated = (sem["dve_chain"], sem["made"], sem["dve_done"],
                                                       sem["pe_done"], sem["act_done"])
        arrays = [dram["dst"], dram["src"], dram["typ"]]
        block = ctx.enter_context(nc.Block())

        @block.gpsimd
        def _(pool):
            with pool.Fori(0, PLAN_GROUPS // 2) as i:
                for j in range(2):
                    wait_apart(pool, mem, starts.sem, starts.at(1 + j) + 2 * i)
                    for a, array in enumerate(arrays + [dram["ew"]]):
                        out = raw_i[:, j, a, :] if a < 3 else raw_w[:, j, :]
                        nc.gpsimd.indirect_dma_start(
                            out=out, out_offset=None, in_=array.rearrange("(e o) -> e o", o=1),
                            in_offset=bass.IndirectOffsetOnAxis(ap=start_now[:, j:j + 1], axis=0)).then_inc(gathered[j].sem, 16)

        @block.vector
        def _(dve):
            link = Links(chain)
            with dve.Fori(0, PLAN_GROUPS // 2) as i:
                k = 0
                for j in range(2):
                    nc.vector.tensor_copy(start_now[:, j:j + 1], mem.start_i[:, bass.ds(2 * i + j, 1)]).then_inc(starts.sem, 1)
                for j in range(2):
                    dve.wait_ge(gathered[j].sem, gathered[j].at(64) + 64 * i)
                    nc.vector.tensor_copy(raw_f[:, j, :, :], raw_i[:, j, :, :]).then_inc(chain.sem, 1)
                    k += 1
                    dve.wait_ge(chain.sem, chain.at(k) + 4 * i)
                    nc.vector.tensor_scalar(raw_f[:, j, 0, :], raw_f[:, j, 0, :], mem.node0[:, bass.ds(2 * i + j, 1)], None,
                                            ALU.subtract).then_inc(raw_ready.sem, 1)
                for j in range(2):
                    dve.wait_ge(turned.sem, turned.at(j + 1) + 2 * i)
                    cols = bass.ds((2 * i + j) * P, P)
                    nc.vector.tensor_copy(mem.drel[:, cols], ps[j][:, 0:P])
                    nc.vector.tensor_copy(mem.typ[:, cols], ps[j][:, 2 * P:3 * P]).then_inc(chain.sem, 1)
                    nc.vector.tensor_copy(mem.ew[:, cols], ps[j][:, 3 * P:4 * P])
                    nc.vector.tensor_copy(mem.src_i[:, cols], ps[j][:, P:2 * P])
                    k += 1
                    dve.wait_ge(chain.sem, chain.at(k) + 4 * i)
                    nc.vector.scalar_tensor_tensor(mem.row_i[:, cols], ps[j][:, P:2 * P], float(R), mem.typ[:, cols],
                                                   ALU.mult, ALU.add).then_inc(evacuated.sem, 1)

        @block.tensor
        def _(pe):
            with pe.Fori(0, PLAN_GROUPS // 2) as i:
                for j in range(2):
                    pe.wait_ge(raw_ready.sem, raw_ready.at(j + 1) + 2 * i)
                    for a in range(3):
                        nc.tensor.transpose(ps[j][:, a * P:(a + 1) * P], raw_f[:, j, a, :], mem.ident[:, :])
                    nc.tensor.transpose(ps[j][:, 3 * P:4 * P], raw_w[:, j, :], mem.ident[:, :]).then_inc(turned.sem, 1)

    n = PLAN_GROUPS // 2
    for g in gathered:
        g.passed(64 * n)
    chain.passed(4 * n), starts.passed(2 * n), raw_ready.passed(2 * n), turned.passed(2 * n), evacuated.passed(2 * n)


def count_relations(nc, mem, dram):
    ctx = ExitStack()
    with ctx:
        sb = lambda name, shape, dt=F32: ctx.enter_context(nc.sbuf_tensor(name, shape, dt))
        onehot = sb("count_onehot", [P, RING * GROUP, P], BF16)
        typ_hot = sb("count_typ_hot", [P, BSTEPS, R], BF16)
        zero_h = sb("count_zero", [1, 512], BF16)
        drel_now = sb("count_drel", [P, BSTEPS])
        table = ctx.enter_context(nc.psum_tensor("count_table", [P, 1024], F32))
        sem = mem.sems
        chain, built, summed, zeroed = sem["dve_chain"], sem["built"], sem["used"], sem["made"]
        block = ctx.enter_context(nc.Block())
        ring = RING * GROUP

        @block.tensor
        def _(pe):
            pe.wait_ge(zeroed.sem, zeroed.at(1))
            for b in range(2):
                nc.tensor.matmul(table[:, 512 * b:512 * (b + 1)], zero_h[0:1, 0:P], zero_h[0:1, :], start=True, stop=True,
                                 skip_group_check=True)
            pe.sem_inc(summed.sem, RING)
            with pe.Fori(0, BODIES) as i:
                for j in range(BODY):
                    tiles = tiles_of_steps(nc, mem, PE_ENGINE, i * BSTEPS + GROUP * j)
                    pe.wait_ge(built.sem, built.at(j + 1) + BODY * i)
                    for u in range(GROUP):
                        k = GROUP * j + u
                        ins = nc.tensor.matmul(table[:, bass.ds(tiles[u] * R, R)], onehot[:, k % ring, :], typ_hot[:, k, :],
                                               start=False, stop=True, skip_group_check=True)
                    ins.then_inc(summed.sem, 1)

        @block.vector
        def _(dve):
            link = Links(chain)
            nc.vector.memset(zero_h[:, :], 0.0).then_inc(zeroed.sem, 1)
            with dve.Fori(0, BODIES) as i:
                for half in range(2):
                    dve.wait_ge(summed.sem, summed.at(max(1, RING - BODY + (half + 1) * BODY // 2)) + BODY * i)
                    n = BSTEPS // 2
                    steps, now = bass.ds(i * BSTEPS + half * n, n), slice(half * n, (half + 1) * n)
                    nc.vector.tensor_copy(drel_now[:, now], mem.drel[:, steps]).then_inc(chain.sem, 1)
                    nc.vector.tensor_tensor(typ_hot[:, now, :], bc(mem.typ[:, steps], 2, R), bc(mem.iota[:, 0:R], 1, n),
                                            ALU.is_equal).then_inc(chain.sem, 1)
                    dve.wait_ge(chain.sem, chain.at(2 * half + 2) + 4 * i)
                    for j in range(half * BODY // 2, (half + 1) * BODY // 2):
                        dve.wait_ge(summed.sem, summed.at(j + 1) + BODY * i)
                        for u in range(GROUP):
                            k = GROUP * j + u
                            ins = nc.vector.tensor_scalar(onehot[:, k % ring, :], mem.iota_h[:, :], drel_now[:, k:k + 1], None,
                                                          ALU.is_equal)
                        ins.then_inc(built.sem, 1)
            dve.wait_ge(summed.sem, summed.at(RING + BODY * BODIES))
            link.n += 4 * BODIES
            nc.vector.tensor_copy(mem.counts[:, 0:512], table[:, 0:512]).then_inc(*link.next())
            dve.wait_ge(*link.done())
            nc.vector.tensor_copy(mem.counts[:, 512:], table[:, 512:TILES_P * R]).then_inc(*link.next())
            dve.wait_ge(*link.done())
            nc.vector.tensor_reduce(mem.degree[:, :], mem.counts[:, :].rearrange("p (t r) -> p t r", r=R), AX.X, ALU.add).then_inc(*link.next())
            dve.wait_ge(*link.done())
            nc.vector.tensor_scalar(mem.counts[:, :], mem.counts[:, :], 1.0, None, ALU.max).then_inc(*link.next())
            dve.wait_ge(*link.done())
            nc.vector.reciprocal(mem.counts[:, :], mem.counts[:, :]).then_inc(*link.next())
            dve.wait_ge(*link.done())
            nc.vector.memset(mem.norm[:, :], 0.0).then_inc(*link.next())
            dve.wait_ge(*link.done())
            link.close()

    zeroed.passed(1), built.passed(BODY * BODIES), summed.passed(RING + BODY * BODIES)


USED0 = RING + 1
ADDED0 = GROUP * RING


def gather_program(nc, mem, table, index_now, rows, width, ahead=0):
    sem = mem.sems
    used, index_ready = sem["used"], sem["index_ready"]

    def gather_group(pool, j, i):
        half = j // (BODY // 2)
        if j % (BODY // 2) == 0:
            wait_apart(pool, mem, index_ready.sem, index_ready.at(half + 1) + 2 * i)
        wait_apart(pool, mem, used.sem, used.at(j - RING + USED0 + 1) + BODY * i)
        for u in range(GROUP):
            k = GROUP * j + u
            slot = k % (RING * GROUP)
            nc.gpsimd.indirect_dma_start(
                out=rows[:, slot * width:(slot + 1) * width], out_offset=None, in_=table,
                in_offset=bass.IndirectOffsetOnAxis(ap=index_now[:, k:k + 1], axis=0),
            ).then_inc(sem[f"gather{j % RING}"].sem, 16)

    def program(pool):
        with pool.Fori(0, BODIES) as i:
            for j in range(BODY):
                gather_group(pool, j, i)
        for j in range(ahead):
            gather_group(pool, j, BODIES)
    return program


def copy_indices(nc, mem, act, i, half, index_now, index):
    used, index_ready = mem.sems["used"], mem.sems["index_ready"]
    n = BSTEPS // 2
    act.wait_ge(used.sem, used.at(half * (BODY // 2) - BODY // 2 + USED0) + BODY * i)
    nc.scalar.activation(index_now[:, half * n:(half + 1) * n], index[:, bass.ds(i * BSTEPS + half * n, n)],
                         ACT.Copy).then_inc(index_ready.sem, 1)


def gathered(mem, j, i):
    s = mem.sems[f"gather{j % RING}"]
    return s.sem, s.at(16 * GROUP * (j // RING + 1)) + 16 * GROUP * (BODY // RING) * i


def pass_ends(mem, ahead=0, groups=BODY * BODIES):
    s = mem.sems
    for q in range(RING):
        s[f"gather{q}"].passed(16 * GROUP * groups // RING)
    s["used"].passed(USED0 + groups)
    s["added"].passed(ADDED0 + GROUP * groups)
    for q in range(ahead):
        s[f"gather{q}"].passed(16 * GROUP)


def add_and_build(nc, mem, dve, i, j, ps, onehot, drel_now, weight_now, lag):
    used, added, built = mem.sems["used"], mem.sems["added"], mem.sems["built"]
    tiles = tiles_of_steps(nc, mem, DVE_ENGINE, i * BSTEPS + GROUP * j)
    dve.wait_ge(used.sem, used.at(USED0 + j + 1) + BODY * i)
    for u in range(GROUP):
        k = GROUP * j + u
        dve.wait_ge(added.sem, added.at(ADDED0 + k) + BSTEPS * i)
        columns = mem.acc[:, bass.ds(tiles[u] * C, C)]
        nc.vector.tensor_tensor(columns, columns, ps[j % RING][:, u * C:(u + 1) * C], ALU.add).then_inc(added.sem, 1)
        build_onehot(nc, mem, onehot, k + GROUP * lag, drel_now[:, k:k + 1],
                     None if weight_now is None else weight_now[:, k:k + 1])


def build_onehot(nc, mem, onehot, k, place, weight):
    out = onehot[:, k % (RING * GROUP), :]
    if weight is None:
        ins = nc.vector.tensor_scalar(out, mem.iota[:, :], place, None, ALU.is_equal)
    else:
        ins = nc.vector.tensor_scalar(out, mem.iota[:, :], place, weight, ALU.is_equal, ALU.mult)
    ins.then_inc(mem.sems["built"].sem, 1)


def stage_columns(nc, mem, dve, i, lag, pairs):
    chain, built = mem.sems["dve_chain"], mem.sems["built"]
    dve.wait_ge(built.sem, built.at(GROUP * lag) + BSTEPS * i)
    for now, table in pairs:
        nc.vector.tensor_copy(now[:, :], table[:, bass.ds(i * BSTEPS + GROUP * lag, BSTEPS)]).then_inc(chain.sem, 1)
    dve.wait_ge(chain.sem, chain.at(len(pairs)) + len(pairs) * i)


def gather_pass(nc, mem, tag, table, index, weight, lag=4, count_sources=False):
    ctx = ExitStack()
    with ctx:
        sb = lambda name, shape, dt=F32: ctx.enter_context(nc.sbuf_tensor(f"{tag}_{name}", shape, dt))
        rows = sb("rows", [P, RING * GROUP * C])
        onehot = sb("onehot", [P, RING * GROUP, P])
        drel_now = sb("drel_now", [P, BSTEPS])
        weight_now = sb("weight_now", [P, BSTEPS])
        index_now = sb("index_now", [P, BSTEPS], I32)
        ps = [ctx.enter_context(nc.psum_tensor(f"{tag}_ps{j}", [P, 512], F32)) for j in range(RING)]
        sem = mem.sems
        used, added, built = sem["used"], sem["added"], sem["built"]
        if count_sources:
            low_now = sb("low_now", [P, BSTEPS])
            high_now = sb("high_now", [P, BSTEPS])
            low_hot = sb("low_hot", [P, 2 * GROUP, P], BF16)
            high_hot = sb("high_hot", [P, 2 * GROUP, TILES_P], BF16)
            zero_h = sb("zero_h", [1, P], BF16)
            source_ps = ctx.enter_context(nc.psum_tensor(f"{tag}_source_ps", [P, 512], F32))
            hots, tallied, zeroed = sem["dve_done"], sem["pe_done"], sem["made"]
        block = ctx.enter_context(nc.Block())
        block.gpsimd(gather_program(nc, mem, table, index_now, rows, C))

        @block.scalar
        def _(act):
            with act.Fori(0, BODIES) as i:
                for half in range(2):
                    copy_indices(nc, mem, act, i, half, index_now, index)

        @block.tensor
        def _(pe):
            pe.sem_inc(used.sem, USED0)
            if count_sources:
                pe.wait_ge(zeroed.sem, zeroed.at(1))
                nc.tensor.matmul(source_ps[:, 0:TILES_P], zero_h[:, :], zero_h[:, 0:TILES_P], start=True, stop=True,
                                 skip_group_check=True)
                pe.sem_inc(tallied.sem, 2)
            with pe.Fori(0, BODIES) as i:
                for j in range(BODY):
                    pe.wait_ge(built.sem, built.at(GROUP * (j + 1)) + BSTEPS * i)
                    pe.wait_ge(added.sem, added.at(GROUP * (j + 1)) + BSTEPS * i)
                    pe.wait_ge(*gathered(mem, j, i))
                    for u in range(GROUP):
                        slot = (GROUP * j + u) % (RING * GROUP)
                        ins = nc.tensor.matmul(ps[j % RING][:, u * C:(u + 1) * C], onehot[:, slot, :],
                                               rows[:, slot * C:(slot + 1) * C], start=True, stop=True)
                    ins.then_inc(used.sem, 1)
                    if count_sources:
                        pe.wait_ge(hots.sem, hots.at(j + 1) + BODY * i)
                        for u in range(GROUP):
                            k = GROUP * (j % 2) + u
                            ins = nc.tensor.matmul(source_ps[:, 0:TILES_P], low_hot[:, k, :], high_hot[:, k, :],
                                                   start=False, stop=True, skip_group_check=True)
                        ins.then_inc(tallied.sem, 1)

        @block.vector
        def _(dve):
            dve.sem_inc(added.sem, ADDED0)
            if count_sources:
                nc.vector.memset(zero_h[:, :], 0.0).then_inc(zeroed.sem, 1)
            for k in range(GROUP * lag):
                build_onehot(nc, mem, onehot, k, mem.drel[:, k:k + 1], weight[:, k:k + 1])
            with dve.Fori(0, BODIES) as i:
                if count_sources:
                    dve.wait_ge(hots.sem, hots.at(0) + BODY * i)
                    chain = sem["dve_chain"]
                    nc.vector.tensor_copy(low_now[:, :], mem.typ[:, bass.ds(i * BSTEPS, BSTEPS)])
                    nc.vector.tensor_copy(high_now[:, :], mem.norm[:, bass.ds(i * BSTEPS, BSTEPS)])
                stage_columns(nc, mem, dve, i, lag, [(drel_now, mem.drel), (weight_now, weight)])
                for j in range(BODY):
                    if count_sources:
                        dve.wait_ge(tallied.sem, tallied.at(j + 1) + BODY * i)
                        for u in range(GROUP):
                            k, slot = GROUP * j + u, GROUP * (j % 2) + u
                            nc.vector.tensor_scalar(low_hot[:, slot, :], mem.iota_h[:, :], low_now[:, k:k + 1], None, ALU.is_equal)
                            ins = nc.vector.tensor_scalar(high_hot[:, slot, :], mem.iota_h[:, 0:TILES_P], high_now[:, k:k + 1],
                                                          None, ALU.is_equal)
                        ins.then_inc(hots.sem, 1)
                    add_and_build(nc, mem, dve, i, j, ps, onehot, drel_now, weight_now, lag)
            if count_sources:
                dve.wait_ge(tallied.sem, tallied.at(2 + BODY * BODIES))
                nc.vector.tensor_scalar(mem.src_scale[:, :], source_ps[:, 0:TILES_P], 1.0, None, ALU.add).then_inc(hots.sem, 1)

    pass_ends(mem)
    sem["index_ready"].passed(2 * BODIES), sem["dve_chain"].passed(2 * BODIES), built.passed(STEPS + GROUP * lag)
    if count_sources:
        hots.passed(BODY * BODIES + 1), tallied.passed(2 + BODY * BODIES), zeroed.passed(1)


def split_sources(nc, mem, dram):
    sem = mem.sems
    loaded, chain = sem["load"], sem["dve_chain"]
    with nc.sbuf_tensor("split_src", [P, STEPS], I32) as src, nc.sbuf_tensor("split_part", [P, STEPS], I32) as part, \
            nc.Block() as block:
        @block.sync
        def _(sp):
            sp.dma_start(src[:, :], dram["src"][0:P * STEPS].rearrange("(p c) -> p c", p=P)).then_inc(loaded.sem, 16)

        @block.vector
        def _(dve):
            link = Links(chain)
            dve.wait_ge(loaded.sem, loaded.at(16))
            nc.vector.tensor_scalar(part[:, :], src[:, :], 7, None, ALU.arith_shift_right).then_inc(*link.next())
            dve.wait_ge(*link.done())
            nc.vector.tensor_copy(mem.norm[:, 0:STEPS], part[:, :]).then_inc(*link.next())
            dve.wait_ge(*link.done())
            nc.vector.tensor_scalar(part[:, :], src[:, :], P - 1, None, ALU.bitwise_and).then_inc(*link.next())
            dve.wait_ge(*link.done())
            nc.vector.tensor_copy(mem.typ[:, 0:STEPS], part[:, :]).then_inc(*link.next())
            dve.wait_ge(*link.done())
            link.close()
    loaded.passed(16)


def relation_pass(nc, mem, dram, tag="rel", lag=4):
    ctx = ExitStack()
    per_body = 2 + 3 * BODY
    with ctx:
        sb = lambda name, shape, dt=F32: ctx.enter_context(nc.sbuf_tensor(f"{tag}_{name}", shape, dt))
        rows = sb("rows", [P, RING * GROUP * C])
        onehot = sb("onehot", [P, RING * GROUP, P])
        turned_hot = sb("turned_hot", [P, 2, GROUP, P])
        typ_now = sb("typ_now", [P, BSTEPS])
        typ_hot = sb("typ_hot", [P, 2, GROUP, R])
        picked = sb("picked", [P, 2, GROUP, R])
        norm_now = sb("norm_now", [P, 2, GROUP])
        drel_now = sb("drel_now", [P, BSTEPS])
        index_now = sb("index_now", [P, BSTEPS], I32)
        ps = [ctx.enter_context(nc.psum_tensor(f"{tag}_ps{j}", [P, 512], F32)) for j in range(RING)]
        turn_ps = [ctx.enter_context(nc.psum_tensor(f"{tag}_turn_ps{j}", [P, GROUP, P], F32)) for j in range(2)]
        pick_ps = [ctx.enter_context(nc.psum_tensor(f"{tag}_pick_ps{j}", [P, 512], F32)) for j in range(2)]
        sem = mem.sems
        used, added, built, chain = sem["used"], sem["added"], sem["built"], sem["dve_chain"]
        turned, copied, expanded, weighed, scaled = (sem["pe_done"], sem["act_done"], sem["pe_done2"], sem["dve_done"],
                                                     sem["act_done2"])
        block = ctx.enter_context(nc.Block())
        block.gpsimd(gather_program(nc, mem, dram["relation_table"], index_now, rows, C, ahead=1))


        @block.tensor
        def _(pe):
            def turn(g, i):
                pe.wait_ge(built.sem, built.at(GROUP * (g + 1)) + BSTEPS * i)
                if g >= 2:
                    pe.wait_ge(copied.sem, copied.at(g - 1) + BODY * i)
                for u in range(GROUP):
                    slot = (GROUP * g + u) % (RING * GROUP)
                    ins = nc.tensor.transpose(turn_ps[g % 2][:, u, :], onehot[:, slot, :], mem.ident[:, :])
                ins.then_inc(turned.sem, 1)

            def expand(g, i):
                tiles = tiles_of_steps(nc, mem, PE_ENGINE, i * BSTEPS + GROUP * g)
                pe.wait_ge(copied.sem, copied.at(g + 1) + BODY * i)
                if g >= 1:
                    pe.wait_ge(weighed.sem, weighed.at(g) + BODY * i)
                for u in range(GROUP):
                    ins = nc.tensor.matmul(pick_ps[g % 2][:, u * R:(u + 1) * R], turned_hot[:, g % 2, u, :],
                                           mem.counts[:, bass.ds(tiles[u] * R, R)], start=True, stop=True)
                ins.then_inc(expanded.sem, 1)

            pe.sem_inc(used.sem, USED0)
            turn(0, 0)
            turn(1, 0)
            expand(0, 0)
            with pe.Fori(0, BODIES) as i:
                for j in range(BODY):
                    turn(j + 2, i)
                    expand(j + 1, i)
                    pe.wait_ge(scaled.sem, scaled.at(j + 1) + BODY * i)
                    pe.wait_ge(added.sem, added.at(GROUP * (j + 1)) + BSTEPS * i)
                    for u in range(GROUP):
                        slot = (GROUP * j + u) % (RING * GROUP)
                        ins = nc.tensor.matmul(ps[j % RING][:, u * C:(u + 1) * C], onehot[:, slot, :],
                                               rows[:, slot * C:(slot + 1) * C], start=True, stop=True)
                    ins.then_inc(used.sem, 1)

        @block.scalar
        def _(act):
            def copy(g, i):
                act.wait_ge(turned.sem, turned.at(g + 1) + BODY * i)
                if g >= 2:
                    act.wait_ge(expanded.sem, expanded.at(g - 1) + BODY * i)
                nc.scalar.activation(turned_hot[:, g % 2, :, :], turn_ps[g % 2][:, :, :], ACT.Copy).then_inc(copied.sem, 1)

            def scale(g, i):
                act.wait_ge(weighed.sem, weighed.at(g + 1) + BODY * i)
                act.wait_ge(*gathered(mem, g, i))
                for u in range(GROUP):
                    slot = (GROUP * g + u) % (RING * GROUP)
                    row = rows[:, slot * C:(slot + 1) * C]
                    ins = nc.scalar.activation(row, row, ACT.Copy, scale=norm_now[:, g % 2, u:u + 1])
                ins.then_inc(scaled.sem, 1)

            copy(0, 0)
            copy(1, 0)
            for half in range(2):
                copy_indices(nc, mem, act, 0, half, index_now, mem.row_i)
            scale(0, 0)
            with act.Fori(0, BODIES) as i:
                for j in range(BODY):
                    copy(j + 2, i)
                    scale(j + 1, i)
                    if j in (BODY // 2 - 1, BODY - 1):
                        copy_indices(nc, mem, act, i + 1, j // (BODY // 2), index_now, mem.row_i)

        @block.vector
        def _(dve):
            def relation(g, typ_columns):
                return nc.vector.tensor_tensor(typ_hot[:, g % 2, :, :], bc(typ_columns, 2, R), bc(mem.iota[:, 0:R], 1, GROUP),
                                               ALU.is_equal).then_inc(chain.sem, 1)

            def weigh(g, i, c):
                dve.wait_ge(chain.sem, c)
                dve.wait_ge(expanded.sem, expanded.at(g + 1) + BODY * i)
                nc.vector.tensor_tensor(picked[:, g % 2, :, :],
                                        pick_ps[g % 2][:, 0:GROUP * R].rearrange("p (u r) -> p u r", r=R),
                                        typ_hot[:, g % 2, :, :], ALU.mult).then_inc(chain.sem, 1)
                dve.wait_ge(chain.sem, c + 1)
                nc.vector.tensor_reduce(norm_now[:, g % 2, :], picked[:, g % 2, :, :], AX.X, ALU.add).then_inc(weighed.sem, 1)

            dve.sem_inc(added.sem, ADDED0)
            for k in range(GROUP * lag):
                build_onehot(nc, mem, onehot, k, mem.drel[:, k:k + 1], None)
            relation(0, mem.typ[:, 0:GROUP])
            weigh(0, 0, chain.at(1))
            with dve.Fori(0, BODIES) as i:
                dve.wait_ge(built.sem, built.at(GROUP * lag) + BSTEPS * i)
                nc.vector.tensor_copy(drel_now[:, :], mem.drel[:, bass.ds(i * BSTEPS + GROUP * lag, BSTEPS)]).then_inc(chain.sem, 1)
                nc.vector.tensor_copy(typ_now[:, :], mem.typ[:, bass.ds(i * BSTEPS + GROUP, BSTEPS)]).then_inc(chain.sem, 1)
                dve.wait_ge(chain.sem, chain.at(4) + per_body * i)
                for j in range(BODY):
                    relation(j + 1, typ_now[:, GROUP * j:GROUP * (j + 1)])
                    weigh(j + 1, i, chain.at(5 + 3 * j) + per_body * i)
                    add_and_build(nc, mem, dve, i, j, ps, onehot, drel_now, None, lag)
                    nc.vector.tensor_copy(mem.norm[:, bass.ds(i * BSTEPS + GROUP * j, GROUP)],
                                          norm_now[:, j % 2, :]).then_inc(chain.sem, 1)

    pass_ends(mem, ahead=1)
    groups = BODY * BODIES
    built.passed(STEPS + GROUP * lag), chain.passed(2 + per_body * BODIES)
    turned.passed(groups + 2), copied.passed(groups + 2), expanded.passed(groups + 1)
    weighed.passed(groups + 1), scaled.passed(groups + 1), sem["index_ready"].passed(2 * BODIES + 2)


def message_pass(nc, mem, dram, tag="msg", lag=4):
    ctx = ExitStack()
    with ctx:
        sb = lambda name, shape, dt=F32: ctx.enter_context(nc.sbuf_tensor(f"{tag}_{name}", shape, dt))
        rows = sb("rows", [P, RING * GROUP * C])
        onehot = sb("onehot", [P, RING * GROUP, P])
        turned_hot = sb("turned_hot", [P, 2, GROUP, P])
        features = sb("features", [GROUP * FE, RING, P])
        feature_w = sb("feature_w", [GROUP * FE, GROUP * C])
        messages = sb("messages", [P, 2, GROUP * C])
        drel_now = sb("drel_now", [P, BSTEPS])
        index_now = sb("index_now", [P, BSTEPS], I32)
        ps = [ctx.enter_context(nc.psum_tensor(f"{tag}_ps{j}", [P, 512], F32)) for j in range(RING)]
        turn_ps = [ctx.enter_context(nc.psum_tensor(f"{tag}_turn_ps{j}", [P, GROUP, P], F32)) for j in range(2)]
        pre_ps = [ctx.enter_context(nc.psum_tensor(f"{tag}_pre_ps{j}", [P, 512], F32)) for j in range(2)]
        sem = mem.sems
        used, added, built, chain = sem["used"], sem["added"], sem["built"], sem["dve_chain"]
        turned, copied, joined, rectified, weights = sem["pe_done"], sem["act_done"], sem["pe_done2"], sem["act_done2"], sem["load"]
        loads = [sem["load1"], sem["load2"], sem["load3"], sem["load4"]]
        block = ctx.enter_context(nc.Block())
        block.gpsimd(gather_program(nc, mem, dram["message_table"], index_now, rows, C, ahead=1))

        @block.sync
        def _(sp):
            sp.dma_start(feature_w[:, :], dram["w_edge"]).then_inc(weights.sem, 16)

            def load_group(j, i):
                _, starts = nc.values_load_multi_w_load_instructions(
                    mem.start_row[0:1, bass.ds(i * BSTEPS + GROUP * j, GROUP)], engines=[SP_ENGINE], min_val=0, max_val=E,
                    skip_runtime_bounds_check_because="the plan caps the first edge at E")
                wait_apart(sp, mem, used.sem, used.at(j - RING + USED0 + 1) + BODY * i)
                for u in range(GROUP):
                    sp.dma_start(features[u * FE:(u + 1) * FE, j % RING, :],
                                 dram["features"][:, bass.ds(starts[u], P)]).then_inc(loads[j % RING].sem, 16)

            with sp.Fori(0, BODIES) as i:
                for j in range(BODY):
                    load_group(j, i)
            load_group(0, BODIES)

        @block.tensor
        def _(pe):
            def turn(g, i):
                pe.wait_ge(built.sem, built.at(GROUP * (g + 1)) + BSTEPS * i)
                if g >= 2:
                    pe.wait_ge(copied.sem, copied.at(g - 1) + BODY * i)
                for u in range(GROUP):
                    slot = (GROUP * g + u) % (RING * GROUP)
                    ins = nc.tensor.transpose(turn_ps[g % 2][:, u, :], onehot[:, slot, :], mem.ident[:, :])
                ins.then_inc(turned.sem, 1)

            def join(g, i):
                tiles = tiles_of_steps(nc, mem, PE_ENGINE, i * BSTEPS + GROUP * g)
                pe.wait_ge(copied.sem, copied.at(g + 1) + BODY * i)
                pe.wait_ge(*gathered(mem, g, i))
                landed = loads[g % RING]
                pe.wait_ge(landed.sem, landed.at(16 * GROUP * (g // RING + 1)) + 16 * GROUP * (BODY // RING) * i)
                if g >= 1:
                    pe.wait_ge(rectified.sem, rectified.at(g) + BODY * i)
                out = pre_ps[g % 2]
                first = g % RING * GROUP * C
                nc.tensor.matmul(out[:, 0:GROUP * C], features[:, g % RING, :], feature_w[:, :], start=True, stop=False,
                                 skip_group_check=True)
                nc.tensor.matmul(out[:, 0:GROUP * C], mem.ident[:, :], rows[:, first:first + GROUP * C], start=False, stop=False,
                                 skip_group_check=True)
                for u in range(GROUP):
                    ins = nc.tensor.matmul(out[:, u * C:(u + 1) * C], turned_hot[:, g % 2, u, :],
                                           mem.dst_side[:, bass.ds(tiles[u] * C, C)], start=False, stop=True, skip_group_check=True)
                ins.then_inc(joined.sem, 1)

            pe.wait_ge(weights.sem, weights.at(16))
            pe.sem_inc(used.sem, USED0)
            turn(0, 0)
            turn(1, 0)
            join(0, 0)
            with pe.Fori(0, BODIES) as i:
                for j in range(BODY):
                    turn(j + 2, i)
                    join(j + 1, i)
                    pe.wait_ge(rectified.sem, rectified.at(j + 1) + BODY * i)
                    pe.wait_ge(added.sem, added.at(GROUP * (j + 1)) + BSTEPS * i)
                    for u in range(GROUP):
                        slot = (GROUP * j + u) % (RING * GROUP)
                        ins = nc.tensor.matmul(ps[j % RING][:, u * C:(u + 1) * C], onehot[:, slot, :],
                                               messages[:, j % 2, u * C:(u + 1) * C], start=True, stop=True)
                    ins.then_inc(used.sem, 1)

        @block.scalar
        def _(act):
            def copy(g, i):
                act.wait_ge(turned.sem, turned.at(g + 1) + BODY * i)
                if g >= 2:
                    act.wait_ge(joined.sem, joined.at(g - 1) + BODY * i)
                nc.scalar.activation(turned_hot[:, g % 2, :, :], turn_ps[g % 2][:, :, :], ACT.Copy).then_inc(copied.sem, 1)

            def rectify(g, i):
                act.wait_ge(joined.sem, joined.at(g + 1) + BODY * i)
                act.wait_ge(used.sem, used.at(USED0 + g - 1) + BODY * i)
                nc.scalar.activation(messages[:, g % 2, :], pre_ps[g % 2][:, 0:GROUP * C], ACT.Relu).then_inc(rectified.sem, 1)

            for half in range(2):
                copy_indices(nc, mem, act, 0, half, index_now, mem.src_i)
            copy(0, 0)
            copy(1, 0)
            rectify(0, 0)
            with act.Fori(0, BODIES) as i:
                for j in range(BODY):
                    copy(j + 2, i)
                    if j in (BODY // 2, BODY - 1):
                        copy_indices(nc, mem, act, i + 1, 0 if j == BODY // 2 else 1, index_now, mem.src_i)
                    rectify(j + 1, i)

        @block.vector
        def _(dve):
            dve.sem_inc(added.sem, ADDED0)
            for k in range(GROUP * lag):
                build_onehot(nc, mem, onehot, k, mem.drel[:, k:k + 1], None)
            with dve.Fori(0, BODIES) as i:
                stage_columns(nc, mem, dve, i, lag, [(drel_now, mem.drel)])
                for j in range(BODY):
                    add_and_build(nc, mem, dve, i, j, ps, onehot, drel_now, None, lag)

    pass_ends(mem, ahead=1)
    groups = BODY * BODIES
    weights.passed(16), built.passed(STEPS + GROUP * lag), chain.passed(BODIES)
    turned.passed(groups + 2), copied.passed(groups + 2), joined.passed(groups + 1), rectified.passed(groups + 1)
    sem["index_ready"].passed(2 * BODIES + 2)
    for q in loads:
        q.passed(16 * GROUP * groups // RING)
    loads[0].passed(16 * GROUP)


def load_weights(sp, mem, pairs):
    for tile, source in pairs:
        sp.dma_start(tile, source).then_inc(mem.sems["load"].sem, 16)


def unit_columns(i, width=C):
    return bass.ds(i * (UNIT * width), UNIT * width)


def unit_done(signal, s, i, per=1):
    return signal.sem, signal.at(per * (s + 3)) + 2 * per * i


def credit_units(eng, signals, per=1):
    for signal in signals:
        eng.sem_inc(signal.sem, 2 * per)


def units_passed(signals, per=1):
    for signal in signals:
        signal.passed(per * (2 + UNITS))


def unit_rows(table, u):
    return table[bass.ds(u * (UNIT * P), UNIT * P), :].rearrange("(t p) c -> p t c", p=P)


def store_units(sp, mem, ready, released, table, staged, per=1):
    stored = mem.sems["store"]
    credit_units(sp, [released])
    with sp.Fori(0, UNITS // 2) as i:
        for s in range(2):
            sp.wait_ge(*unit_done(ready, s, i, per))
            sp.dma_start(unit_rows(table, 2 * i + s), staged(s)).then_inc(stored.sem, 16)
            sp.wait_ge(stored.sem, stored.at(16 * (s + 1)) + 32 * i)
            sp.sem_inc(released.sem, 1)
    stored.passed(16 * UNITS)


def turn_unit(nc, mem, pe, s, i, started, copied, turned, h, turn_ps, width=C):
    pe.wait_ge(*unit_done(started, s, i))
    wait_apart(pe, mem, *unit_done(copied, s - 2, i))
    for t in range(UNIT):
        ins = nc.tensor.transpose(turn_ps[:, t * P:(t + 1) * P], h[:, t * width:(t + 1) * width], mem.ident[:, :])
    ins.then_inc(turned.sem, 1)


def relation_nodes(nc, mem, dram, tag, w_all, root_b, rectify):
    ctx = ExitStack()
    with ctx:
        sb = lambda name, shape, dt=F32: ctx.enter_context(nc.sbuf_tensor(f"{tag}_{name}", shape, dt))
        w_sb = sb("w", [C, R * C])
        root_sb = sb("root", [C + 1, C])
        h = sb("h", [P, 2, UNIT * C])
        h_turned = sb("h_turned", [C + 1, 2, UNIT * P])
        table = sb("table", [P, 2, UNIT, R * C])
        turn_ps = [ctx.enter_context(nc.psum_tensor(f"{tag}_turn_ps{j}", [C, UNIT * P], F32)) for j in range(2)]
        root_ps = [ctx.enter_context(nc.psum_tensor(f"{tag}_root_ps{j}", [P, 512], F32)) for j in range(2)]
        table_ps = [ctx.enter_context(nc.psum_tensor(f"{tag}_table_ps{j}", [P, R * C], F32)) for j in range(UNIT)]
        sem = mem.sems
        weights, started, turned, copied = sem["load"], sem["act_done"], sem["pe_done"], sem["act_done2"]
        made, rooted, table_copied, released = sem["pe_done2"], sem["pe_done3"], sem["dve_done3"], sem["act_done4"]
        ones_set, acc_set = sem["made"], sem["dve_done2"]
        source = mem.acc if rectify else mem.xs
        block = ctx.enter_context(nc.Block())
        rows = dram["relation_table"].rearrange("(n r) c -> n (r c)", r=R)

        @block.sync
        def _(sp):
            load_weights(sp, mem, [(w_sb[:, :], w_all), (root_sb[:, :], root_b)])
            store_units(sp, mem, table_copied, released, rows, lambda s: table[:, s, :, :], per=UNIT)

        @block.scalar
        def _(act):
            credit_units(act, [started, copied])
            with act.Fori(0, UNITS // 2) as i:
                for s in range(2):
                    act.wait_ge(*unit_done(turned, s - 2, i))
                    nc.scalar.activation(h[:, s, :], source[:, unit_columns(2 * i + s)],
                                         ACT.Relu if rectify else ACT.Copy).then_inc(started.sem, 1)
                for s in range(2):
                    act.wait_ge(*unit_done(turned, s, i))
                    act.wait_ge(*unit_done(rooted, s - 2, i))
                    nc.scalar.activation(h_turned[0:C, s, :], turn_ps[s][:, :], ACT.Copy).then_inc(copied.sem, 1)

        @block.vector
        def _(dve):
            nc.vector.memset(h_turned[C:C + 1, :, :], 1.0).then_inc(ones_set.sem, 1)
            credit_units(dve, [acc_set])
            credit_units(dve, [table_copied], UNIT)
            with dve.Fori(0, UNITS // 2) as i:
                for s in range(2):
                    dve.wait_ge(*unit_done(released, s - 2, i))
                    for t in range(UNIT):
                        dve.wait_ge(made.sem, made.at(2 * UNIT + UNIT * s + t + 1) + 2 * UNIT * i)
                        nc.vector.tensor_copy(table[:, s, t, :], table_ps[t][:, :]).then_inc(table_copied.sem, 1)
                    dve.wait_ge(*unit_done(rooted, s, i))
                    nc.vector.tensor_copy(mem.acc[:, unit_columns(2 * i + s)], root_ps[s][:, 0:UNIT * C]).then_inc(acc_set.sem, 1)

        @block.tensor
        def _(pe):
            pe.wait_ge(weights.sem, weights.at(32))
            pe.wait_ge(ones_set.sem, ones_set.at(1))
            credit_units(pe, [turned, rooted])
            credit_units(pe, [made], UNIT)
            with pe.Fori(0, UNITS // 2) as i:
                for s in range(2):
                    turn_unit(nc, mem, pe, s, i, started, copied, turned, h[:, s, :], turn_ps[s])
                for s in range(2):
                    pe.wait_ge(*unit_done(copied, s, i))
                    pe.wait_ge(*unit_done(acc_set, s - 2, i))
                    for t in range(UNIT):
                        turned_t = h_turned[:, s, t * P:(t + 1) * P]
                        pe.wait_ge(table_copied.sem, table_copied.at(2 * UNIT + UNIT * (s - 1) + t + 1) + 2 * UNIT * i)
                        nc.tensor.matmul(table_ps[t][:, :], turned_t[0:C, :], w_sb[:, :], start=True, stop=True).then_inc(made.sem, 1)
                        ins = nc.tensor.matmul(root_ps[s][:, t * C:(t + 1) * C], turned_t, root_sb[:, :], start=True, stop=True)
                    ins.then_inc(rooted.sem, 1)

    weights.passed(32), ones_set.passed(1)
    units_passed([started, turned, copied, rooted, released, acc_set])
    units_passed([made, table_copied], UNIT)


def project_nodes(nc, mem, dram, tag, table, width, w_all, by_source_degree):
    ctx = ExitStack()
    with ctx:
        sb = lambda name, shape, dt=F32: ctx.enter_context(nc.sbuf_tensor(f"{tag}_{name}", shape, dt))
        w_sb = sb("w", [C + 1, P])
        h = sb("h", [P, 2, UNIT * C])
        h_turned = sb("h_turned", [C + 1, 2, UNIT * P])
        staged = sb("staged", [P, 2, UNIT, width])
        turn_ps = [ctx.enter_context(nc.psum_tensor(f"{tag}_turn_ps{j}", [C, UNIT * P], F32)) for j in range(2)]
        out_ps = [ctx.enter_context(nc.psum_tensor(f"{tag}_out_ps{j}", [P, UNIT, P], F32)) for j in range(2)]
        sem = mem.sems
        weights, started, turned, copied = sem["load"], sem["act_done"], sem["pe_done"], sem["act_done2"]
        projected, taken, released, ones_set, chain = (sem["pe_done2"], sem["dve_done"], sem["dve_done2"], sem["made"],
                                                       sem["dve_chain"])
        block = ctx.enter_context(nc.Block())

        @block.sync
        def _(sp):
            load_weights(sp, mem, [(w_sb[:, :], w_all)])
            store_units(sp, mem, taken, released, table, lambda s: staged[:, s, :, :])

        @block.scalar
        def _(act):
            credit_units(act, [started, copied])
            with act.Fori(0, UNITS // 2) as i:
                for s in range(2):
                    act.wait_ge(*unit_done(turned, s - 2, i))
                    nc.scalar.activation(h[:, s, :], mem.xs[:, unit_columns(2 * i + s)], ACT.Copy).then_inc(started.sem, 1)
                for s in range(2):
                    act.wait_ge(*unit_done(turned, s, i))
                    act.wait_ge(*unit_done(projected, s - 2, i))
                    nc.scalar.activation(h_turned[0:C, s, :], turn_ps[s][:, :], ACT.Copy).then_inc(copied.sem, 1)

        @block.vector
        def _(dve):
            nc.vector.memset(h_turned[C:C + 1, :, :], 1.0).then_inc(ones_set.sem, 1)
            if not by_source_degree:
                nc.vector.memset(mem.acc[:, :], 0.0).then_inc(chain.sem, 1)
            credit_units(dve, [taken])
            side = P - width
            with dve.Fori(0, UNITS // 2) as i:
                for s in range(2):
                    dve.wait_ge(*unit_done(projected, s, i))
                    dve.wait_ge(*unit_done(released, s - 2, i))
                    nc.vector.tensor_copy(mem.dst_side[:, unit_columns(2 * i + s, side)],
                                          out_ps[s][:, :, width:P])
                    if by_source_degree:
                        nc.vector.tensor_copy(staged[:, s, :, C:width], out_ps[s][:, :, C:width])
                        scale = mem.src_scale[:, bass.ds((2 * i + s) * UNIT, UNIT)]
                        nc.vector.tensor_tensor(mem.acc[:, unit_columns(2 * i + s)], out_ps[s][:, :, 0:C], bc(scale, 2, C),
                                                ALU.mult)
                        nc.vector.tensor_tensor(staged[:, s, :, 0:C], out_ps[s][:, :, 0:C], bc(scale, 2, C),
                                                ALU.mult).then_inc(taken.sem, 1)
                    else:
                        nc.vector.tensor_copy(staged[:, s, :, :], out_ps[s][:, :, 0:width]).then_inc(taken.sem, 1)

        @block.tensor
        def _(pe):
            pe.wait_ge(weights.sem, weights.at(16))
            pe.wait_ge(ones_set.sem, ones_set.at(1))
            credit_units(pe, [turned, projected])
            with pe.Fori(0, UNITS // 2) as i:
                for s in range(2):
                    turn_unit(nc, mem, pe, s, i, started, copied, turned, h[:, s, :], turn_ps[s])
                for s in range(2):
                    pe.wait_ge(*unit_done(copied, s, i))
                    pe.wait_ge(*unit_done(taken, s - 2, i))
                    for t in range(UNIT):
                        ins = nc.tensor.matmul(out_ps[s][:, t, :], h_turned[:, s, t * P:(t + 1) * P], w_sb[:, :],
                                               start=True, stop=True)
                    ins.then_inc(projected.sem, 1)

    weights.passed(16), ones_set.passed(1)
    units_passed([started, turned, copied, projected, taken, released])
    if not by_source_degree:
        chain.passed(1)


def mlp_nodes(nc, mem, dram, tag, table, hidden, w1, w2, b2, last):
    ctx = ExitStack()
    with ctx:
        sb = lambda name, shape, dt=F32: ctx.enter_context(nc.sbuf_tensor(f"{tag}_{name}", shape, dt))
        w1_sb = sb("w1", [C + 1, hidden])
        w2_sb = sb("w2", [hidden, C])
        b2_sb = sb("b2", [1, UNIT * C])
        ones = sb("ones", [1, P])
        h = sb("h", [P, 2, UNIT * C])
        h_turned = sb("h_turned", [C + 1, 2, UNIT * P])
        inner = sb("inner", [hidden, 2, UNIT * P])
        staged = sb("staged", [P, 2, UNIT * C])
        turn_ps = [ctx.enter_context(nc.psum_tensor(f"{tag}_turn_ps{j}", [C, UNIT * P], F32)) for j in range(2)]
        inner_ps = [ctx.enter_context(nc.psum_tensor(f"{tag}_inner_ps{j}", [hidden, UNIT * P], F32)) for j in range(2)]
        out_ps = [ctx.enter_context(nc.psum_tensor(f"{tag}_out_ps{j}", [P, UNIT * C], F32)) for j in range(2)]
        sem = mem.sems
        weights, started, turned, copied = sem["load"], sem["act_done"], sem["pe_done"], sem["act_done2"]
        widened, rectified, narrowed = sem["pe_done2"], sem["act_done3"], sem["pe_done3"]
        staged_set, acc_set, released, ones_set = sem["act_done4"], sem["dve_done"], sem["dve_done2"], sem["made"]
        block = ctx.enter_context(nc.Block())

        @block.sync
        def _(sp):
            load_weights(sp, mem, [(w1_sb[:, :], w1), (w2_sb[:, :], w2), (b2_sb[:, :], b2)])
            if not last:
                store_units(sp, mem, staged_set, released, table,
                            lambda s: staged[:, s, :].rearrange("p (t c) -> p t c", c=C))

        @block.scalar
        def _(act):
            credit_units(act, [started, copied, rectified] + [staged_set] * (not last))
            with act.Fori(0, UNITS // 2) as i:
                for s in range(2):
                    act.wait_ge(*unit_done(turned, s - 2, i))
                    nc.scalar.activation(h[:, s, :], mem.acc[:, unit_columns(2 * i + s)], ACT.Copy).then_inc(started.sem, 1)
                for s in range(2):
                    act.wait_ge(*unit_done(turned, s, i))
                    act.wait_ge(*unit_done(widened, s - 2, i))
                    nc.scalar.activation(h_turned[0:C, s, :], turn_ps[s][:, :], ACT.Copy).then_inc(copied.sem, 1)
                for s in range(2):
                    act.wait_ge(*unit_done(widened, s, i))
                    act.wait_ge(*unit_done(narrowed, s - 2, i))
                    nc.scalar.activation(inner[:, s, :], inner_ps[s][:, :], ACT.Relu).then_inc(rectified.sem, 1)
                if not last:
                    for s in range(2):
                        act.wait_ge(*unit_done(narrowed, s, i))
                        act.wait_ge(*unit_done(released, s - 2, i))
                        act.wait_ge(*unit_done(acc_set, s - 2, i))
                        nc.scalar.activation(staged[:, s, :], out_ps[s][:, :], ACT.Relu).then_inc(staged_set.sem, 1)

        @block.vector
        def _(dve):
            nc.vector.memset(h_turned[C:C + 1, :, :], 1.0).then_inc(ones_set.sem, 1)
            nc.vector.memset(ones[:, :], 1.0).then_inc(ones_set.sem, 1)
            credit_units(dve, [acc_set])
            with dve.Fori(0, UNITS // 2) as i:
                for s in range(2):
                    if last:
                        dve.wait_ge(*unit_done(narrowed, s, i))
                        nc.vector.tensor_tensor(mem.acc[:, unit_columns(2 * i + s)], out_ps[s][:, :],
                                                mem.xs[:, unit_columns(2 * i + s)], ALU.add).then_inc(acc_set.sem, 1)
                    else:
                        dve.wait_ge(*unit_done(staged_set, s, i))
                        nc.vector.tensor_copy(mem.acc[:, unit_columns(2 * i + s)], staged[:, s, :]).then_inc(acc_set.sem, 1)

        @block.tensor
        def _(pe):
            pe.wait_ge(weights.sem, weights.at(48))
            pe.wait_ge(ones_set.sem, ones_set.at(2))
            credit_units(pe, [turned, widened, narrowed])
            with pe.Fori(0, UNITS // 2) as i:
                for s in range(2):
                    turn_unit(nc, mem, pe, s, i, started, copied, turned, h[:, s, :], turn_ps[s])
                for s in range(2):
                    pe.wait_ge(*unit_done(copied, s, i))
                    pe.wait_ge(*unit_done(rectified, s - 2, i))
                    nc.tensor.matmul(inner_ps[s][:, :], w1_sb[:, :], h_turned[:, s, :], start=True, stop=True).then_inc(widened.sem, 1)
                for s in range(2):
                    pe.wait_ge(*unit_done(rectified, s, i))
                    if last:
                        pe.wait_ge(*unit_done(acc_set, s - 2, i))
                    else:
                        pe.wait_ge(*unit_done(staged_set, s - 2, i))
                    nc.tensor.matmul(out_ps[s][:, :], ones[:, :], b2_sb[:, :], start=True, stop=False, skip_group_check=True)
                    for t in range(UNIT):
                        out = out_ps[s][:, t * C:(t + 1) * C]
                        ins = nc.tensor.matmul(out, inner[:, s, t * P:(t + 1) * P], w2_sb[:, :], start=False, stop=True,
                                               skip_group_check=True)
                    ins.then_inc(narrowed.sem, 1)

    weights.passed(48), ones_set.passed(2)
    units_passed([started, turned, copied, widened, rectified, narrowed, acc_set])
    if not last:
        units_passed([staged_set, released])


def gru_nodes(nc, mem, dram, tag="gru"):
    ctx = ExitStack()
    W = C + 1
    with ctx:
        sb = lambda name, shape, dt=F32: ctx.enter_context(nc.sbuf_tensor(f"{tag}_{name}", shape, dt))
        w2_sb = sb("w2", [W, C])
        wi_sb = sb("wi", [W, 3 * C])
        wh_sb = sb("wh", [W, 3 * C])
        sums = sb("sums", [P, 2, UNIT, W])
        h = sb("h", [P, 2, UNIT * C])
        sums_turned = sb("sums_turned", [W, 2, UNIT * P])
        h_turned = sb("h_turned", [W, 2, UNIT * P])
        agg = sb("agg", [W, 2, UNIT * P])
        gates = sb("gates", [P, 2, UNIT, 2 * C])
        fresh = sb("fresh", [P, 2, UNIT, C])
        blend = sb("blend", [P, 2, UNIT, C])
        turn_ps = [ctx.enter_context(nc.psum_tensor(f"{tag}_turn_ps{j}", [W, UNIT * P], F32)) for j in range(2)]
        agg_ps = ctx.enter_context(nc.psum_tensor(f"{tag}_agg_ps", [C, UNIT * P], F32))
        gate_ps = [ctx.enter_context(nc.psum_tensor(f"{tag}_gate_ps{j}", [P, UNIT, 2 * C], F32)) for j in range(2)]
        fresh_ps = [ctx.enter_context(nc.psum_tensor(f"{tag}_fresh_ps{j}", [P, UNIT, 2, C], F32)) for j in range(2)]
        sem = mem.sems
        weights, started, turned, copied = sem["load"], sem["act_done"], sem["pe_done"], sem["act_done2"]
        summed, summed_copied, gated, opened = sem["pe_done2"], sem["act_done3"], sem["pe_done3"], sem["act_done4"]
        mixed, squashed, acc_set, ones_set, chain = (sem["dve_done"], sem["act_done5"], sem["dve_done2"], sem["made"],
                                                     sem["dve_chain"])
        block = ctx.enter_context(nc.Block())

        @block.sync
        def _(sp):
            load_weights(sp, mem, [(w2_sb[:, :], dram["w2_msg"]), (wi_sb[:, :], dram["w_ih"]), (wh_sb[:, :], dram["w_hh"])])

        @block.scalar
        def _(act):
            credit_units(act, [started, copied, summed_copied, opened, squashed])
            with act.Fori(0, UNITS // 2) as i:
                for s in range(2):
                    u = 2 * i + s
                    act.wait_ge(*unit_done(turned, s - 2, i))
                    nc.scalar.activation(sums[:, s, :, 0:C], mem.acc[:, unit_columns(u)].rearrange("p (t c) -> p t c", c=C), ACT.Copy)
                    nc.scalar.activation(sums[:, s, :, C:W], mem.degree[:, bass.ds(u * UNIT, UNIT)].unsqueeze(2), ACT.Copy)
                    act.wait_ge(*unit_done(acc_set, s - 2, i))
                    nc.scalar.activation(h[:, s, :], mem.xs[:, unit_columns(u)], ACT.Copy).then_inc(started.sem, 1)
                for s in range(2):
                    act.wait_ge(*unit_done(turned, s, i))
                    act.wait_ge(*unit_done(gated, s - 2, i))
                    nc.scalar.activation(sums_turned[:, s, :], turn_ps[0][:, :], ACT.Copy)
                    nc.scalar.activation(h_turned[0:C, s, :], turn_ps[1][0:C, :], ACT.Copy).then_inc(copied.sem, 1)
                for s in range(2):
                    act.wait_ge(*unit_done(summed, s, i))
                    nc.scalar.activation(agg[0:C, s, :], agg_ps[:, :], ACT.Copy).then_inc(summed_copied.sem, 1)
                for s in range(2):
                    act.wait_ge(*unit_done(gated, s, i))
                    act.wait_ge(*unit_done(acc_set, s - 2, i))
                    nc.scalar.activation(gates[:, s, :, :], gate_ps[s][:, :, :], ACT.Sigmoid).then_inc(opened.sem, 1)
                for s in range(2):
                    act.wait_ge(*unit_done(mixed, s, i))
                    nc.scalar.activation(fresh[:, s, :, :], blend[:, s, :, :], ACT.Tanh).then_inc(squashed.sem, 1)

        @block.vector
        def _(dve):
            nc.vector.memset(h_turned[C:W, :, :], 1.0).then_inc(ones_set.sem, 1)
            nc.vector.memset(agg[C:W, :, :], 1.0).then_inc(ones_set.sem, 1)
            credit_units(dve, [mixed, acc_set])
            with dve.Fori(0, UNITS // 2) as i:
                for s in range(2):
                    dve.wait_ge(*unit_done(opened, s, i))
                    nc.vector.tensor_tensor(blend[:, s, :, :], gates[:, s, :, 0:C], fresh_ps[s][:, :, 1, :], ALU.mult).then_inc(chain.sem, 1)
                    dve.wait_ge(chain.sem, chain.at(s + 1) + 8 * i)
                    nc.vector.tensor_tensor(blend[:, s, :, :], blend[:, s, :, :], fresh_ps[s][:, :, 0, :], ALU.add).then_inc(mixed.sem, 1)
                for s in range(2):
                    c = 1 + 3 * s
                    dve.wait_ge(*unit_done(squashed, s, i))
                    x = h[:, s, :].rearrange("p (t c) -> p t c", c=C)
                    nc.vector.tensor_tensor(blend[:, s, :, :], x, fresh[:, s, :, :], ALU.subtract).then_inc(chain.sem, 1)
                    dve.wait_ge(chain.sem, chain.at(c + 2) + 8 * i)
                    nc.vector.tensor_tensor(blend[:, s, :, :], blend[:, s, :, :], gates[:, s, :, C:2 * C], ALU.mult).then_inc(chain.sem, 1)
                    dve.wait_ge(chain.sem, chain.at(c + 3) + 8 * i)
                    nc.vector.tensor_tensor(blend[:, s, :, :], blend[:, s, :, :], fresh[:, s, :, :], ALU.add).then_inc(chain.sem, 1)
                    dve.wait_ge(chain.sem, chain.at(c + 4) + 8 * i)
                    nc.vector.tensor_tensor(mem.acc[:, unit_columns(2 * i + s)].rearrange("p (t c) -> p t c", c=C),
                                            blend[:, s, :, :], x, ALU.add).then_inc(acc_set.sem, 1)

        @block.tensor
        def _(pe):
            pe.wait_ge(weights.sem, weights.at(48))
            pe.wait_ge(ones_set.sem, ones_set.at(2))
            credit_units(pe, [turned, summed, gated])
            with pe.Fori(0, UNITS // 2) as i:
                for s in range(2):
                    pe.wait_ge(*unit_done(started, s, i))
                    pe.wait_ge(*unit_done(copied, s - 1, i))
                    for t in range(UNIT):
                        nc.tensor.transpose(turn_ps[0][:, t * P:(t + 1) * P], sums[:, s, t, :], mem.ident[:, :])
                        ins = nc.tensor.transpose(turn_ps[1][0:C, t * P:(t + 1) * P], h[:, s, t * C:(t + 1) * C], mem.ident[:, :])
                    ins.then_inc(turned.sem, 1)
                for s in range(2):
                    pe.wait_ge(*unit_done(copied, s, i))
                    pe.wait_ge(*unit_done(summed_copied, s - 1, i))
                    nc.tensor.matmul(agg_ps[:, :], w2_sb[:, :], sums_turned[:, s, :], start=True, stop=True).then_inc(summed.sem, 1)
                for s in range(2):
                    pe.wait_ge(*unit_done(summed_copied, s, i))
                    pe.wait_ge(*unit_done(mixed, s - 2, i))
                    for t in range(UNIT):
                        cols = slice(t * P, (t + 1) * P)
                        nc.tensor.matmul(gate_ps[s][:, t, :], agg[:, s, cols], wi_sb[:, 0:2 * C], start=True, stop=False)
                        nc.tensor.matmul(gate_ps[s][:, t, :], h_turned[:, s, cols], wh_sb[:, 0:2 * C], start=False, stop=True)
                        nc.tensor.matmul(fresh_ps[s][:, t, 0, :], agg[:, s, cols], wi_sb[:, 2 * C:], start=True, stop=True)
                        ins = nc.tensor.matmul(fresh_ps[s][:, t, 1, :], h_turned[:, s, cols], wh_sb[:, 2 * C:], start=True, stop=True)
                    ins.then_inc(gated.sem, 1)

    weights.passed(48), ones_set.passed(2), chain.passed(4 * UNITS)
    units_passed([started, turned, copied, summed, summed_copied, gated, opened, mixed, squashed, acc_set])


def layernorm(nc, mem, tag, table=None):
    ctx = ExitStack()
    with ctx:
        sb = lambda name, shape, dt=F32: ctx.enter_context(nc.sbuf_tensor(f"{tag}_{name}", shape, dt))
        parts = 2
        T = TILES_P // parts
        squares = sb("squares", [P, T * C])
        mean = sb("mean", [P, parts, T])
        var = sb("var", [P, parts, T])
        dev = sb("dev", [P, parts, T])
        sem = mem.sems
        chain, centred, rooted, squared, done, stored, scaled = (sem["dve_chain"], sem["dve_done"], sem["act_done"], sem["act_done2"],
                                                         sem["dve_done2"], sem["store"], sem["dve_done3"])
        block = ctx.enter_context(nc.Block())
        view = lambda m, q: m[:, q * T * C:(q + 1) * T * C].rearrange("p (t c) -> p t c", c=C)

        @block.scalar
        def _(act):
            for q in range(parts):
                act.wait_ge(centred.sem, centred.at(2 * q + 1))
                nc.scalar.activation(squares[:, :], mem.acc[:, q * T * C:(q + 1) * T * C], ACT.Square).then_inc(squared.sem, 1)
                act.wait_ge(centred.sem, centred.at(2 * q + 2))
                nc.scalar.activation(dev[:, q, :], var[:, q, :], ACT.Sqrt).then_inc(rooted.sem, 1)

        @block.vector
        def _(dve):
            link = Links(chain)
            for q in range(parts):
                x = view(mem.acc, q)
                nc.vector.tensor_reduce(mean[:, q, :], x, AX.X, ALU.add).then_inc(*link.next())
                dve.wait_ge(*link.done())
                nc.vector.tensor_scalar(mean[:, q, :], mean[:, q, :], 1.0 / C, None, ALU.mult).then_inc(*link.next())
                dve.wait_ge(*link.done())
                nc.vector.tensor_tensor(x, x, bc(mean[:, q, :], 2, C), ALU.subtract).then_inc(centred.sem, 1)
                dve.wait_ge(squared.sem, squared.at(q + 1))
                nc.vector.tensor_reduce(var[:, q, :], squares[:, :].rearrange("p (t c) -> p t c", c=C), AX.X, ALU.add).then_inc(*link.next())
                dve.wait_ge(*link.done())
                nc.vector.tensor_scalar(var[:, q, :], var[:, q, :], 1.0 / C, EPS, ALU.mult, ALU.add).then_inc(centred.sem, 1)
                dve.wait_ge(rooted.sem, rooted.at(q + 1))
                nc.vector.reciprocal(dev[:, q, :], dev[:, q, :]).then_inc(*link.next())
                dve.wait_ge(*link.done())
                nc.vector.tensor_tensor(view(mem.xs, q), x, bc(dev[:, q, :], 2, C), ALU.mult).then_inc(done.sem, 1)
                if table is not None:
                    dve.wait_ge(done.sem, done.at(q + 1))
                    nc.vector.tensor_copy(x, view(mem.xs, q)).then_inc(scaled.sem, 1)
            link.close()

        if table is not None:
            @block.sync
            def _(sp):
                for q in range(parts):
                    sp.wait_ge(done.sem, done.at(q + 1))
                    sp.dma_start(table[q * T * P:(q + 1) * T * P, :].rearrange("(t p) c -> p t c", p=P),
                                 view(mem.xs, q)).then_inc(stored.sem, 16)
                sp.wait_ge(stored.sem, stored.at(16 * parts))

    centred.passed(2 * parts), squared.passed(parts), rooted.passed(parts), done.passed(parts)
    if table is not None:
        scaled.passed(parts), stored.passed(16 * parts)


def residual_sum(nc, mem, tag):
    done = mem.sems["dve_done"]
    with nc.Block() as block:
        @block.vector
        def _(dve):
            nc.vector.tensor_tensor(mem.acc[:, :], mem.acc[:, :], mem.xs[:, :], ALU.add).then_inc(done.sem, 1)
    done.passed(1)


def sheaf_pass(nc, mem, dram, tag="sheaf"):
    ctx = ExitStack()
    B, SB = BATCH, SHEAF_BODY
    GB = B // GROUP
    HB = B // 2
    D, H = 4, C // 4
    F = 2 * B
    with ctx:
        sb = lambda name, shape, dt=F32: ctx.enter_context(nc.sbuf_tensor(f"{tag}_{name}", shape, dt))
        rows = sb("rows", [P, SB * B * TROW])
        side = TILES_P * 2 * HID
        onehot = [table.rearrange("p (u n) -> p u n", n=P) for table in (
            mem.typ[:, 0:B * P], mem.norm[:, 0:B * P], mem.dst_side[:, side:side + B * P], mem.row_i[:, 0:B * P].bitcast(F32))]
        turned_hot = sb("turned_hot", [P, 2, GROUP, P])
        hidden = sb("hidden", [P, 2, GROUP * 2 * HID])
        hidden_turned = sb("hidden_turned", [GROUP * 2 * HID, 2, P])
        w2_sb = sb("w2", [GROUP * 2 * HID, GROUP * 2 * NPAR])
        b2_sb = sb("b2", [1, B * 2 * NPAR])
        ones = sb("ones", [1, P])
        drel_now = sb("drel_now", [P, 2, B])
        index_now = sb("index_now", [P, SB * B], I32)
        par = sb("par", [P, 2, NPAR, F])
        cols = sb("cols", [P, 6, D, F])
        prods = sb("prods", [P, 4, D, F])
        halves = sb("halves", [P, 4, 2, F])
        norms = sb("norms", [P, D, F])
        roots = sb("roots", [P, D, F])
        dots = sb("dots", [P, 2, F])
        small = sb("small", [P, 4, F])
        scales = sb("scales", [P, D, D, B])
        outer = sb("outer", [P, D, D * D * B])
        pair = sb("pair", [P, 2, D * D * B])
        both = sb("both", [P, D * D, B])
        parts = sb("parts", [P, D, HB * C])
        messages = mem.ew[:, 0:B * C].rearrange("p (g w) -> p g w", g=GB)
        turn_ps = [ctx.enter_context(nc.psum_tensor(f"{tag}_turn_ps{j}", [P, GROUP, P], F32)) for j in range(2)]
        pre_ps = ctx.enter_context(nc.psum_tensor(f"{tag}_pre_ps", [P, 512], F32))
        back_ps = ctx.enter_context(nc.psum_tensor(f"{tag}_back_ps", [P, 512], F32))
        par_ps = [ctx.enter_context(nc.psum_tensor(f"{tag}_par_ps{j}", [P, 512], F32)) for j in range(2)]
        sum_ps = [ctx.enter_context(nc.psum_tensor(f"{tag}_sum_ps{j}", [P, 512], F32)) for j in range(2)]
        sem = mem.sems
        weights, ones_set, chain, marked = sem["load"], sem["made"], sem["dve_chain"], sem["act_chain"]
        turned_back, placed = sem["pe_done4"], sem["act_done5"]
        built, turned, copied, joined, rectified = sem["built"], sem["pe_done"], sem["act_done"], sem["pe_done2"], sem["act_done2"]
        widened, taken, indices, batch_read = sem["pe_done3"], sem["act_done3"], sem["index_ready"], sem["dve_done"]
        normed, rooted, message_ready, used, added = (sem["dve_done2"], sem["act_done4"], sem["dve_done3"], sem["used"],
                                                      sem["added"])
        gathers = [sem[f"gather{q}"] for q in range(4)]
        block = ctx.enter_context(nc.Block())


        @block.sync
        def _(sp):
            load_weights(sp, mem, [(w2_sb[:, :], dram["w2_sheaf"]), (b2_sb[:, :], dram["b2_sheaf"])])

        @block.gpsimd
        def _(pool):
            with pool.Fori(0, SHEAF_BODIES) as i:
                for s in range(SB):
                    wait_apart(pool, mem, indices.sem, indices.at(s + 1) + SB * i)
                    wait_apart(pool, mem, batch_read.sem, batch_read.at(s + 2) + SB * i)
                    for u in range(B):
                        slot = s * B + u
                        nc.gpsimd.indirect_dma_start(
                            out=rows[:, slot * TROW:(slot + 1) * TROW], out_offset=None, in_=dram["sheaf_table"],
                            in_offset=bass.IndirectOffsetOnAxis(ap=index_now[:, slot:slot + 1], axis=0),
                        ).then_inc(gathers[s].sem, 16)
            wait_apart(pool, mem, indices.sem, indices.at(1) + SB * SHEAF_BODIES)
            wait_apart(pool, mem, batch_read.sem, batch_read.at(2) + SB * SHEAF_BODIES)
            for u in range(B):
                nc.gpsimd.indirect_dma_start(
                    out=rows[:, u * TROW:(u + 1) * TROW], out_offset=None, in_=dram["sheaf_table"],
                    in_offset=bass.IndirectOffsetOnAxis(ap=index_now[:, u:u + 1], axis=0),
                ).then_inc(gathers[0].sem, 16)

        def gathered_batch(s, i):
            g = gathers[s % SB]
            return g.sem, g.at(16 * B * (s // SB + 1)) + 16 * B * i

        @block.scalar
        def _(act):
            def place(s, i):
                act.wait_ge(built.sem, built.at(GB * s) + SB * GB * i)
                nc.scalar.activation(drel_now[:, s % 2, :], mem.drel[:, bass.ds(i * (SB * B) + s * B, B)],
                                     ACT.Copy).then_inc(marked.sem, 1)

            def build(s, g, i):
                if g == 0:
                    act.wait_ge(used.sem, used.at(GB * s) + SB * GB * i)
                    act.wait_ge(marked.sem, marked.at((GB + 1) * s + 1) + SB * (GB + 1) * i)
                for u in range(GROUP * g, GROUP * (g + 1)):
                    ins = nc.scalar.activation(onehot[s % SB][:, u, :], mem.iota[:, :], ACT.Abs, scale=-1.0,
                                               bias=drel_now[:, s % 2, u:u + 1])
                ins.then_inc(marked.sem, 1)
                act.wait_ge(marked.sem, marked.at((GB + 1) * s + g + 2) + SB * (GB + 1) * i)
                group = onehot[s % SB][:, GROUP * g:GROUP * (g + 1), :]
                nc.scalar.activation(group, group, ACT.Relu, scale=-1.0, bias=mem.iota[:, 1:2]).then_inc(built.sem, 1)

            def copy(s, g, i):
                n = GB * s + g
                act.wait_ge(turned.sem, turned.at(n + 1) + SB * GB * i)
                act.wait_ge(joined.sem, joined.at(n + 1) + SB * GB * i)
                nc.scalar.activation(turned_hot[:, n % 2, :, :], turn_ps[n % 2][:, :, :], ACT.Copy).then_inc(copied.sem, 1)

            def rectify(s, g, i):
                n = GB * s + g
                act.wait_ge(joined.sem, joined.at(n + 3) + SB * GB * i)
                act.wait_ge(turned_back.sem, turned_back.at(n + 1) + SB * GB * i)
                nc.scalar.activation(hidden[:, n % 2, :], pre_ps[:, 0:GROUP * 2 * HID], ACT.Relu).then_inc(rectified.sem, 1)

            def put(s, g, i):
                n = GB * s + g
                act.wait_ge(turned_back.sem, turned_back.at(n + 3) + SB * GB * i)
                act.wait_ge(widened.sem, widened.at(n + 1) + SB * GB * i)
                nc.scalar.activation(hidden_turned[:, n % 2, :], back_ps[:, 0:P], ACT.Copy).then_inc(placed.sem, 1)

            def take(s, i):
                act.wait_ge(widened.sem, widened.at(2 + GB * (s + 1)) + SB * GB * i)
                act.wait_ge(batch_read.sem, batch_read.at(s + SB) + SB * i)
                nc.scalar.activation(par[:, s % 2, :, :].rearrange("p f (m u) -> p u f m", u=B),
                                     par_ps[s % 2][:, 0:B * 2 * NPAR].rearrange("p (u f m) -> p u f m", u=B, m=2),
                                     ACT.Copy).then_inc(taken.sem, 1)

            def front_begins(s, i):
                copy(s, 0, i)
                copy(s, 1, i)

            def front(s, i, ahead=True):
                if ahead:
                    place(s + 1, i)
                rectify(s, 0, i)
                copy(s, 2, i)
                if ahead:
                    build(s + 1, 0, i)
                rectify(s, 1, i)
                put(s, 0, i)
                copy(s, 3, i)
                if ahead:
                    build(s + 1, 1, i)
                rectify(s, 2, i)
                put(s, 1, i)
                if ahead:
                    build(s + 1, 2, i)
                rectify(s, 3, i)
                put(s, 2, i)
                if ahead:
                    build(s + 1, 3, i)
                put(s, 3, i)
                take(s, i)

            def root(s, i):
                act.wait_ge(normed.sem, normed.at(s + 1) + SB * i)
                nc.scalar.activation(roots[:, :, :], norms[:, :, :], ACT.Sqrt).then_inc(rooted.sem, 1)

            def place_indices(s, i):
                act.wait_ge(batch_read.sem, batch_read.at(s + 2) + SB * i)
                nc.scalar.activation(index_now[:, (s % SB) * B:(s % SB + 1) * B], mem.src_i[:, bass.ds(i * (SB * B) + s * B, B)],
                                     ACT.Copy).then_inc(indices.sem, 1)

            for s in range(SB):
                place_indices(s, 0)
            for s in range(2):
                place(s, 0)
                for g in range(GB):
                    build(s, g, 0)
            front_begins(0, 0)
            front(0, 0, ahead=False)
            front_begins(1, 0)
            root(0, 0)
            with act.Fori(0, SHEAF_BODIES) as i:
                for s in range(SB):
                    front(s + 1, i)
                    front_begins(s + 2, i)
                    root(s + 1, i)
                    if s > 0:
                        place_indices(SB + s - 1, i)
                place_indices(SB + SB - 1, i)

        @block.tensor
        def _(pe):
            def turn(s, g, i):
                n = GB * s + g
                pe.wait_ge(built.sem, built.at(n + 1) + SB * GB * i)
                pe.wait_ge(copied.sem, copied.at(n + 1) + SB * GB * i)
                for u in range(GROUP):
                    ins = nc.tensor.transpose(turn_ps[n % 2][:, u, :], onehot[s % SB][:, GROUP * g + u, :], mem.ident[:, :])
                ins.then_inc(turned.sem, 1)

            def join(s, g, i):
                n = GB * s + g
                tiles = tiles_of_steps(nc, mem, PE_ENGINE, i * (SB * B) + GROUP * n)
                if g == 0:
                    pe.wait_ge(*gathered_batch(s, i))
                pe.wait_ge(copied.sem, copied.at(n + 3) + SB * GB * i)
                pe.wait_ge(rectified.sem, rectified.at(n + 2) + SB * GB * i)
                first = (s % SB) * B + GROUP * g
                source = rows[:, first * TROW:(first + GROUP) * TROW].rearrange("p (u w) -> p u w", u=GROUP)[:, :, C:TROW]
                width = 2 * HID
                nc.tensor.matmul(pre_ps[:, 0:GROUP * width], mem.ident[:, :], source, start=True, stop=False, skip_group_check=True)
                for u in range(GROUP):
                    ins = nc.tensor.matmul(pre_ps[:, u * width:(u + 1) * width], turned_hot[:, n % 2, u, :],
                                           mem.dst_side[:, bass.ds(tiles[u] * width, width)], start=False, stop=True,
                                           skip_group_check=True)
                ins.then_inc(joined.sem, 1)

            def turn_back(s, g, i):
                n = GB * s + g
                pe.wait_ge(rectified.sem, rectified.at(n + 3) + SB * GB * i)
                pe.wait_ge(placed.sem, placed.at(n + 2) + SB * GB * i)
                nc.tensor.transpose(back_ps[:, 0:P], hidden[:, n % 2, :], mem.ident[:, :]).then_inc(turned_back.sem, 1)

            def widen(s, g, i):
                n = GB * s + g
                if g == 0:
                    pe.wait_ge(taken.sem, taken.at(s + 1) + SB * i)
                    nc.tensor.matmul(par_ps[s % 2][:, 0:B * 2 * NPAR], ones[:, :], b2_sb[:, :], start=True, stop=False,
                                     skip_group_check=True)
                pe.wait_ge(placed.sem, placed.at(n + 3) + SB * GB * i)
                width = GROUP * 2 * NPAR
                nc.tensor.matmul(par_ps[s % 2][:, g * width:(g + 1) * width], hidden_turned[:, n % 2, :], w2_sb[:, :],
                                 start=False, stop=True, skip_group_check=True).then_inc(widened.sem, 1)

            def add_up(s, g, i):
                pe.wait_ge(message_ready.sem, message_ready.at(GB * s + g + 1) + SB * GB * i)
                for u in range(GROUP):
                    at = (g % 2) * GROUP * C + u * C
                    ins = nc.tensor.matmul(sum_ps[g // 2][:, at:at + C], onehot[s % SB][:, GROUP * g + u, :],
                                           messages[:, g, u * C:(u + 1) * C], start=True, stop=True)
                ins.then_inc(used.sem, 1)

            def front_begins(s, i):
                turn(s, 0, i)
                turn(s, 1, i)

            def front(s, i, last=None):
                join(s, 0, i)
                turn(s, 2, i)
                join(s, 1, i)
                turn_back(s, 0, i)
                turn(s, 3, i)
                join(s, 2, i)
                turn_back(s, 1, i)
                widen(s, 0, i)
                join(s, 3, i)
                turn_back(s, 2, i)
                widen(s, 1, i)
                turn_back(s, 3, i)
                if last is not None:
                    add_up(last, 0, i)
                widen(s, 2, i)
                if last is not None:
                    add_up(last, 1, i)
                widen(s, 3, i)
                if last is not None:
                    add_up(last, 2, i)
                    add_up(last, 3, i)

            pe.wait_ge(weights.sem, weights.at(32))
            pe.wait_ge(ones_set.sem, ones_set.at(1))
            pe.sem_inc(joined.sem, 2)
            pe.sem_inc(turned_back.sem, 2)
            pe.sem_inc(widened.sem, 2)
            pe.sem_inc(used.sem, SHEAF_USED0)
            front_begins(0, 0)
            front(0, 0)
            front_begins(1, 0)
            with pe.Fori(0, SHEAF_BODIES) as i:
                for s in range(SB):
                    front(s + 1, i, last=s)
                    front_begins(s + 2, i)

        per_body = SB * SHEAF_LINKS
        before = 5 + SHEAF_LINKS

        @block.vector
        def _(dve):
            def add(s, k, i, tiles):
                g, u = k // GROUP, k % GROUP
                if u == 0:
                    tiles = tiles_of_steps(nc, mem, DVE_ENGINE, i * (SB * B) + s * B + GROUP * g)
                    if g % 2 == 0:
                        dve.wait_ge(used.sem, used.at(SHEAF_USED0 + GB * s + g + 2) + SB * GB * i)
                dve.wait_ge(added.sem, added.at(1 + s * B + k) + SB * B * i)
                at = (g % 2) * GROUP * C + u * C
                columns = mem.acc[:, bass.ds(tiles[u] * C, C)]
                nc.vector.tensor_tensor(columns, columns, sum_ps[g // 2][:, at:at + C], ALU.add).then_inc(added.sem, 1)
                return tiles

            def orthogonalise(s, i, link, add_next):
                p0, p1, p3, p2, p4, p5 = (par[:, s % 2, f, :] for f in range(NPAR))
                w, v, u = cols[:, 0:4:3], cols[:, 4:6], cols[:, 1:3]
                nc.vector.tensor_copy(cols[:, 0, 1:4, :], par[:, s % 2, 0:3, :]).then_inc(*link.next())
                nc.vector.tensor_copy(cols[:, 4, 2:4, :], par[:, s % 2, 3:5, :]).then_inc(*link.next())
                nc.vector.tensor_scalar(cols[:, 3, 2, :], p5, -1.0, None, ALU.mult).then_inc(*link.next())
                nc.vector.tensor_scalar(cols[:, 5, 1, :], p2, -1.0, None, ALU.mult).then_inc(*link.next())
                nc.vector.tensor_tensor(small[:, 0, :], p2, p0, ALU.mult).then_inc(*link.next())
                nc.vector.tensor_tensor(small[:, 1, :], p2, p5, ALU.mult).then_inc(*link.next())
                nc.vector.tensor_tensor(small[:, 2, :], p1, p5, ALU.mult).then_inc(*link.next())
                add_next()
                dve.wait_ge(*link.done())
                nc.vector.tensor_tensor(cols[:, 3, 1, :], small[:, 1, :], p4, ALU.subtract).then_inc(*link.next())
                nc.vector.tensor_tensor(cols[:, 5, 0, :], small[:, 0, :], p1, ALU.subtract).then_inc(*link.next())
                add_next()
                dve.wait_ge(*link.done())
                nc.vector.tensor_tensor(small[:, 3, :], cols[:, 3, 1, :], p0, ALU.mult).then_inc(*link.next())
                add_next()
                dve.wait_ge(*link.done())
                nc.vector.tensor_tensor(small[:, 3, :], small[:, 3, :], small[:, 2, :], ALU.subtract).then_inc(*link.next())
                add_next()
                dve.wait_ge(*link.done())
                nc.vector.scalar_tensor_tensor(cols[:, 3, 0, :], small[:, 3, :], -1.0, p3, ALU.mult, ALU.subtract).then_inc(*link.next())
                add_next()
                dve.wait_ge(*link.done())
                nc.vector.tensor_tensor(prods[:, 0:2], w, w, ALU.mult).then_inc(*link.next())
                nc.vector.tensor_tensor(prods[:, 2:4], w, v, ALU.mult).then_inc(*link.next())
                add_next()
                dve.wait_ge(*link.done())
                nc.vector.tensor_tensor(halves[:, :, :, :], prods[:, :, 0:2, :], prods[:, :, 2:4, :], ALU.add).then_inc(*link.next())
                add_next()
                dve.wait_ge(*link.done())
                nc.vector.tensor_tensor(norms[:, 0:4:3, :], halves[:, 0:2, 0, :], halves[:, 0:2, 1, :], ALU.add).then_inc(*link.next())
                nc.vector.tensor_tensor(dots[:, :, :], halves[:, 2:4, 0, :], halves[:, 2:4, 1, :], ALU.add).then_inc(*link.next())
                add_next()
                dve.wait_ge(*link.done())
                nc.vector.tensor_tensor(prods[:, 0:2], v, bc(norms[:, 0:4:3, :], 2, D), ALU.mult).then_inc(*link.next())
                nc.vector.tensor_tensor(prods[:, 2:4], w, bc(dots[:, :, :], 2, D), ALU.mult).then_inc(*link.next())
                add_next()
                dve.wait_ge(*link.done())
                nc.vector.tensor_tensor(u, prods[:, 0:2], prods[:, 2:4], ALU.subtract).then_inc(*link.next())
                add_next()
                dve.wait_ge(*link.done())
                nc.vector.tensor_tensor(prods[:, 0:2], u, u, ALU.mult).then_inc(*link.next())
                add_next()
                dve.wait_ge(*link.done())
                nc.vector.tensor_tensor(halves[:, 0:2, :, :], prods[:, 0:2, 0:2, :], prods[:, 0:2, 2:4, :], ALU.add).then_inc(*link.next())
                add_next()
                dve.wait_ge(*link.done())
                nc.vector.tensor_tensor(norms[:, 1:3, :], halves[:, 0:2, 0, :], halves[:, 0:2, 1, :], ALU.add).then_inc(normed.sem, 1)

            def multiply_maps(s, i, link, add_next):
                for r in range(D):
                    ve = cols[:, 0:4, r, 0:B]
                    ue = cols[:, 0:4, r, B:F]
                    nc.vector.tensor_tensor(outer[:, r, :].rearrange("p (a b u) -> p a b u", a=D, b=D), bc(ve, 2, D), bc(ue, 1, D),
                                            ALU.mult).then_inc(*link.next())
                    add_next()
                dve.wait_ge(*link.done())
                nc.vector.tensor_tensor(pair[:, :, :], outer[:, 0:2, :], outer[:, 2:4, :], ALU.add).then_inc(*link.next())
                add_next()
                dve.wait_ge(rooted.sem, rooted.at(s + 1) + SB * i)
                nc.vector.reciprocal(roots[:, :, :], roots[:, :, :]).then_inc(*link.next())
                add_next()
                dve.wait_ge(*link.done())
                nc.vector.tensor_tensor(both[:, :, :], pair[:, 0, :].rearrange("p (m u) -> p m u", u=B),
                                        pair[:, 1, :].rearrange("p (m u) -> p m u", u=B), ALU.add).then_inc(*link.next())
                nc.vector.tensor_tensor(scales[:, :, :, :], bc(roots[:, :, 0:B], 2, D), bc(roots[:, :, B:F], 1, D),
                                        ALU.mult).then_inc(*link.next())
                add_next()
                dve.wait_ge(*link.done())
                nc.vector.tensor_tensor(both[:, :, :], both[:, :, :], scales[:, :, :, :].rearrange("p a b u -> p (a b) u"),
                                        ALU.mult).then_inc(*link.next())
                add_next()
                dve.wait_ge(*link.done())

            def apply(s, half, i, link):
                first = s % SB * B + half * HB
                x = rows[:, first * TROW:(first + HB) * TROW].rearrange("p (u w) -> p u w", u=HB)
                for b in (2, 3, 0, 1):
                    if b == 0 and half == 1:
                        dve.wait_ge(message_ready.sem, message_ready.at(GB * s + GB // 2) + SB * GB * i)
                    xb = bc(x[:, :, b * H:(b + 1) * H], 2, D)
                    m = both[:, b::D, half * HB:(half + 1) * HB].rearrange("p a u -> p u a")
                    nc.vector.tensor_tensor(parts[:, b, :].rearrange("p (u a h) -> p u a h", a=D, h=H), xb,
                                            bc(m, 3, H), ALU.mult).then_inc(*link.next())
                dve.wait_ge(*link.done())
                nc.vector.tensor_tensor(parts[:, 0:2, :], parts[:, 0:2, :], parts[:, 2:4, :], ALU.add).then_inc(*link.next())
                dve.wait_ge(*link.done())
                nc.vector.tensor_tensor(messages[:, half * GB // 2:(half + 1) * GB // 2, :].rearrange("p g w -> p (g w)"),
                                        parts[:, 0, :], parts[:, 1, :], ALU.add).then_inc(message_ready.sem, GB // 2)

            def apply_all(s, i, link):
                for half in range(2):
                    apply(s, half, i, link)
                dve.wait_ge(message_ready.sem, message_ready.at(GB * (s + 1)) + SB * GB * i)
                dve.sem_inc(batch_read.sem, 1)

            nc.vector.memset(ones[:, :], 1.0).then_inc(ones_set.sem, 1)
            nc.vector.memset(cols[:, :, :, :], 0.0).then_inc(chain.sem, 1)
            dve.wait_ge(chain.sem, chain.at(1))
            nc.vector.memset(cols[:, 0, 0, :], 1.0).then_inc(chain.sem, 1)
            nc.vector.memset(cols[:, 3, 3, :], 1.0).then_inc(chain.sem, 1)
            nc.vector.memset(cols[:, 4, 1, :], 1.0).then_inc(chain.sem, 1)
            nc.vector.memset(cols[:, 5, 2, :], 1.0).then_inc(chain.sem, 1)
            dve.wait_ge(chain.sem, chain.at(5))
            dve.sem_inc(copied.sem, 2)
            dve.sem_inc(rectified.sem, 2)
            dve.sem_inc(placed.sem, 2)
            dve.sem_inc(batch_read.sem, SB + 1)
            dve.sem_inc(taken.sem, 1)
            dve.sem_inc(added.sem, 1)
            link = Links(chain, 5)
            dve.wait_ge(taken.sem, taken.at(2))
            orthogonalise(0, 0, link, lambda: None)
            multiply_maps(0, 0, link, lambda: None)
            apply_all(0, 0, link)
            assert link.n == before, link.n
            with dve.Fori(0, SHEAF_BODIES) as i:
                link = Links(chain, before, per_body, i)
                for s in range(SB):
                    done = [0, None]

                    def add_next():
                        done[:] = done[0] + 1, add(s, done[0], i, done[1])

                    dve.wait_ge(taken.sem, taken.at(s + 3) + SB * i)
                    orthogonalise(s + 1, i, link, lambda: add_next() if done[0] < B // 2 else None)
                    while done[0] < B // 2:
                        add_next()
                    multiply_maps(s + 1, i, link, add_next)
                    while done[0] < B:
                        add_next()
                    apply_all(s + 1, i, link)
                assert link.n == before + per_body, link.n

    n = SHEAF_BODIES
    groups, batches = SB * GB * n, SB * n
    weights.passed(32), ones_set.passed(1), chain.passed(before + per_body * n), built.passed(groups + 2 * GB)
    marked.passed((GB + 1) * (batches + 2)), turned.passed(groups + GB + 2)
    copied.passed(groups + GB + 4)
    for signal in (joined, rectified, turned_back, placed, widened):
        signal.passed(groups + GB + 2)
    taken.passed(batches + 2), indices.passed(batches + SB), batch_read.passed(batches + SB + 2)
    normed.passed(batches + 1), rooted.passed(batches + 1), message_ready.passed(groups + GB), used.passed(SHEAF_USED0 + groups)
    added.passed(1 + B * batches)
    for g in gathers:
        g.passed(16 * B * n)
    gathers[0].passed(16 * B)


def sheaf_weights(nc, mem, dram, tag="sheafw"):
    ctx = ExitStack()
    with ctx:
        sb = lambda name, shape, dt=F32: ctx.enter_context(nc.sbuf_tensor(f"{tag}_{name}", shape, dt))
        w1t = sb("w1t", [C, C])
        w2 = sb("w2", [C, C])
        halves = sb("halves", [C, 2 * HID])
        kt = sb("kt", [C, C])
        all_sb = sb("all", [C, P])
        root = sb("root", [P, TILES_P])
        ps = [ctx.enter_context(nc.psum_tensor(f"{tag}_ps{j}", [C, 512], F32)) for j in range(3)]
        sem = mem.sems
        weights, products, taken, stored, chain, rooted = (sem["load"], sem["pe_done"], sem["dve_done"], sem["store"],
                                                           sem["dve_chain"], sem["act_done"])
        block = ctx.enter_context(nc.Block())

        @block.sync
        def _(sp):
            load_weights(sp, mem, [(w1t[:, :], dram["w1_mix"]), (w2[:, :], dram["w2_mix"]), (halves[:, :], dram["mlp1"])])
            sp.wait_ge(taken.sem, taken.at(2))
            sp.dma_start(dram["w_sheaf"][0:C, :], all_sb[:, :]).then_inc(stored.sem, 16)
            sp.dma_start(dram["w_sheaf"][C:C + 1, :], dram["sheaf_bias"]).then_inc(stored.sem, 16)
            sp.wait_ge(stored.sem, stored.at(32))

        @block.tensor
        def _(pe):
            pe.wait_ge(weights.sem, weights.at(48))
            nc.tensor.matmul(ps[0][:, 0:C], w1t[:, :], w2[:, :], start=True, stop=True)
            nc.tensor.matmul(ps[1][:, 0:C], w2[:, :], w1t[:, :], start=True, stop=True).then_inc(products.sem, 1)
            pe.wait_ge(taken.sem, taken.at(1))
            nc.tensor.matmul(ps[2][:, 0:2 * HID], kt[:, :], halves[:, :], start=True, stop=True).then_inc(products.sem, 1)

        @block.scalar
        def _(act):
            nc.scalar.activation(root[:, :], mem.src_scale[:, :], ACT.Sqrt).then_inc(rooted.sem, 1)

        @block.vector
        def _(dve):
            dve.wait_ge(products.sem, products.at(1))
            nc.vector.tensor_copy(kt[:, :], ps[1][:, 0:C]).then_inc(taken.sem, 1)
            nc.vector.tensor_copy(all_sb[:, 0:C], ps[0][:, 0:C])
            dve.wait_ge(products.sem, products.at(2))
            nc.vector.tensor_copy(all_sb[:, C:C + 2 * HID], ps[2][:, 0:2 * HID])
            nc.vector.tensor_copy(all_sb[:, C + 2 * HID:C + 3 * HID], ps[2][:, HID:2 * HID])
            nc.vector.tensor_copy(all_sb[:, C + 3 * HID:C + 4 * HID], ps[2][:, 0:HID]).then_inc(taken.sem, 1)
            dve.wait_ge(rooted.sem, rooted.at(1))
            nc.vector.reciprocal(mem.src_scale[:, :], root[:, :]).then_inc(chain.sem, 1)

    weights.passed(48), products.passed(2), taken.passed(2), stored.passed(32), chain.passed(1), rooted.passed(1)


def sheaf_finish(nc, mem, dram, tag="finish"):
    ctx = ExitStack()
    parts = 2
    T = TILES_P // parts
    H = C // 4
    with ctx:
        sb = lambda name, shape, dt=F32: ctx.enter_context(nc.sbuf_tensor(f"{tag}_{name}", shape, dt))
        eps = sb("eps", [P, 4])
        factor = sb("factor", [P, 4])
        below = sb("below", [P, T * C])
        sem = mem.sems
        weights, chain, ready, raised = sem["load"], sem["dve_chain"], sem["dve_done"], sem["act_done"]
        block = ctx.enter_context(nc.Block())
        view = lambda m, q: m[:, q * T * C:(q + 1) * T * C].rearrange("p (t c) -> p t c", c=C)

        @block.sync
        def _(sp):
            load_weights(sp, mem, [(eps[:, :], dram["epsilons"].rearrange("(o d) -> o d", o=1).to_broadcast([P, 4]))])

        @block.scalar
        def _(act):
            act.wait_ge(weights.sem, weights.at(16))
            nc.scalar.activation(factor[:, :], eps[:, :], ACT.Tanh).then_inc(raised.sem, 1)
            for q in range(parts):
                act.wait_ge(ready.sem, ready.at(q + 1))
                nc.scalar.activation(below[:, :], below[:, :], ACT.Exp).then_inc(raised.sem, 1)

        @block.vector
        def _(dve):
            link = Links(chain)
            dve.wait_ge(raised.sem, raised.at(1))
            nc.vector.tensor_scalar(factor[:, :], factor[:, :], 2.0, None, ALU.add).then_inc(*link.next())
            dve.wait_ge(*link.done())
            for q in range(parts):
                v, x = view(mem.acc, q), view(mem.xs, q)
                nc.vector.tensor_tensor(v, v, bc(mem.src_scale[:, q * T:(q + 1) * T], 2, C), ALU.mult).then_inc(*link.next())
                dve.wait_ge(*link.done())
                nc.vector.tensor_scalar(below[:, :], mem.acc[:, q * T * C:(q + 1) * T * C], 0.0, None, ALU.min).then_inc(ready.sem, 1)
                dve.wait_ge(raised.sem, raised.at(q + 2))
                nc.vector.scalar_tensor_tensor(v, v, 0.0, below[:, :].rearrange("p (t c) -> p t c", c=C), ALU.max, ALU.add).then_inc(*link.next())
                dve.wait_ge(*link.done())
                xd, bd = (m.rearrange("p t (d h) -> p t d h", h=H) for m in (x, below[:, :].rearrange("p (t c) -> p t c", c=C)))
                for d in range(4):
                    nc.vector.tensor_scalar(bd[:, :, d, :], xd[:, :, d, :], factor[:, d:d + 1], 1.0, ALU.mult, ALU.add).then_inc(*link.next())
                    dve.wait_ge(*link.done())
                nc.vector.tensor_tensor(v, below[:, :].rearrange("p (t c) -> p t c", c=C), v, ALU.subtract).then_inc(*link.next())
                dve.wait_ge(*link.done())
            link.close()

    weights.passed(16), ready.passed(parts), raised.passed(parts + 1)


def store_output(nc, mem, out):
    stored = mem.sems["store"]
    full = N // P
    with nc.Block() as block:
        @block.sync
        def _(sp):
            sp.dma_start(out[0:full * P, :].rearrange("(t p) c -> p t c", p=P),
                         mem.xs[:, 0:full * C].rearrange("p (t c) -> p t c", c=C)).then_inc(stored.sem, 16)
            sp.dma_start(out[full * P:N, :], mem.xs[0:N - full * P, full * C:(full + 1) * C]).then_inc(stored.sem, 16)
            sp.wait_ge(stored.sem, stored.at(32))
    stored.passed(32)


def allocate(nc, ctx):
    mem = Memory()
    sb = lambda name, shape, dt=F32: ctx.enter_context(nc.sbuf_tensor(name, shape, dt))
    mem.ident = sb("ident", [P, P])
    mem.iota = sb("iota", [P, P])
    mem.iota_h = sb("iota_h", [P, P], BF16)
    mem.acc = sb("acc", [P, TILES_P * C])
    mem.xs = sb("xs", [P, TILES_P * C])
    mem.dst_side = sb("dst_side", [P, TILES_P * C])
    mem.counts = sb("counts", [P, TILES_P * R])
    mem.degree = sb("degree", [P, TILES_P])
    mem.src_i = sb("src_i", [P, STEPS_P], I32)
    mem.row_i = sb("row_i", [P, STEPS_P], I32)
    mem.drel = sb("drel", [P, STEPS_P])
    mem.typ = sb("typ", [P, STEPS_P])
    mem.ew = sb("ew", [P, STEPS_P])
    mem.norm = sb("norm", [P, STEPS_P])
    mem.tile_row = sb("tile_row", [1, STEPS_P], I32)
    mem.start_row = sb("start_row", [1, STEPS_P], I32)
    mem.start_i = sb("start_i", [P, PLAN_GROUPS], I32)
    mem.node0 = sb("node0", [P, PLAN_GROUPS])
    mem.src_scale = sb("src_scale", [P, TILES_P])
    names = ["load", "load1", "load2", "load3", "load4", "made", "store", "store2", "dve_chain", "act_chain", "dve_done", "dve_done2", "pe_done",
             "pe_done2", "pe_done3", "pe_done4", "act_done", "act_done2", "act_done3", "act_done4", "act_done5", "dve_done3", "built", "used", "added",
             "index_ready", "waited", "gather0", "gather1", "gather2", "gather3"]
    mem.sems = {name: Signal(ctx, nc, name) for name in names}
    return mem


def program(nc, dram, out):
    ctx = ExitStack()
    scratch = lambda name, shape, dt=F32: nc.dram_tensor(name, shape, dt, kind="Internal").ap()
    dram["plan_rows"] = scratch("plan_rows", [2, STEPS_P], I32)
    dram["relation_table"] = scratch("relation_table", [NODES_P * R, C])
    dram["message_table"] = scratch("message_table", [NODES_P, C])
    dram["node_table"] = scratch("node_table", [NODES_P, C])
    dram["node_table2"] = scratch("node_table2", [NODES_P, C])
    dram["sheaf_table"] = scratch("sheaf_table", [NODES_P, TROW])
    dram["w_sheaf"] = scratch("w_sheaf", [C + 1, P])
    with ctx:
        mem = allocate(nc, ctx)
        constants_and_plan(nc, mem, dram)
        align_edges(nc, mem, dram)
        count_relations(nc, mem, dram)
        relation_nodes(nc, mem, dram, "rel1", dram["rel_w1"], dram["rel_root1"], False)
        relation_pass(nc, mem, dram)
        relation_nodes(nc, mem, dram, "rel2", dram["rel_w2"], dram["rel_root2"], True)
        gather_pass(nc, mem, "rel2", dram["relation_table"], mem.row_i, mem.norm)
        residual_sum(nc, mem, "rel_sum")
        layernorm(nc, mem, "ln0")
        project_nodes(nc, mem, dram, "msg", dram["message_table"], C, dram["msg_w"], False)
        message_pass(nc, mem, dram, "msgp")
        gru_nodes(nc, mem, dram)
        layernorm(nc, mem, "ln1", dram["node_table"])
        split_sources(nc, mem, dram)
        gather_pass(nc, mem, "gin1", dram["node_table"], mem.src_i, mem.ew, count_sources=True)
        mlp_nodes(nc, mem, dram, "mlp1", dram["node_table2"], C, dram["gin_w11"], dram["gin_w12"], dram["gin_b12"], False)
        gather_pass(nc, mem, "gin2", dram["node_table2"], mem.src_i, mem.ew)
        mlp_nodes(nc, mem, dram, "mlp2", dram["node_table"], 2 * C, dram["gin_w21"], dram["gin_w22"], dram["gin_b22"], False)
        gather_pass(nc, mem, "gin3", dram["node_table"], mem.src_i, mem.ew)
        mlp_nodes(nc, mem, dram, "mlp3", None, C, dram["gin_w31"], dram["gin_w32"], dram["gin_b32"], True)
        layernorm(nc, mem, "ln2")
        sheaf_weights(nc, mem, dram)
        project_nodes(nc, mem, dram, "shf", dram["sheaf_table"], TROW, dram["w_sheaf"], True)
        sheaf_pass(nc, mem, dram)
        sheaf_finish(nc, mem, dram)
        layernorm(nc, mem, "ln3")
        store_output(nc, mem, out)


def kernel(**inputs):
    import numpy as np
    import concourse.bacc as bacc
    from concourse.bass_utils import run_bass_kernel_spmd

    a = {k: np.asarray(v) for k, v in inputs.items()}

    def edges(x, fill, length=P * STEPS_P):
        padded = np.full(length, fill, x.dtype)
        padded[:E] = x
        return padded

    def rows(*parts):
        return np.concatenate([p[None] if p.ndim == 1 else p for p in parts], 0)

    x = np.zeros((NODES_P, C), np.float32)
    x[:N] = a["x"]
    features = np.zeros((FE, EDGES_P + P), np.float32)
    features[:, :E] = a["edge_attr_32"].T
    zeros = np.zeros(C, np.float32)
    w1 = a["L1_gnn_W1"]
    w_edge = np.zeros((GROUP * FE, GROUP * C), np.float32)
    for u in range(GROUP):
        w_edge[u * FE:(u + 1) * FE, u * C:(u + 1) * C] = w1[:, 2 * C:].T
    w1_mix, w2_mix = np.zeros((C, C), np.float32), np.zeros((C, C), np.float32)
    for k in range(4):
        for d in range(4):
            for f in range(HID):
                w1_mix[k * HID + f, d * HID + f] = a["L3_gnn_W1"][d, k]
        w2_mix[k * HID:(k + 1) * HID, k * HID:(k + 1) * HID] = a["L3_gnn_W2"]
    m1, m2, b2 = a["L3_gnn_mlp1_w"], a["L3_gnn_mlp2_w"], a["L3_gnn_mlp2_b"]
    w2_sheaf = np.zeros((GROUP, 2, HID, GROUP, NPAR, 2), np.float32)
    b2_sheaf = np.zeros((1, BATCH, NPAR, 2), np.float32)
    for f, source in enumerate((0, 1, 3, 2, 4, 5)):
        b2_sheaf[:, :, f, :] = b2[source]
        for u in range(GROUP):
            for m in range(2):
                w2_sheaf[u, m, :, u, f, m] = m2[source]
    bias = np.zeros((1, P), np.float32)
    bias[0, TROW:TROW + HID] = a["L3_gnn_mlp1_b"]
    bias[0, TROW + HID:] = a["L3_gnn_mlp1_b"]
    given = {
        "dst": edges(a["dst"], NO_NODE), "src": edges(a["src"], PAD_SRC), "typ": edges(a["edge_type_8"], 0),
        "ew": edges(a["edge_weight"], 0), "x": x, "features": features,
        "rel_w1": a["L0_gnn_W1"].transpose(1, 0, 2).reshape(C, R * C), "rel_root1": rows(a["L0_gnn_root1"], a["L0_gnn_b1"]),
        "rel_w2": a["L0_gnn_W2"].transpose(1, 0, 2).reshape(C, R * C), "rel_root2": rows(a["L0_gnn_root2"], a["L0_gnn_b2"]),
        "msg_w": np.concatenate([rows(w1[:, :C].T, zeros), rows(w1[:, C:2 * C].T, a["L1_gnn_b1"])], 1),
        "w_edge": w_edge, "w2_msg": rows(a["L1_gnn_W2"].T, a["L1_gnn_b2"]),
        "w_ih": rows(a["L1_gnn_w_ih"].T, a["L1_gnn_b_ih"]), "w_hh": rows(a["L1_gnn_w_hh"].T, a["L1_gnn_b_hh"]),
        "w1_mix": w1_mix, "w2_mix": w2_mix, "mlp1": np.concatenate([m1[:, C:].T, m1[:, :C].T], 1), "sheaf_bias": bias,
        "w2_sheaf": w2_sheaf.reshape(GROUP * 2 * HID, GROUP * 2 * NPAR), "b2_sheaf": b2_sheaf.reshape(1, -1), "epsilons": a["L3_gnn_epsilons"],
    }
    for n in "123":
        given[f"gin_w{n}1"] = rows(a[f"L2_gnn_w{n}1"], a[f"L2_gnn_b{n}1"])
        given[f"gin_w{n}2"] = a[f"L2_gnn_w{n}2"]
        given[f"gin_b{n}2"] = np.tile(a[f"L2_gnn_b{n}2"], UNIT)[None]
    given = {k: np.ascontiguousarray(v) for k, v in given.items()}

    nc = bacc.Bacc("TRN2", target_bir_lowering=False, num_devices=1)
    dram = {k: nc.dram_tensor(f"in_{k}", v.shape, mybir.dt.from_np(v.dtype), kind="ExternalInput").ap() for k, v in given.items()}
    out = nc.dram_tensor("out", (N, C), F32, kind="ExternalOutput").ap()
    program(nc, dram, out)
    r = run_bass_kernel_spmd(nc, [{f"in_{k}": v for k, v in given.items()}], core_ids=[0])
    return r.results[0]["out"]
```
